# Optimizing a Trainium2 kernel written in Bass

```python
import numpy as np
import jax
import jax.numpy as jnp

def _softmax(x, axis=-1):
    return jax.nn.softmax(x, axis=axis)

def _gelu(x):
    return jax.nn.gelu(x, approximate=True)

def _silu(x):
    return jax.nn.silu(x)

def _sigmoid(x):
    return jax.nn.sigmoid(x)

def _layernorm(x, axis=-1, eps=1e-05):
    m = jnp.mean(x, axis=axis, keepdims=True)
    v = jnp.var(x, axis=axis, keepdims=True)
    return (x - m) / jnp.sqrt(v + eps)

def _scatter_add(tgt, idx, src, axis=0):
    return tgt.at[idx].add(src)

def _segment_sum(src, seg, n):
    return jax.ops.segment_sum(src, seg, n)
kernel_name = 'mk_seq_postln_d1_jaxref_r8_c4c50a'

def setup_inputs(seed: int=0):
    np.random.seed(seed)
    _w = jnp.asarray

    def _L0_attn_setup():
        import jax, jax.numpy as jnp
        import numpy as np
        ROPE_THETA = 10000.0
        INF_APPROX = 1e+30
        D_HEAD = 128

        def _rope(x, theta=ROPE_THETA):
            *_, L, D = x.shape
            half = D // 2
            pos = jnp.arange(L, dtype=jnp.float32)[:, None]
            freqs = jnp.power(theta, -jnp.arange(half, dtype=jnp.float32) / half)[None, :]
            angles = pos * freqs
            cos = jnp.cos(angles).astype(x.dtype)
            sin = jnp.sin(angles).astype(x.dtype)
            even, odd = jnp.split(x, 2, axis=-1)
            r_even = even * cos - odd * sin
            r_odd = even * sin + odd * cos
            return jnp.concatenate([r_even, r_odd], axis=-1)
        key = jax.random.key(seed)
        kx, kq, kk, kv, ko = jax.random.split(key, 5)
        B, T, M, D, G, H = (2, 128, 256, 128, 4, 4)
        std_m = M ** (-0.5)
        std_d = D ** (-0.5)
        return {'x': jax.random.normal(kx, (B, T, M), jnp.float32), 'w_aq': jax.random.normal(kq, (G, H, M, D), jnp.float32) * std_m, 'w_ak': jax.random.normal(kk, (G, M, D), jnp.float32) * std_m, 'w_av': jax.random.normal(kv, (G, M, D), jnp.float32) * std_m, 'w_ao': jax.random.normal(ko, (G, H, D, M), jnp.float32) * std_d}
    _L0_attn_in = _L0_attn_setup()

    def _L0_ffn_setup():
        import jax, jax.numpy as jnp
        import numpy as np
        E, K, H, F = (64, 6, 256, 96)
        G, KG = (8, 4)
        SHARED_F = 96
        SCALE = 2.5
        T = 2 * 128
        CAP = 2 * (T * K // E)

        def _grouped_topk(logits, bias):
            scores = jax.nn.sigmoid(logits.astype(jnp.float32))
            scores_b = scores + bias[None, :]
            gs = scores_b.reshape(-1, G, E // G)
            group_scores = jnp.sum(jax.lax.top_k(gs, 2)[0], axis=-1)
            gidx = jax.lax.top_k(group_scores, KG)[1]
            rows = jnp.arange(group_scores.shape[0])[:, None]
            group_mask = jnp.zeros_like(group_scores).at[rows, gidx].set(1.0)
            score_mask = jnp.repeat(group_mask, E // G, axis=-1) > 0
            tmp = jnp.where(score_mask, scores_b, -jnp.inf)
            topk_ids = jax.lax.top_k(tmp, K)[1]
            topk_w = jnp.take_along_axis(scores, topk_ids, axis=-1)
            topk_w = topk_w / jnp.sum(topk_w, axis=-1, keepdims=True)
            return (topk_w * SCALE, topk_ids)

        def _routed_moe(x, topk_w, topk_ids, w_gate, w_up, w_down):
            Tn = x.shape[0]
            flat_e = topk_ids.reshape(-1)
            order = jnp.argsort(flat_e)
            se = flat_e[order]
            pos = jnp.arange(Tn * K) - jnp.searchsorted(se, se, side='left')
            tok = order // K
            valid = pos < CAP
            slot = jnp.where(valid, pos, CAP)
            buf = jnp.zeros((E, CAP + 1, H), x.dtype).at[se, slot].set(x[tok])[:, :CAP]
            h = jax.nn.silu(jnp.einsum('ech,ehf->ecf', buf, w_gate)) * jnp.einsum('ech,ehf->ecf', buf, w_up)
            out = jnp.einsum('ecf,efh->ech', h, w_down)
            gathered = out[se, jnp.minimum(pos, CAP - 1)] * valid.astype(x.dtype)[:, None]
            w = topk_w.reshape(-1)[order].astype(x.dtype)[:, None]
            return jax.ops.segment_sum(gathered * w, tok, num_segments=Tn)
        key = jax.random.key(seed)
        ks = jax.random.split(key, 9)
        s = 0.02
        return dict(hidden_states=jax.random.normal(ks[0], (2, 128, H), jnp.float32), gate_w=jax.random.normal(ks[1], (H, E), jnp.float32) * s, bias=jax.random.normal(ks[2], (E,), jnp.float32) * s, w_gate=jax.random.normal(ks[3], (E, H, F), jnp.float32) * s, w_up=jax.random.normal(ks[4], (E, H, F), jnp.float32) * s, w_down=jax.random.normal(ks[5], (E, F, H), jnp.float32) * s, ws_gate=jax.random.normal(ks[6], (H, SHARED_F), jnp.float32) * s, ws_up=jax.random.normal(ks[7], (H, SHARED_F), jnp.float32) * s, ws_down=jax.random.normal(ks[8], (SHARED_F, H), jnp.float32) * s)
    _L0_ffn_in = _L0_ffn_setup()
    _d = {'L0_attn_x': _L0_attn_in['x'], 'L0_attn_w_aq': _L0_attn_in['w_aq'], 'L0_attn_w_ak': _L0_attn_in['w_ak'], 'L0_attn_w_av': _L0_attn_in['w_av'], 'L0_attn_w_ao': _L0_attn_in['w_ao'], 'L0_ffn_gate_w': _L0_ffn_in['gate_w'], 'L0_ffn_bias': _L0_ffn_in['bias'], 'L0_ffn_w_gate': _L0_ffn_in['w_gate'], 'L0_ffn_w_up': _L0_ffn_in['w_up'], 'L0_ffn_w_down': _L0_ffn_in['w_down'], 'L0_ffn_ws_gate': _L0_ffn_in['ws_gate'], 'L0_ffn_ws_up': _L0_ffn_in['ws_up'], 'L0_ffn_ws_down': _L0_ffn_in['ws_down']}
    _x0 = _d['L0_attn_x']
    _d['L0_attn_x'] = jax.random.normal(jax.random.fold_in(jax.random.key(seed), 1), (2, 1024, 256), dtype=_x0.dtype)
    del _x0
    return _d

def reference(L0_attn_x, L0_attn_w_aq, L0_attn_w_ak, L0_attn_w_av, L0_attn_w_ao, L0_ffn_gate_w, L0_ffn_bias, L0_ffn_w_gate, L0_ffn_w_up, L0_ffn_w_down, L0_ffn_ws_gate, L0_ffn_ws_up, L0_ffn_ws_down):

    def _L0_attn_ref(x, w_aq, w_ak, w_av, w_ao):
        import jax, jax.numpy as jnp
        import numpy as np
        ROPE_THETA = 10000.0
        INF_APPROX = 1e+30
        D_HEAD = 128

        def _rope(x, theta=ROPE_THETA):
            *_, L, D = x.shape
            half = D // 2
            pos = jnp.arange(L, dtype=jnp.float32)[:, None]
            freqs = jnp.power(theta, -jnp.arange(half, dtype=jnp.float32) / half)[None, :]
            angles = pos * freqs
            cos = jnp.cos(angles).astype(x.dtype)
            sin = jnp.sin(angles).astype(x.dtype)
            even, odd = jnp.split(x, 2, axis=-1)
            r_even = even * cos - odd * sin
            r_odd = even * sin + odd * cos
            return jnp.concatenate([r_even, r_odd], axis=-1)
        B, T, M = x.shape
        q = jnp.einsum('bim,ghmd->bghid', x, w_aq)
        k = jnp.einsum('bim,gmd->bgid', x, w_ak)
        v = jnp.einsum('bim,gmd->bgid', x, w_av)
        q = _rope(q)
        k = _rope(k)
        qk_mult = jnp.asarray(D_HEAD ** (-0.25), dtype=x.dtype)
        s = jnp.einsum('bghid,bgjd->bghij', q * qk_mult, k * qk_mult)
        i = jnp.arange(T)[:, None]
        j = jnp.arange(T)[None, :]
        mask = (i < j).astype(s.dtype)
        s = s - jnp.asarray(INF_APPROX, dtype=s.dtype) * mask
        p = jax.nn.softmax(s, axis=-1)
        o = jnp.einsum('bghij,bgjd->bghid', p, v)
        r = jnp.einsum('bghid,ghdm->bim', o, w_ao)
        return r

    def _L0_ffn_ref(hidden_states, gate_w, bias, w_gate, w_up, w_down, ws_gate, ws_up, ws_down):
        import jax, jax.numpy as jnp
        import numpy as np
        E, K, H, F = (64, 6, 256, 96)
        G, KG = (8, 4)
        SHARED_F = 96
        SCALE = 2.5
        T = 2 * 128
        CAP = 2 * (T * K // E)

        def _grouped_topk(logits, bias):
            scores = jax.nn.sigmoid(logits.astype(jnp.float32))
            scores_b = scores + bias[None, :]
            gs = scores_b.reshape(-1, G, E // G)
            group_scores = jnp.sum(jax.lax.top_k(gs, 2)[0], axis=-1)
            gidx = jax.lax.top_k(group_scores, KG)[1]
            rows = jnp.arange(group_scores.shape[0])[:, None]
            group_mask = jnp.zeros_like(group_scores).at[rows, gidx].set(1.0)
            score_mask = jnp.repeat(group_mask, E // G, axis=-1) > 0
            tmp = jnp.where(score_mask, scores_b, -jnp.inf)
            topk_ids = jax.lax.top_k(tmp, K)[1]
            topk_w = jnp.take_along_axis(scores, topk_ids, axis=-1)
            topk_w = topk_w / jnp.sum(topk_w, axis=-1, keepdims=True)
            return (topk_w * SCALE, topk_ids)

        def _routed_moe(x, topk_w, topk_ids, w_gate, w_up, w_down):
            Tn = x.shape[0]
            flat_e = topk_ids.reshape(-1)
            order = jnp.argsort(flat_e)
            se = flat_e[order]
            pos = jnp.arange(Tn * K) - jnp.searchsorted(se, se, side='left')
            tok = order // K
            valid = pos < CAP
            slot = jnp.where(valid, pos, CAP)
            buf = jnp.zeros((E, CAP + 1, H), x.dtype).at[se, slot].set(x[tok])[:, :CAP]
            h = jax.nn.silu(jnp.einsum('ech,ehf->ecf', buf, w_gate)) * jnp.einsum('ech,ehf->ecf', buf, w_up)
            out = jnp.einsum('ecf,efh->ech', h, w_down)
            gathered = out[se, jnp.minimum(pos, CAP - 1)] * valid.astype(x.dtype)[:, None]
            w = topk_w.reshape(-1)[order].astype(x.dtype)[:, None]
            return jax.ops.segment_sum(gathered * w, tok, num_segments=Tn)
        orig_shape = hidden_states.shape
        x = hidden_states.reshape(-1, H)
        router_logits = x @ gate_w
        topk_w, topk_ids = _grouped_topk(router_logits, bias)
        y = _routed_moe(x, topk_w, topk_ids, w_gate, w_up, w_down)
        shared = jax.nn.silu(x @ ws_gate) * (x @ ws_up) @ ws_down
        return (y + shared).reshape(orig_shape)
    x = L0_attn_x
    x = _layernorm(x + _L0_attn_ref(x, L0_attn_w_aq, L0_attn_w_ak, L0_attn_w_av, L0_attn_w_ao), axis=-1)
    x = _layernorm(x + _L0_ffn_ref(x, L0_ffn_gate_w, L0_ffn_bias, L0_ffn_w_gate, L0_ffn_w_up, L0_ffn_w_down, L0_ffn_ws_gate, L0_ffn_ws_up, L0_ffn_ws_down), axis=-1)
    return x

_drawn_inputs = setup_inputs


def setup_inputs(seed=0):
    import zlib

    import numpy as np

    out = dict(_drawn_inputs(seed))
    spreads = {}
    factors = {'L0_ffn_gate_w': 8.0,
     'L0_ffn_bias': 8.0,
     'L0_ffn_w_gate': 8.0,
     'L0_ffn_w_up': 8.0,
     'L0_ffn_w_down': 8.0,
     'L0_ffn_ws_gate': 5.611,
     'L0_ffn_ws_up': 5.581,
     'L0_ffn_ws_down': 5.561}
    for name, (base, spread) in spreads.items():
        noise = np.random.default_rng([zlib.crc32(name.encode()), seed]).standard_normal(out[name].shape)
        drawn = base * np.exp(spread * noise) if base else spread * noise
        out[name] = jnp.asarray(drawn.astype(out[name].dtype))
    for name, factor in factors.items():
        out[name] = (out[name] * factor).astype(out[name].dtype)
    return out
```

```python
from contextlib import ExitStack

import numpy as np

import concourse.bass as bass
from concourse import mybir

ALU = mybir.AluOpType
ACT = mybir.ActivationFunctionType
AX_X = mybir.AxisListType.X
F32 = mybir.dt.float32
F32R = mybir.dt.float32r
BF16 = mybir.dt.bfloat16
U32 = mybir.dt.uint32

P = 128
B, T, M = 2, 1024, 256
G, H, D = 4, 4, 128
NT = T // P
MC = M // P
HD = H * D
NEG = -1e30
EPS = 1e-5
E, K, F = 64, 6, 96
EG, KG = 8, 4
SCALE = 2.5
CAP = 2 * (256 * K // E)
PAIRS = E // 2
WB = 8
EB = 4
SLOTS = 2 * CAP
TOKENS = B * T
W_AT, S_AT, T_AT, ROW = M, M + K, M + 2 * K, M + 16
FAR = 1.0e5

UNITS = NT * G
HEADS = UNITS * H
PTB = 3
LAG = 2
LINKS_A_TILE = 27
EXPERT_LINKS = 6
RING = 3
XB = 3
BLOCKS = ["K", "V", 0, 1, 2, 3]


def schedule():
    seq, waiting = [], []

    def product():
        u, j = waiting.pop(0)
        if j == 0:
            seq.append(("linv", u))
        seq.append(("pv", u, j))
        if j == u // G:
            seq.append(("omul", u))

    def tick(n, misc):
        u, h = divmod(n, H)
        if u < UNITS:
            seq.append(("score", u, h))
        first = True
        if n >= H + 1:
            bu, bh = divmod(n - H - 1, H)
            tiles = bu // G + 1
            for j in range(-(-bh * tiles // H), -(-(bh + 1) * tiles // H)):
                seq.append(("ptrans", bu, j))
                waiting.append((bu, j))
                if len(waiting) > LAG:
                    product()
                if first and u < UNITS:
                    seq.append(("exp", u, h))
                first = False
        if first and u < UNITS:
            seq.append(("exp", u, h))
        seq.extend(misc)

    def misc(i, g, h):
        n, p = i + 1, i - 1
        nx, pv = n < NT, p >= 0
        out = []
        at = (g, h)
        if h == 0 and g < 3:
            out += [("proj", i, g + 1)]
        if h == 2 and g < 3:
            out += [("qkt", i, g + 1)]
        if pv:
            out += {(1, 3): [("outproj", p)], (2, 0): [("norm", p)], (2, 1): [("x1t", p)], (2, 3): [("rtr", p)],
                    (3, 0): [("pick", p)], (3, 1): [("ht", p), ("count", p)], (3, 2): [("sd", p)],
                    (3, 3): [("place", p)]}.get(at, [])
        if nx:
            out += {(2, 2): [("xt", n)], (2, 3): [("proj", n, "K")], (3, 0): [("proj", n, "V")],
                    (3, 1): [("qkt", n, "K"), ("proj", n, 0)], (3, 3): [("qkt", n, 0)]}.get(at, [])
        return out

    seq += [("xt", 0), ("proj", 0, "K"), ("proj", 0, "V"), ("qkt", 0, "K"), ("proj", 0, 0), ("qkt", 0, 0)]
    for n in range(HEADS):
        u, h = divmod(n, H)
        i, g = divmod(u, G)
        if i > 0 and (g, h) == (1, 3):
            while waiting and waiting[0][0] < i * G:
                product()
        tick(n, misc(i, g, h))
    for n in range(HEADS, HEADS + H + 1):
        tick(n, [])
    while waiting:
        product()
    p = NT - 1
    seq += [(s, p) for s in ("outproj", "norm", "x1t", "rtr", "pick", "ht", "count", "sd", "place")]
    return seq


RINGED = ("xt", "proj", "qkt", "ptrans", "linv", "outproj", "x1t", "rtr", "ht", "count", "sd")


def ring_places(seq):
    places, n = {}, 0
    for s in seq:
        if s[0] in RINGED:
            places[s] = (n % RING, n // RING)
            n += 1
    return places, [len(range(r, n, RING)) for r in range(RING)]


SEQ = schedule()
PLACE, TURNS = ring_places(SEQ)
PT_AT = {s[1:]: n for n, s in enumerate(s for s in SEQ if s[0] == "ptrans")}
PT_ALL = len(PT_AT)
PROJ_AT = {s[1:]: n for n, s in enumerate(s for s in SEQ if s[0] == "proj")}
ROPE_AT = {k: n for n, k in enumerate(k for k in PROJ_AT if k[1] != "V")}
QKT_AT = {s[1:]: n for n, s in enumerate(s for s in SEQ if s[0] == "qkt")}
assert [s[1:] for s in SEQ if s[0] == "qkt"] == list(ROPE_AT)


def build(nc, x, w_aq, w_ak, w_av, w_ao, gate_w, bias, w_gate, w_up, w_down, ws_gate, ws_up, ws_down,
          rope_cos, rope_sin, out):
    slot_rows = nc.dram_tensor("slot_rows", (E * CAP, ROW), F32, kind="Internal").ap()
    expert_rows = nc.dram_tensor("expert_rows", (TOKENS * K, M), F32, kind="Internal").ap()
    z_rows = nc.dram_tensor("z_rows", (TOKENS, M), F32, kind="Internal").ap()
    xf = x.rearrange("b t m -> (b t) m")
    of = out.rearrange("b t m -> (b t) m")

    with ExitStack() as ctx:
        def sb(name, shape, dt, where=ctx):
            return where.enter_context(nc.sbuf_tensor(name, shape, dt))

        def sem(name):
            return ctx.enter_context(nc.semaphore(name))

        ident = sb("ident", [P, P], F32)
        ident_bf = sb("ident_bf", [P, P], BF16)
        causal_bf = sb("causal_bf", [P, P], BF16)
        before_bf = sb("before_bf", [P, P], BF16)
        ones_bf = sb("ones_bf", [P, P], BF16)
        minus_half = sb("minus_half", [P, 1], F32)
        iota_e = sb("iota_e", [P, E], F32)
        choice_far = sb("choice_far", [P, K], F32)
        pool_cell = sb("pool_cell", [P, 2], F32)
        dve_cell = sb("dve_cell", [P, 1], F32)
        held = sb("held", [1, 8], F32)
        bias_sb = sb("bias_sb", [P, E], F32)
        blank = sb("blank", [P, ROW], F32)
        token = sb("token", [P, 1], F32)
        taken = sb("taken", [P, E], BF16)
        wr_hi = sb("wr_hi", [P, MC, 256], F32R)
        wr_lo = sb("wr_lo", [P, MC, 256], F32R)
        wsd_hi = sb("wsd_hi", [F, M], F32R)
        wsd_lo = sb("wsd_lo", [F, M], F32R)

        att = ExitStack()
        w_hi = sb("w_hi", [P, 6, H, MC, D], F32R, att)
        w_lo = sb("w_lo", [P, 6, H, MC, D], F32R, att)
        wo = sb("wo", [P, G * H, M], F32, att)
        kt_hi = sb("kt_hi", [P, G, T], F32R, att)
        kt_lo = sb("kt_lo", [P, G, T], F32R, att)
        v_sb = sb("v_sb", [P, NT, G * D], F32, att)
        probs = sb("probs", [P, 2, H, T], F32, att)
        pt = sb("pt", [P, PTB, HD], F32, att)
        qt_hi = sb("qt_hi", [P, 2, HD], F32R, att)
        qt_lo = sb("qt_lo", [P, 2, HD], F32R, att)
        cos_sb = sb("cos_sb", [P, NT, D // 2], F32, att)
        sin_sb = sb("sin_sb", [P, NT, D // 2], F32, att)
        x_sb = sb("x_sb", [P, XB, M], F32, att)
        xt_hi = sb("xt_hi", [P, MC, P], F32R, att)
        xt_lo = sb("xt_lo", [P, MC, P], F32R, att)
        q_cos = sb("q_cos", [P, H, 2, D // 2], F32, att)
        q_sin = sb("q_sin", [P, H, 2, D // 2], F32, att)
        q_rot = sb("q_rot", [P, H, 2, D // 2], F32, att)
        neg_max = sb("neg_max", [P, 8], F32, att)
        row_sum = sb("row_sum", [P, 2, H], F32, att)
        inv_sum = sb("inv_sum", [P, 2, H], F32, att)
        inv_row = sb("inv_row", [P, HD], F32, att)
        ot = sb("ot", [P, G, HD], F32, att)
        row = sb("row", [P, 2, ROW], F32, att)
        y_sb = sb("y_sb", [P, M], F32, att)
        stats = sb("stats", [P, 6], F32, att)
        mean_var = sb("mean_var", [P, 2], F32, att)
        var_eps = sb("var_eps", [P, 1], F32, att)
        rstd = sb("rstd", [P, 1], F32, att)
        x1t_hi = sb("x1t_hi", [P, MC, P], F32R, att)
        x1t_lo = sb("x1t_lo", [P, MC, P], F32R, att)
        sig = sb("sig", [P, E + F], F32, att)
        hid = sb("hid", [P, F], F32, att)
        ht_hi = sb("ht_hi", [F, P], F32R, att)
        ht_lo = sb("ht_lo", [F, P], F32R, att)
        z_sb = sb("z_sb", [P, M], F32, att)
        biased = sb("biased", [P, E], F32, att)
        top2 = sb("top2", [P, EG, 8], F32, att)
        group = sb("group", [P, EG], F32, att)
        group_top = sb("group_top", [P, 8], F32, att)
        group_at = sb("group_at", [P, 8], U32, att)
        group_atf = sb("group_atf", [P, 8], F32, att)
        kept4 = sb("kept4", [P, EG, KG], F32, att)
        kept = sb("kept", [P, EG], F32, att)
        barred = sb("barred", [P, EG], F32, att)
        open_ = sb("open_", [P, E], F32, att)
        top8 = sb("top8", [P, 8], F32, att)
        top_at = sb("top_at", [P, 8], U32, att)
        top_atf = sb("top_atf", [P, 8], F32, att)
        onehot = sb("onehot", [P, K, E], F32, att)
        onehot_s = sb("onehot_s", [P, K, E], F32, att)
        chose = sb("chose", [P, E], BF16, att)
        top_s = sb("top_s", [P, K], F32, att)
        top_sum = sb("top_sum", [P, 1], F32, att)
        top_inv = sb("top_inv", [P, 1], F32, att)
        pos6 = sb("pos6", [P, K], F32, att)
        over = sb("over", [P, K], F32, att)
        slot_u = sb("slot_u", [P, 2, K], U32, att)
        att.close()

        exp = ExitStack()
        wgu = sb("wgu", [P, WB, 2, 2, MC, F], F32, exp)
        wdn = sb("wdn", [F, WB, 2, M], F32, exp)
        srow = sb("srow", [SLOTS, WB, ROW], F32, exp)
        sxt = sb("sxt", [P, 2, MC, SLOTS], F32, exp)
        gexp = sb("gexp", [F, SLOTS], F32, exp)
        gsig = sb("gsig", [F, SLOTS], F32, exp)
        gact = sb("gact", [F, SLOTS], F32, exp)
        hid_t = sb("hid_t", [F, 2, 2, SLOTS], F32, exp)
        slot_now = sb("slot_now", [SLOTS, 1], F32, exp)
        mine = sb("mine", [SLOTS, K], F32, exp)
        mine_k = sb("mine_k", [SLOTS, K], F32, exp)
        slot_w = sb("slot_w", [SLOTS, WB], F32, exp)
        which = sb("which", [SLOTS, 1], F32, exp)
        goal = sb("goal", [SLOTS, 1], F32, exp)
        goal_u = sb("goal_u", [SLOTS, EB], U32, exp)
        erow = sb("erow", [SLOTS, EB, M], F32, exp)
        yk = sb("yk", [P, 2, K, M], F32, exp)
        zf = sb("zf", [P, 2, M], F32, exp)
        ysum = sb("ysum", [P, 2, M], F32, exp)
        fstats = sb("fstats", [P, 6], F32, exp)
        fmv = sb("fmv", [P, 2, 2], F32, exp)
        fve = sb("fve", [P, 2, 1], F32, exp)
        frs = sb("frs", [P, 2, 1], F32, exp)
        fout = sb("fout", [P, 2, M], F32, exp)
        exp.close()

        s_ps = ctx.enter_context(nc.psum_tensor("s_ps", [P, 2, T], F32))
        o_ps = ctx.enter_context(nc.psum_tensor("o_ps", [P, 512], F32))
        ring = ctx.enter_context(nc.psum_tensor("ring", [P, RING, 512], F32))

        const_ready = sem("const_ready")
        pool_own = sem("pool_own")
        w_loaded = [sem(f"w_loaded{n}") for n in range(6)]
        wo_loaded = sem("wo_loaded")
        wr_loaded = sem("wr_loaded")
        wsd_loaded = sem("wsd_loaded")
        table_loaded = sem("table_loaded")
        bias_loaded = sem("bias_loaded")
        whi_ready = sem("whi_ready")
        wlo_ready = sem("wlo_ready")
        wlo_pool_ready = sem("wlo_pool_ready")
        wmisc_hi_ready = sem("wmisc_hi_ready")
        wmisc_lo_ready = sem("wmisc_lo_ready")
        rows_free = sem("rows_free")
        picked = sem("picked")
        slot_now_ready = sem("slot_now_ready")
        dve_own2 = sem("dve_own2")
        blank_stored = sem("blank_stored")
        gate = sem("gate")
        x_loaded = [sem(f"x_loaded{n}") for n in range(XB)]
        ring_read = [sem(f"ring_read{r}") for r in range(RING)]
        xt_ready = sem("xt_ready")
        xt_hi_ready = sem("xt_hi_ready")
        proj_ready = sem("proj_ready")
        rot_ready = sem("rot_ready")
        qkt_ready = sem("qkt_ready")
        qk_hi_ready = sem("qk_hi_ready")
        scores_ready = sem("scores_ready")
        max_ready = sem("max_ready")
        probs_ready = sem("probs_ready")
        ptrans_ready = sem("ptrans_ready")
        pv_done = sem("pv_done")
        inv_ready = sem("inv_ready")
        linv_ready = sem("linv_ready")
        o_ready = sem("o_ready")
        attn_ready = sem("attn_ready")
        var_ready = sem("var_ready")
        rstd_ready = sem("rstd_ready")
        x1_ready = sem("x1_ready")
        x1t_ready = sem("x1t_ready")
        x1t_hi_ready = sem("x1t_hi_ready")
        rtr_ready = sem("rtr_ready")
        exp_ready = sem("exp_ready")
        ht_ready = sem("ht_ready")
        ht_hi_ready = sem("ht_hi_ready")
        sd_ready = sem("sd_ready")
        z_stored = sem("z_stored")
        chose_ready = sem("chose_ready")
        count_ready = sem("count_ready")
        placed = sem("placed")
        scattered = [sem(f"scattered{n}") for n in range(2)]
        stood = sem("stood")
        dve_own = sem("dve_own")

        experts_loaded = [sem(f"experts_loaded{n}") for n in range(WB)]
        srow_loaded = [sem(f"srow_loaded{n}") for n in range(WB)]
        st_ready = sem("st_ready")
        sxt_ready = sem("sxt_ready")
        gu_ready = sem("gu_ready")
        gexp_ready = sem("gexp_ready")
        hid_t_ready = sem("hid_t_ready")
        dn_ready = sem("dn_ready")
        goal_ready = sem("goal_ready")
        erow_ready = sem("erow_ready")
        erow_sent = [sem(f"erow_sent{n}") for n in range(EB)]
        yk_loaded = [sem(f"yk_loaded{n}") for n in range(2)]
        zf_loaded = [sem(f"zf_loaded{n}") for n in range(2)]
        fvar_ready = sem("fvar_ready")
        frs_ready = sem("frs_ready")
        fout_ready = sem("fout_ready")
        fin_own = sem("fin_own")
        out_stored = [sem(f"out_stored{n}") for n in range(2)]

        block = ctx.enter_context(nc.Block())

        def at(b, per, n):
            return b * per + n

        w_raw = probs[:, :, :, :].rearrange("p s h t -> p (s h t)")[:, 0:6 * H * MC * D].rearrange(
            "p (n x) -> p n x", n=6)
        w_hi_f = w_hi[:, :, :, :, :].rearrange("p n h c d -> p n (h c d)")
        w_lo_f = w_lo[:, :, :, :, :].rearrange("p n h c d -> p n (h c d)")
        raw_r = v_sb[:, 0, :].rearrange("p (c n) -> p c n", c=MC)
        raw_d = v_sb[0:F, 1, 0:M]

        PASSES = ((0, 0), (0, 1), (1, 0))

        def read(eng, b, step):
            r, turn = PLACE[step]
            eng.wait_ge(ring_read[r], at(b, TURNS[r], turn + 1))

        def reader(ins, step):
            ins.then_inc(ring_read[PLACE[step][0]], 1)

        def bank(step):
            return ring[:, PLACE[step][0], :]

        def used(eng, semaphore, n):
            if not (isinstance(n, int) and n <= 0):
                eng.wait_ge(semaphore, n)

        @block.sync
        def _(sp):
            for n, name in enumerate(BLOCKS):
                src = {"K": w_ak, "V": w_av}.get(name)
                src = w_aq[name] if src is None else src
                sp.dma_start(w_raw[:, n, :].rearrange("p (h y) -> p h y", h=H),
                             src.rearrange("h (p c) d -> p h (c d)", c=MC)).then_inc(w_loaded[n], 16)
                if n == 0:
                    sp.dma_start(cos_sb[:, :, :], rope_cos.rearrange("(n p) d -> p n d", p=P)).then_inc(table_loaded, 16)
                    sp.dma_start(sin_sb[:, :, :], rope_sin.rearrange("(n p) d -> p n d", p=P)).then_inc(table_loaded, 16)
            sp.dma_start(raw_r[:, :, 0:E], gate_w.rearrange("(p c) e -> p c e", c=MC)).then_inc(wr_loaded, 16)
            sp.dma_start(raw_r[:, :, E:E + F], ws_gate.rearrange("(p c) e -> p c e", c=MC)).then_inc(wr_loaded, 16)
            sp.dma_start(raw_r[:, :, E + F:], ws_up.rearrange("(p c) e -> p c e", c=MC)).then_inc(wr_loaded, 16)
            sp.dma_start(raw_d, ws_down).then_inc(wsd_loaded, 16)
            sp.dma_start(wo[:, :, :], w_ao.rearrange("g h d m -> d (g h) m")).then_inc(wo_loaded, 16)
            sp.dma_start(bias_sb[:, :], bias.rearrange("(a e) -> a e", a=1).to_broadcast([P, E])).then_inc(bias_loaded, 16)
            sp.wait_ge(const_ready, 1)
            sp.dma_start(slot_rows.rearrange("(p n) r -> p n r", p=P),
                         blank[:, :].rearrange("p (a r) -> p a r", a=1).to_broadcast([P, E * CAP // P, ROW])
                         ).then_inc(blank_stored, 16)
            sp.dma_start(expert_rows.rearrange("(p n) m -> p n m", p=P),
                         blank[:, 0:M].rearrange("p (a r) -> p a r", a=1).to_broadcast([P, TOKENS * K // P, M])
                         ).then_inc(blank_stored, 16)
            with sp.Fori(0, B) as b:
                sp.wait_ge(gate, at(b, 1, 1))

                def load_x(i):
                    sp.dma_start(x_sb[:, i % XB, :], xf[bass.ds(b * T + i * P, P), :]).then_inc(x_loaded[i % XB], 16)

                load_x(0)
                load_x(1)
                for s in SEQ:
                    if s[0] == "xt" and 1 <= s[1] < NT - 1:
                        i = s[1] + 1
                        if i >= XB:
                            sp.wait_ge(var_ready, at(b, NT, i - XB + 1))
                        load_x(i)
                    if s[0] == "sd":
                        i = s[1]
                        read(sp, b, s)
                        sp.dma_start(z_rows[bass.ds(b * T + i * P, P), :], z_sb[:, :]).then_inc(z_stored, 16)
            sp.wait_ge(z_stored, 16 * B * NT)

            sp.wait_ge(gate, B + 1)

            def load_pair(n, k):
                for a, w in enumerate((w_gate, w_up)):
                    for e in range(2):
                        sp.dma_start(wgu[:, k, e, a, :, :],
                                     w[bass.ds(2 * n + e, 1), :, :].rearrange("a (p c) f -> p (a c) f", c=MC)
                                     ).then_inc(experts_loaded[k], 16)
                sp.dma_start(wdn[:, k, :, :], w_down[bass.ds(2 * n, 2), :, :].rearrange("e f m -> f e m")
                             ).then_inc(experts_loaded[k], 16)

            def load_slots(n, k):
                sp.dma_start(srow[:, k, :], slot_rows[bass.ds(n * SLOTS, SLOTS), :]).then_inc(srow_loaded[k], 16)

            for k in range(WB):
                load_pair(k, k)
            for n in range(2):
                sp.wait_ge(scattered[n], 8 * K * B * NT)
            for k in range(WB):
                load_slots(k, k)
            with sp.Fori(1, PAIRS // WB) as r:
                for k in range(WB):
                    sp.wait_ge(dn_ready, at(r, WB, k + 1 - WB))
                    load_slots(r * WB + k, k)
                    load_pair(r * WB + k, k)
            for n in range(EB):
                sp.wait_ge(erow_sent[n], 16 * (PAIRS // EB))

            def sums(t, k):
                used(sp, fvar_ready, t - 1)
                sp.dma_start(yk[:, k, :, :], expert_rows[bass.ds(t * P * K, P * K), :].rearrange(
                    "(p k) m -> p k m", k=K)).then_inc(yk_loaded[k], 16)
                sp.dma_start(zf[:, k, :], z_rows[bass.ds(t * P, P), :]).then_inc(zf_loaded[k], 16)

            def store(t, k):
                sp.wait_ge(fout_ready, t + 1)
                sp.dma_start(of[bass.ds(t * P, P), :], fout[:, k, :]).then_inc(out_stored[k], 16)

            sums(0, 0)
            sums(1, 1)
            with sp.Fori(1, B * NT // 2) as r:
                for k in range(2):
                    sums(r * 2 + k, k)
                    store(r * 2 + k - 2, k)
            for k in range(2):
                store(B * NT - 2 + k, k)
            for k in range(2):
                sp.wait_ge(out_stored[k], 16 * (B * NT // 2))

        @block.gpsimd
        def _(pool):
            own = [0]

            def link(ins):
                own[0] += 1
                ins.then_inc(pool_own, 1)
                pool.wait_ge(pool_own, own[0])

            link(pool.memset(blank[:, :], 0.0))
            pool.memset(blank[:, S_AT:S_AT + K], -1.0).then_inc(const_ready, 1)
            link(pool.memset(ident[:, :], 0.0))
            link(pool.affine_select(out=ident[:, :], in_=ident[:, :], compare_op=ALU.not_equal, fill=1.0, base=0,
                                    pattern=[[-1, P]], channel_multiplier=1))
            link(pool.tensor_copy(ident_bf[:, :], ident[:, :]))
            link(pool.memset(causal_bf[:, :], 0.0))
            link(pool.affine_select(out=causal_bf[:, :], in_=causal_bf[:, :], compare_op=ALU.is_ge, fill=NEG, base=0,
                                    pattern=[[-1, P]], channel_multiplier=1))
            link(pool.memset(before_bf[:, :], 0.0))
            link(pool.affine_select(out=before_bf[:, :], in_=before_bf[:, :], compare_op=ALU.is_ge, fill=1.0, base=0,
                                    pattern=[[-1, P]], channel_multiplier=1))
            link(pool.memset(ones_bf[:, :], 1.0))
            link(pool.memset(minus_half[:, :], -0.5))
            link(pool.memset(taken[:, :], 0.0))
            link(pool.memset(row[:, :, :], 0.0))
            link(pool.iota(iota_e[:, :], pattern=[[1, E]], base=0, channel_multiplier=0,
                           allow_small_or_imprecise_dtypes=True))
            link(pool.iota(choice_far[:, :], pattern=[[1, K]], base=-int(FAR), channel_multiplier=0,
                           allow_small_or_imprecise_dtypes=True))
            pool.iota(token[:, :], pattern=[[0, 1]], base=-P, channel_multiplier=1,
                      allow_small_or_imprecise_dtypes=True).then_inc(const_ready, 1)
            for n in (4, 5):
                pool.wait_ge(whi_ready, n + 1)
                pool.tensor_tensor(w_lo_f[:, n, :], w_raw[:, n, :], w_hi_f[:, n, :].bitcast(F32), ALU.subtract
                                   ).then_inc(wlo_pool_ready, 1)
            pool.wait_ge(blank_stored, 32)
            pool.memset(pool_cell[:, 1:2], 0.0).then_inc(rows_free, 1)

            def stand(n):
                used(pool, stood, n)
                pool.tensor_tensor(pool_cell[:, 0:1], minus_half[:, :], minus_half[:, :], ALU.mult).then_inc(stood, 1)

            with pool.Fori(0, B) as b:
                pool.wait_ge(gate, at(b, 1, 1))
                for s in SEQ:
                    if s[0] == "proj" and s[2] != "V":
                        n = ROPE_AT[s[1:]]
                        read(pool, b, s)
                        if n >= 1:
                            pool.wait_ge(qkt_ready, at(b, len(ROPE_AT), n))
                        pool.tensor_tensor(q_rot[:, :, 0, :], q_cos[:, :, 0, :], q_sin[:, :, 1, :], ALU.subtract)
                        pool.tensor_tensor(q_rot[:, :, 1, :], q_cos[:, :, 1, :], q_sin[:, :, 0, :], ALU.add
                                           ).then_inc(rot_ready, 1)
                    if s[0] == "outproj":
                        pool.wait_ge(var_ready, at(b, NT, s[1] + 1))
                        pool.tensor_tensor(rstd[:, :], var_eps[:, :], minus_half[:, :], ALU.pow).then_inc(rstd_ready, 1)
                    if s[0] == "place":
                        i = s[1]
                        pool.wait_ge(placed, at(b, NT, i + 1))
                        stand(at(b, NT, i))
                        for k in range(K):
                            pool.indirect_dma_start(
                                slot_rows[:, :], bass.IndirectOffsetOnAxis(ap=slot_u[:, i % 2, k:k + 1], axis=0),
                                row[:, i % 2, :], None, bounds_check=E * CAP - 1, oob_is_err=False
                            ).then_inc(scattered[i % 2], 16)
                for n in range(2):
                    pool.wait_ge(scattered[n], at(b, 8 * K * NT, 8 * K * NT))
                pool.tensor_tensor(pool_cell[:, 1:2], minus_half[:, :], minus_half[:, :], ALU.mult).then_inc(rows_free, 1)

            def send(n, k):
                pool.wait_ge(goal_ready, n + 1)
                pool.wait_ge(erow_ready, n + 1)
                stand(B * NT + n)
                pool.indirect_dma_start(
                    expert_rows[:, :], bass.IndirectOffsetOnAxis(ap=goal_u[:, k % EB:k % EB + 1], axis=0),
                    erow[:, k % EB, :], None, bounds_check=TOKENS * K - 1, oob_is_err=False
                ).then_inc(erow_sent[k % EB], 16)

            pool.wait_ge(gate, B + 1)
            pool.iota(slot_now[:, :], pattern=[[0, 1]], base=-SLOTS, channel_multiplier=1,
                      allow_small_or_imprecise_dtypes=True).then_inc(slot_now_ready, 1)
            pool.memset(hid_t[:, :, :, :], 0.0).then_inc(slot_now_ready, 1)
            with pool.Fori(0, PAIRS // WB) as r:
                for k in range(WB):
                    send(r * WB + k, k)
            with pool.Fori(0, B * NT // 2) as r:
                for k in range(2):
                    pool.wait_ge(fvar_ready, at(r, 2, k + 1))
                    pool.tensor_tensor(frs[:, k, :], fve[:, k, :], minus_half[:, :], ALU.pow).then_inc(frs_ready, 1)

        @block.scalar
        def _(act):
            def split(hi, raw):
                return act.activation(hi, raw, ACT.Copy)

            for n in range(6):
                act.wait_ge(w_loaded[n], 16)
                split(w_hi_f[:, n, :], w_raw[:, n, :]).then_inc(whi_ready, 1)
            act.wait_ge(wr_loaded, 48)
            split(wr_hi[:, :, :], raw_r).then_inc(wmisc_hi_ready, 1)
            act.wait_ge(wsd_loaded, 16)
            split(wsd_hi[:, :], raw_d).then_inc(wmisc_hi_ready, 1)
            act.wait_ge(wmisc_lo_ready, 2)

            with act.Fori(0, B) as b:
                act.wait_ge(gate, at(b, 1, 1))
                for s in SEQ:
                    kind = s[0]
                    if kind == "xt":
                        act.wait_ge(xt_ready, at(b, NT, s[1] + 1))
                        if s[1] >= 1:
                            act.wait_ge(proj_ready, at(b, len(PROJ_AT), 6 * s[1]))
                        split(xt_hi[:, :, :], bank(s)[:, 0:MC * P].rearrange("p (c t) -> p c t", c=MC)
                              ).then_inc(xt_hi_ready, 1)
                    if kind == "proj" and s[2] == "V":
                        act.wait_ge(proj_ready, at(b, len(PROJ_AT), PROJ_AT[s[1:]] + 1))
                        reader(act.activation(v_sb[:, s[1], :], bank(s), ACT.Copy), s)
                    if kind == "qkt":
                        i, name = s[1:]
                        act.wait_ge(qkt_ready, at(b, len(QKT_AT), QKT_AT[s[1:]] + 1))
                        if name == "K":
                            dst, src = kt_hi[:, :, i * P:(i + 1) * P], bank(s).rearrange("p (g t) -> p g t", g=G)
                        else:
                            u = i * G + name
                            dst, src = qt_hi[:, u % 2, :], bank(s)
                            if u >= 2:
                                act.wait_ge(scores_ready, at(b, HEADS, H * (u - 1)))
                        split(dst, src).then_inc(qk_hi_ready, 1)
                    if kind == "exp":
                        u, h = s[1:]
                        i, n = u // G, u * H + h
                        act.wait_ge(max_ready, at(b, HEADS, n + 1))
                        if u < 2:
                            act.wait_ge(wlo_ready, 4)
                            act.wait_ge(wlo_pool_ready, 2)
                        else:
                            act.wait_ge(ptrans_ready, at(b, PT_ALL, PT_AT[(u - 2, (u - 2) // G)] + 1))
                            act.wait_ge(inv_ready, at(b, UNITS, u - 1))
                        act.activation(probs[:, u % 2, h, 0:(i + 1) * P], s_ps[:, n % 2, 0:(i + 1) * P], ACT.Exp,
                                       bias=neg_max[:, n % 8:n % 8 + 1],
                                       accum_out=row_sum[:, u % 2, h:h + 1]).then_inc(probs_ready, 1)
                    if kind == "ptrans":
                        n = PT_AT[s[1:]]
                        act.wait_ge(ptrans_ready, at(b, PT_ALL, n + 1))
                        if n >= PTB:
                            act.wait_ge(pv_done, at(b, PT_ALL, n - PTB + 1))
                        reader(act.activation(pt[:, n % PTB, :], bank(s), ACT.Copy), s)
                    if kind == "linv":
                        u = s[1]
                        act.wait_ge(linv_ready, at(b, UNITS, u + 1))
                        if u >= 1:
                            act.wait_ge(o_ready, at(b, UNITS, u))
                        reader(act.activation(inv_row[:, :], bank(s), ACT.Copy), s)
                    if kind == "x1t":
                        act.wait_ge(x1t_ready, at(b, NT, s[1] + 1))
                        if s[1] >= 1:
                            act.wait_ge(rtr_ready, at(b, NT, s[1]))
                        split(x1t_hi[:, :, :], bank(s)[:, 0:MC * P].rearrange("p (c t) -> p c t", c=MC)
                              ).then_inc(x1t_hi_ready, 1)
                    if kind == "rtr":
                        act.wait_ge(rtr_ready, at(b, NT, s[1] + 1))
                        if s[1] >= 1:
                            act.wait_ge(picked, at(b, NT, s[1]))
                        act.activation(sig[:, :], bank(s)[:, 0:E + F], ACT.Exp, scale=-1.0).then_inc(exp_ready, 1)
                    if kind == "ht":
                        act.wait_ge(ht_ready, at(b, NT, s[1] + 1))
                        if s[1] >= 1:
                            act.wait_ge(sd_ready, at(b, NT, s[1]))
                        split(ht_hi[:, :], bank(s)[0:F, 0:P]).then_inc(ht_hi_ready, 1)

            act.wait_ge(gate, B + 1)

            def slots_in(n, k):
                act.wait_ge(st_ready, n + 1)
                used(act, gu_ready, n - 1)
                act.activation(sxt[:, k % 2, :, :], s_ps[:, k % 2, 0:MC * SLOTS].rearrange("p (c s) -> p c s", c=MC),
                               ACT.Copy).then_inc(sxt_ready, 1)

            def gate_exp(n, k):
                act.wait_ge(gu_ready, n + 1)
                used(act, hid_t_ready, n)
                act.activation(gexp[:, :], s_ps[0:F, k % 2, 512:512 + SLOTS], ACT.Exp, scale=-1.0
                               ).then_inc(gexp_ready, 1)

            def rows_out(n, k):
                act.wait_ge(dn_ready, n + 1)
                act.activation(erow[:, k % EB, :], ring[0:SLOTS, k % 2, 0:M], ACT.Copy, scale=slot_w[:, k:k + 1]
                               ).then_inc(erow_ready, 1)

            def expert_round(r):
                slots_in(at(r, WB, 0), 0)
                for k in range(WB + 1):
                    if k + 1 < WB:
                        slots_in(at(r, WB, k + 1), k + 1)
                    if k < WB:
                        gate_exp(at(r, WB, k), k)
                    if k >= 1:
                        used(act, erow_sent[(k - 1) % EB], at(r, 16 * WB // EB, 16 * ((k - 1) // EB)))
                        rows_out(at(r, WB, k - 1), k - 1)

            expert_round(0)
            with act.Fori(1, PAIRS // WB) as r:
                expert_round(r)

        @block.tensor
        def _(pe):
            def begin(b, step):
                r, turn = PLACE[step]
                if turn >= 1:
                    pe.wait_ge(ring_read[r], at(b, TURNS[r], turn))

            pe.wait_ge(const_ready, 2)
            with pe.Fori(0, B) as b:
                pe.wait_ge(gate, at(b, 1, 1))
                for s in SEQ:
                    kind = s[0]
                    if kind in RINGED:
                        begin(b, s)
                    if kind == "xt":
                        i = s[1]
                        pe.wait_ge(x_loaded[i % XB], at(b, 16 * len(range(i % XB, NT, XB)), 16 * (i // XB + 1)))
                        xc = x_sb[:, i % XB, :].rearrange("t (p c) -> t c p", c=MC)
                        for c in range(MC):
                            ins = pe.transpose(bank(s)[:, c * P:(c + 1) * P], xc[:, c, :], ident[:, :])
                        ins.then_inc(xt_ready, 1)
                    if kind == "proj":
                        i, name = s[1:]
                        n = BLOCKS.index(name)
                        read(pe, b, ("xt", i))
                        pe.wait_ge(whi_ready, n + 1)
                        if n < 4:
                            pe.wait_ge(wlo_ready, n + 1)
                        else:
                            pe.wait_ge(wlo_pool_ready, n - 3)
                        for c in range(MC):
                            for xp, wp in PASSES:
                                ins = pe.matmul(bank(s), (xt_hi, xt_lo)[xp][:, c, :], (w_hi, w_lo)[wp][:, n, :, c, :],
                                                start=(c == 0 and xp == wp == 0), stop=(c == MC - 1 and xp == 1))
                        ins.then_inc(proj_ready, 1)
                    if kind == "qkt":
                        pe.wait_ge(rot_ready, at(b, len(QKT_AT), QKT_AT[s[1:]] + 1))
                        for h in range(H):
                            ins = pe.transpose(bank(s)[:, h * P:(h + 1) * P],
                                               q_rot[:, h, :, :].rearrange("p a d -> p (a d)"), ident[:, :])
                        ins.then_inc(qkt_ready, 1)
                    if kind == "score":
                        u, h = s[1:]
                        (i, g), n = divmod(u, G), u * H + h
                        read(pe, b, ("qkt", i, g))
                        if h == 0:
                            read(pe, b, ("qkt", i, "K"))
                        if n >= 2:
                            pe.wait_ge(probs_ready, at(b, HEADS, n - 1))
                        q = [z[:, u % 2, h * P:(h + 1) * P] for z in (qt_hi, qt_lo)]
                        k = [z[:, g, :] for z in (kt_hi, kt_lo)]
                        width = (i + 1) * P
                        for a in range(0, width, 512):
                            e = min(a + 512, width)
                            last = e == width
                            for qp, kp in PASSES:
                                pe.matmul(s_ps[:, n % 2, a:e], q[qp], k[kp][:, a:e],
                                          start=(qp == kp == 0), stop=(qp == 1 and not last))
                            if last:
                                ins = pe.matmul(s_ps[:, n % 2, i * P:e], ident_bf[:, :], causal_bf[:, :],
                                                start=False, stop=True)
                        ins.then_inc(scores_ready, 1)
                    if kind == "ptrans":
                        u, j = s[1:]
                        pe.wait_ge(probs_ready, at(b, HEADS, H * (u + 1)))
                        for h in range(H):
                            ins = pe.transpose(bank(s)[:, h * P:(h + 1) * P], probs[:, u % 2, h, j * P:(j + 1) * P],
                                               ident[:, :])
                        ins.then_inc(ptrans_ready, 1)
                    if kind == "pv":
                        u, j = s[1:]
                        (i, g), n = divmod(u, G), PT_AT[s[1:]]
                        read(pe, b, ("ptrans", u, j))
                        if g == 0 and j == i:
                            read(pe, b, ("proj", i, "V"))
                        if j == 0 and u >= 1:
                            pe.wait_ge(o_ready, at(b, UNITS, u))
                        pe.matmul(o_ps[:, :], v_sb[:, j, g * D:(g + 1) * D], pt[:, n % PTB, :],
                                  start=(j == 0), stop=(j == i)).then_inc(pv_done, 1)
                    if kind == "linv":
                        u = s[1]
                        pe.wait_ge(inv_ready, at(b, UNITS, u + 1))
                        for h in range(H):
                            ins = pe.transpose(bank(s)[:, h * P:(h + 1) * P],
                                               inv_sum[:, u % 2, h:h + 1].to_broadcast([P, P]), ident[:, :])
                        ins.then_inc(linv_ready, 1)
                    if kind == "outproj":
                        i = s[1]
                        pe.wait_ge(wo_loaded, 16)
                        pe.wait_ge(o_ready, at(b, UNITS, G * (i + 1)))
                        for h in range(G * H):
                            ins = pe.matmul(bank(s)[:, 0:M], ot[:, h // H, (h % H) * P:(h % H + 1) * P], wo[:, h, :],
                                            start=(h == 0), stop=(h == G * H - 1))
                        ins.then_inc(attn_ready, 1)
                    if kind == "x1t":
                        i = s[1]
                        pe.wait_ge(x1_ready, at(b, NT, i + 1))
                        xc = row[:, i % 2, 0:M].rearrange("t (p c) -> t c p", c=MC)
                        for c in range(MC):
                            ins = pe.transpose(bank(s)[:, c * P:(c + 1) * P], xc[:, c, :], ident[:, :])
                        ins.then_inc(x1t_ready, 1)
                    if kind == "rtr":
                        read(pe, b, ("x1t", s[1]))
                        pe.wait_ge(wmisc_lo_ready, 2)
                        for c in range(MC):
                            for xp, wp in PASSES:
                                ins = pe.matmul(bank(s)[:, 0:E + 2 * F], (x1t_hi, x1t_lo)[xp][:, c, :],
                                                (wr_hi, wr_lo)[wp][:, c, :],
                                                start=(c == 0 and xp == wp == 0), stop=(c == MC - 1 and xp == 1))
                        ins.then_inc(rtr_ready, 1)
                    if kind == "ht":
                        read(pe, b, ("rtr", s[1]))
                        pe.transpose(bank(s)[0:F, 0:P], hid[:, :], ident[:, :]).then_inc(ht_ready, 1)
                    if kind == "count":
                        pe.wait_ge(chose_ready, at(b, NT, s[1] + 1))
                        pe.matmul(bank(s)[:, 0:E], before_bf[:, :], chose[:, :], start=True, stop=False)
                        pe.matmul(bank(s)[:, 0:E], ones_bf[:, :], taken[:, :], start=False, stop=True
                                  ).then_inc(count_ready, 1)
                    if kind == "sd":
                        read(pe, b, ("ht", s[1]))
                        for n, (hp, wp) in enumerate(PASSES):
                            ins = pe.matmul(bank(s)[:, 0:M], (ht_hi, ht_lo)[hp][:, :], (wsd_hi, wsd_lo)[wp][:, :],
                                            start=(n == 0), stop=(n == 2))
                        ins.then_inc(sd_ready, 1)

            pe.wait_ge(gate, B + 1)

            def slots_t(r, k):
                n = at(r, WB, k)
                pe.wait_ge(srow_loaded[k], at(r, 16, 16))
                used(pe, sxt_ready, n - 1)
                xc = srow[:, k, 0:M].rearrange("t (p c) -> t c p", c=MC)
                for c in range(MC):
                    ins = pe.transpose(s_ps[:, k % 2, c * SLOTS:(c + 1) * SLOTS], xc[:, c, :],
                                       ident[0:SLOTS, 0:SLOTS])
                ins.then_inc(st_ready, 1)

            def gate_up(r, k):
                n = at(r, WB, k)
                pe.wait_ge(experts_loaded[k], at(r, 80, 80))
                pe.wait_ge(sxt_ready, n + 1)
                used(pe, hid_t_ready, n - 1)
                for a in range(2):
                    for e in range(2):
                        for c in range(MC):
                            ins = pe.matmul(s_ps[0:F, k % 2, 512 + a * SLOTS + e * CAP:512 + a * SLOTS + (e + 1) * CAP],
                                            wgu[:, k, e, a, c, :], sxt[:, k % 2, c, e * CAP:(e + 1) * CAP],
                                            start=(c == 0), stop=(c == MC - 1))
                ins.then_inc(gu_ready, 1)

            def down(r, k):
                n = at(r, WB, k)
                pe.wait_ge(hid_t_ready, n + 1)
                used(pe, erow_ready, n - 1)
                for e in range(2):
                    ins = pe.matmul(ring[0:SLOTS, k % 2, 0:M], hid_t[:, k % 2, e, :], wdn[:, k, e, :],
                                    start=(e == 0), stop=(e == 1))
                ins.then_inc(dn_ready, 1)

            def expert_round(r):
                slots_t(r, 0)
                for k in range(WB + 1):
                    if k + 1 < WB:
                        slots_t(r, k + 1)
                    if k < WB:
                        gate_up(r, k)
                    if k >= 1:
                        down(r, k - 1)

            expert_round(0)
            with pe.Fori(1, PAIRS // WB) as r:
                expert_round(r)

        @block.vector
        def _(dve):
            def low(lo, raw, hi):
                return dve.tensor_tensor(lo, raw, hi.bitcast(F32), ALU.subtract)

            for n in range(4):
                dve.wait_ge(whi_ready, n + 1)
                low(w_lo_f[:, n, :], w_raw[:, n, :], w_hi_f[:, n, :]).then_inc(wlo_ready, 1)
            dve.wait_ge(wmisc_hi_ready, 2)
            low(wr_lo[:, :, :], raw_r, wr_hi[:, :, :]).then_inc(wmisc_lo_ready, 1)
            low(wsd_lo[:, :], raw_d, wsd_hi[:, :]).then_inc(wmisc_lo_ready, 1)
            dve.wait_ge(bias_loaded, 16)
            dve.wait_ge(const_ready, 2)
            dve.wait_ge(table_loaded, 32)
            dve.memset(dve_cell[:, :], 0.0).then_inc(gate, 1)

            links = [0]

            def after(b, per, ins):
                links[0] += 1
                ins.then_inc(dve_own, 1)
                dve.wait_ge(dve_own, at(b, per, links[0]))

            def hold(n):
                dve.tensor_copy(held[0:1, n:n + 1], minus_half[0:1, :])

            def wide(ap, n):
                return ap.rearrange("p (a x) -> p a x", a=1).to_broadcast([P, n, ap.shape[1]])

            def each(ap, n):
                return ap.rearrange("p (x a) -> p x a", a=1).to_broadcast([P, ap.shape[1], n])

            LINKS = NT * LINKS_A_TILE
            with dve.Fori(0, B) as b:
                dve.wait_ge(gate, at(b, 1, 1))
                for s in SEQ:
                    kind = s[0]
                    if kind == "xt":
                        dve.wait_ge(xt_hi_ready, at(b, NT, s[1] + 1))
                        reader(low(xt_lo[:, :, :], bank(s)[:, 0:MC * P].rearrange("p (c t) -> p c t", c=MC),
                                   xt_hi[:, :, :]), s)
                    if kind == "proj" and s[2] != "V":
                        i, n = s[1], ROPE_AT[s[1:]]
                        dve.wait_ge(proj_ready, at(b, len(PROJ_AT), PROJ_AT[s[1:]] + 1))
                        if n >= 1:
                            dve.wait_ge(rot_ready, at(b, len(ROPE_AT), n))
                        src = bank(s).rearrange("p (x d) -> p x d", d=D // 2)
                        dve.tensor_tensor(q_cos[:, :, :, :].rearrange("p h a d -> p (h a) d"), src,
                                          wide(cos_sb[:, i, :], 2 * H), ALU.mult)
                        reader(dve.tensor_tensor(q_sin[:, :, :, :].rearrange("p h a d -> p (h a) d"), src,
                                                 wide(sin_sb[:, i, :], 2 * H), ALU.mult), s)
                    if kind == "qkt":
                        i, name = s[1:]
                        dve.wait_ge(qk_hi_ready, at(b, len(QKT_AT), QKT_AT[s[1:]] + 1))
                        if name == "K":
                            cols = slice(i * P, (i + 1) * P)
                            reader(low(kt_lo[:, :, cols], bank(s).rearrange("p (g t) -> p g t", g=G),
                                       kt_hi[:, :, cols]), s)
                        else:
                            u = i * G + name
                            reader(low(qt_lo[:, u % 2, :], bank(s), qt_hi[:, u % 2, :]), s)
                    if kind == "score":
                        u, h = s[1:]
                        n = u * H + h
                        dve.wait_ge(scores_ready, at(b, HEADS, n + 1))
                        dve.tensor_reduce(neg_max[:, n % 8:n % 8 + 1], s_ps[:, n % 2, 0:(u // G + 1) * P], AX_X, ALU.max,
                                          negate=True).then_inc(max_ready, 1)
                    if kind == "ptrans" and s[2] == 0:
                        u = s[1]
                        dve.wait_ge(probs_ready, at(b, HEADS, H * (u + 1)))
                        if u >= 2:
                            dve.wait_ge(linv_ready, at(b, UNITS, u - 1))
                        dve.reciprocal(inv_sum[:, u % 2, :], row_sum[:, u % 2, :]).then_inc(inv_ready, 1)
                    if kind == "omul":
                        u = s[1]
                        i, g = divmod(u, G)
                        read(dve, b, ("linv", u))
                        dve.wait_ge(pv_done, at(b, PT_ALL, PT_AT[(u, i)] + 1))
                        if i >= 1:
                            dve.wait_ge(attn_ready, at(b, NT, i))
                        dve.tensor_tensor(ot[:, g, :], o_ps[:, :], inv_row[:, :], ALU.mult).then_inc(o_ready, 1)
                    if kind == "outproj":
                        i = s[1]
                        dve.wait_ge(attn_ready, at(b, NT, i + 1))
                        reader(dve.tensor_tensor(y_sb[:, :], bank(s)[:, 0:M], x_sb[:, i % XB, :], ALU.add), s)
                        read(dve, b, s)
                        after(b, LINKS, dve.bn_stats(stats[:, :], y_sb[:, :]))
                        hold(0)
                        after(b, LINKS, dve.bn_aggr(mean_var[:, :], stats[:, :]))
                        dve.tensor_scalar(var_eps[:, :], mean_var[:, 1:2], EPS, None, ALU.add).then_inc(var_ready, 1)
                    if kind == "norm":
                        i = s[1]
                        dve.wait_ge(rstd_ready, at(b, NT, i + 1))
                        if i >= 2:
                            dve.wait_ge(scattered[i % 2], at(b, 8 * K * NT, 16 * K * (i // 2)))
                        else:
                            dve.wait_ge(rows_free, at(b, 1, 1))
                        dve.tensor_scalar(row[:, i % 2, 0:M], y_sb[:, :], mean_var[:, 0:1], rstd[:, 0:1],
                                          ALU.subtract, ALU.mult).then_inc(x1_ready, 1)
                        after(b, LINKS, dve.tensor_scalar(token[:, :], token[:, :], float(P), None, ALU.add))
                        dve.tensor_copy(row[:, i % 2, T_AT:T_AT + 1], token[:, :])
                    if kind == "x1t":
                        dve.wait_ge(x1t_hi_ready, at(b, NT, s[1] + 1))
                        reader(low(x1t_lo[:, :, :], bank(s)[:, 0:MC * P].rearrange("p (c t) -> p c t", c=MC),
                                   x1t_hi[:, :, :]), s)
                    if kind == "rtr":
                        dve.wait_ge(exp_ready, at(b, NT, s[1] + 1))
                        if s[1] >= 1:
                            dve.wait_ge(ht_ready, at(b, NT, s[1]))
                        after(b, LINKS, dve.tensor_scalar(sig[:, :], sig[:, :], 1.0, None, ALU.add))
                        after(b, LINKS, dve.reciprocal(sig[:, :], sig[:, :]))
                        after(b, LINKS, dve.tensor_tensor(hid[:, :], bank(s)[:, E:E + F], sig[:, E:], ALU.mult))
                        reader(dve.tensor_tensor(hid[:, :], bank(s)[:, E + F:E + 2 * F], hid[:, :], ALU.mult), s)
                    if kind == "pick":
                        i = s[1]
                        after(b, LINKS, dve.tensor_tensor(biased[:, :], sig[:, 0:E], bias_sb[:, :], ALU.add))
                        hold(1)
                        for n in range(EG - 1):
                            dve.max(top2[:, n, :], biased[:, n * 8:(n + 1) * 8])
                        after(b, LINKS, dve.max(top2[:, EG - 1, :], biased[:, E - 8:]))
                        after(b, LINKS, dve.tensor_tensor(group[:, :], top2[:, :, 0], top2[:, :, 1], ALU.add))
                        hold(2)
                        after(b, LINKS, dve.max(group_top[:, :], group[:, :]))
                        hold(3)
                        after(b, LINKS, dve.max_index(group_at[:, :], group_top[:, :], group[:, :]))
                        after(b, LINKS, dve.tensor_copy(group_atf[:, :], group_at[:, :]))
                        after(b, LINKS, dve.tensor_tensor(kept4[:, :, :], each(iota_e[:, 0:EG], KG),
                                                          wide(group_atf[:, 0:KG], EG), ALU.is_equal))
                        after(b, LINKS, dve.tensor_reduce(kept[:, :], kept4[:, :, :], AX_X, ALU.add))
                        dve.tensor_tensor(open_[:, :].rearrange("p (g e) -> p g e", g=EG),
                                          biased[:, :].rearrange("p (g e) -> p g e", g=EG),
                                          each(kept[:, :], E // EG), ALU.mult)
                        after(b, LINKS, dve.tensor_scalar(barred[:, :], kept[:, :], 1.0, -NEG, ALU.subtract, ALU.mult))
                        after(b, LINKS, dve.tensor_tensor(open_[:, :].rearrange("p (g e) -> p g e", g=EG),
                                                          open_[:, :].rearrange("p (g e) -> p g e", g=EG),
                                                          each(barred[:, :], E // EG), ALU.add))
                        hold(4)
                        after(b, LINKS, dve.max(top8[:, :], open_[:, :]))
                        hold(5)
                        after(b, LINKS, dve.max_index(top_at[:, :], top8[:, :], open_[:, :]))
                        after(b, LINKS, dve.tensor_copy(top_atf[:, :], top_at[:, :]))
                        after(b, LINKS, dve.tensor_tensor(onehot[:, :, :], wide(iota_e[:, :], K),
                                                          each(top_atf[:, 0:K], E), ALU.is_equal))
                        if i >= 1:
                            dve.wait_ge(count_ready, at(b, NT, i))
                        with nc.allow_low_precision("zeros and ones"):
                            dve.tensor_reduce(chose[:, :], onehot[:, :, :].rearrange("p k e -> p e k"), AX_X, ALU.add
                                              ).then_inc(chose_ready, 1)
                        after(b, LINKS, dve.tensor_tensor(onehot_s[:, :, :], onehot[:, :, :], wide(sig[:, 0:E], K), ALU.mult))
                        dve.tensor_reduce(top_s[:, :], onehot_s[:, :, :], AX_X, ALU.add).then_inc(picked, 1)
                        dve.wait_ge(picked, at(b, NT, i + 1))
                        after(b, LINKS, dve.tensor_reduce(top_sum[:, :], top_s[:, :], AX_X, ALU.add))
                        after(b, LINKS, dve.reciprocal(top_inv[:, :], top_sum[:, :]))
                        dve.tensor_scalar(row[:, i % 2, W_AT:W_AT + K], top_s[:, :], top_inv[:, 0:1], SCALE,
                                          ALU.mult, ALU.mult)
                    if kind == "ht":
                        dve.wait_ge(ht_hi_ready, at(b, NT, s[1] + 1))
                        reader(low(ht_lo[:, :], bank(s)[0:F, 0:P], ht_hi[:, :]), s)
                    if kind == "count":
                        dve.wait_ge(count_ready, at(b, NT, s[1] + 1))
                        reader(dve.tensor_tensor(onehot_s[:, :, :], onehot[:, :, :], wide(bank(s)[:, 0:E], K), ALU.mult), s)
                    if kind == "sd":
                        i = s[1]
                        dve.wait_ge(sd_ready, at(b, NT, i + 1))
                        if i >= 1:
                            dve.wait_ge(z_stored, at(b, 16 * NT, 16 * i))
                        reader(dve.tensor_tensor(z_sb[:, :], bank(s)[:, 0:M], row[:, i % 2, 0:M], ALU.add), s)
                    if kind == "place":
                        i = s[1]
                        read(dve, b, ("count", i))
                        after(b, LINKS, dve.tensor_reduce(pos6[:, :], onehot_s[:, :, :], AX_X, ALU.add))
                        with nc.allow_low_precision("at most one a tile"):
                            dve.tensor_tensor(taken[:, :], taken[:, :], chose[:, :], ALU.add)
                        after(b, LINKS, dve.tensor_scalar(over[:, :], pos6[:, :], float(CAP), FAR, ALU.is_ge, ALU.mult))
                        after(b, LINKS, dve.tensor_tensor(pos6[:, :], pos6[:, :], over[:, :], ALU.add))
                        after(b, LINKS, dve.scalar_tensor_tensor(row[:, i % 2, S_AT:S_AT + K], top_atf[:, 0:K], float(CAP),
                                                                 pos6[:, :], ALU.mult, ALU.add))
                        dve.tensor_copy(slot_u[:, i % 2, :], row[:, i % 2, S_AT:S_AT + K]).then_inc(placed, 1)
                dve.wait_ge(placed, at(b, NT, NT))
                dve.tensor_copy(dve_cell[:, :], pos6[:, 0:1]).then_inc(gate, 1)
            assert links[0] == LINKS, links[0] / NT

            dve.wait_ge(slot_now_ready, 2)
            links[0] = 0

            def expert_round(r):
                start = links[0]
                for k in range(WB):
                    n = at(r, WB, k)
                    per = EXPERT_LINKS * WB
                    dve.wait_ge(srow_loaded[k], at(r, 16, 16))
                    after(r, per, dve.tensor_scalar(slot_now[:, :], slot_now[:, :], float(SLOTS), None, ALU.add))
                    dve.scalar_tensor_tensor(mine[:, :], srow[:, k, S_AT:S_AT + K], slot_now[:, 0:1],
                                             srow[:, k, W_AT:W_AT + K], ALU.is_equal, ALU.mult,
                                             accum_out=slot_w[:, k:k + 1])
                    after(r, per, dve.scalar_tensor_tensor(mine_k[:, :], srow[:, k, S_AT:S_AT + K], slot_now[:, 0:1],
                                                           choice_far[0:SLOTS, :], ALU.is_equal, ALU.mult,
                                                           accum_out=which[:, :]))
                    after(r, per, dve.tensor_scalar(goal[:, :], srow[:, k, T_AT:T_AT + 1], float(K), which[:, 0:1],
                                                    ALU.mult, ALU.add))
                    used(dve, erow_sent[k % EB], at(r, 16 * WB // EB, 16 * (k // EB)))
                    dve.tensor_scalar(goal_u[:, k % EB:k % EB + 1], goal[:, :], FAR, None, ALU.add
                                      ).then_inc(goal_ready, 1)
                    dve.wait_ge(gexp_ready, n + 1)
                    after(r, per, dve.tensor_scalar(gsig[:, :], gexp[:, :], 1.0, None, ALU.add))
                    after(r, per, dve.reciprocal(gact[:, :], gsig[:, :]))
                    after(r, per, dve.tensor_tensor(gsig[:, :], s_ps[0:F, k % 2, 512:512 + SLOTS], gact[:, :], ALU.mult))
                    used(dve, dn_ready, n - 1)
                    for e in range(2):
                        cols = slice(e * CAP, (e + 1) * CAP)
                        ins = dve.tensor_tensor(hid_t[:, k % 2, e, cols],
                                                s_ps[0:F, k % 2, 512 + SLOTS + e * CAP:512 + SLOTS + (e + 1) * CAP],
                                                gsig[:, cols], ALU.mult)
                    ins.then_inc(hid_t_ready, 1)
                assert links[0] - start == EXPERT_LINKS * WB, (links[0] - start) / WB
                links[0] = start

            dve.wait_ge(dve_own, B * LINKS)

            def after(r, per, ins):
                links[0] += 1
                ins.then_inc(dve_own2, 1)
                dve.wait_ge(dve_own2, at(r, per, links[0]))

            expert_round(0)
            with dve.Fori(1, PAIRS // WB) as r:
                expert_round(r)

            def add_up(r, k):
                t = at(r, 2, k)
                dve.wait_ge(yk_loaded[k], at(r, 16, 16))
                add(r, dve.tensor_tensor(yk[:, k, 0:3, :], yk[:, k, 0:3, :], yk[:, k, 3:6, :], ALU.add))
                dve.wait_ge(zf_loaded[k], at(r, 16, 16))
                dve.tensor_tensor(ysum[:, k, :], yk[:, k, 0, :], zf[:, k, :], ALU.add)
                add(r, dve.tensor_tensor(yk[:, k, 1, :], yk[:, k, 1, :], yk[:, k, 2, :], ALU.add))
                add(r, dve.tensor_tensor(ysum[:, k, :], ysum[:, k, :], yk[:, k, 1, :], ALU.add))
                add(r, dve.bn_stats(fstats[:, :], ysum[:, k, :]))
                hold(6)
                add(r, dve.bn_aggr(fmv[:, k, :], fstats[:, :]))
                dve.tensor_scalar(fve[:, k, :], fmv[:, k, 1:2], EPS, None, ALU.add).then_inc(fvar_ready, 1)

            def scale(r, k):
                t = at(r, 2, k)
                dve.wait_ge(frs_ready, t + 1)
                used(dve, out_stored[k], at(r, 16, 0))
                dve.tensor_scalar(fout[:, k, :], ysum[:, k, :], fmv[:, k, 0:1], frs[:, k, 0:1], ALU.subtract, ALU.mult
                                  ).then_inc(fout_ready, 1)

            FL = 10
            fl = [0]

            def add(r, ins):
                fl[0] += 1
                ins.then_inc(fin_own, 1)
                dve.wait_ge(fin_own, at(r, FL, fl[0]))

            def final_round(r):
                fl[0] = 0
                add_up(r, 0)
                add_up(r, 1)
                scale(r, 0)
                scale(r, 1)
                assert fl[0] == FL, fl

            final_round(0)
            with dve.Fori(1, B * NT // 2) as r:
                final_round(r)


_INS = ["L0_attn_x", "L0_attn_w_aq", "L0_attn_w_ak", "L0_attn_w_av", "L0_attn_w_ao", "L0_ffn_gate_w", "L0_ffn_bias",
        "L0_ffn_w_gate", "L0_ffn_w_up", "L0_ffn_w_down", "L0_ffn_ws_gate", "L0_ffn_ws_up", "L0_ffn_ws_down"]


def rope_tables():
    half = D // 2
    freqs = np.power(10000.0, -np.arange(half) / half).astype(np.float32)
    angles = (np.arange(T, dtype=np.float32)[:, None] * freqs[None, :]).astype(np.float64)
    scale = float(D) ** -0.25
    return (np.cos(angles) * scale).astype(np.float32), (np.sin(angles) * scale).astype(np.float32)


def kernel(**inputs):
    import concourse.bacc as _bacc
    from concourse import mybir as _mybir
    from concourse.bass_utils import run_bass_kernel_spmd as _run

    nc = _bacc.Bacc("TRN2", target_bir_lowering=False, num_devices=1)
    arrays, args = {}, []
    cos, sin = rope_tables()
    for name, a in [(n, np.ascontiguousarray(inputs[n])) for n in _INS] + [("rope_cos", cos), ("rope_sin", sin)]:
        arrays[f"in_{name}_dram"] = a
        args.append(nc.dram_tensor(f"in_{name}_dram", a.shape, _mybir.dt.from_np(a.dtype), kind="ExternalInput").ap())
    args.append(nc.dram_tensor("out_0_dram", (B, T, M), F32, kind="ExternalOutput").ap())
    build(nc, *args)
    r = _run(nc, [arrays], core_ids=[0])
    return r.results[0]["out_0_dram"]
```

```python
from contextlib import ExitStack

import numpy as np

import concourse.bass as bass
from concourse import mybir

ALU = mybir.AluOpType
ACT = mybir.ActivationFunctionType
AX_X = mybir.AxisListType.X
F32 = mybir.dt.float32
F32R = mybir.dt.float32r
BF16 = mybir.dt.bfloat16
U32 = mybir.dt.uint32

P = 128
B, T, M = 2, 1024, 256
G, H, D = 4, 4, 128
NT = T // P
TILES = B * NT
MC = M // P
HD = H * D
NEG = -1e30
EPS = 1e-5
E, K, F = 64, 6, 96
EG, KG = 8, 4
SCALE = 2.5
CAP = 2 * (256 * K // E)
PAIRS = E // 2
WB = 8
ROUNDS = PAIRS // WB
EB = 4
FB = 4
SLOTS = 2 * CAP
TOKENS = B * T
W_AT, S_AT, T_AT, ROW = M, M + K, M + 2 * K, M + 16
FAR = 1.0e5

UNITS = TILES * G
HEADS = UNITS * H
PTB = 3
LAG = 2
SUM_LINKS = 4
EXPERT_LINKS = 6
RING = 3
XB = 3
BLOCKS = ["K", "V", 0, 1, 2, 3]


def blocks(u):
    return u // G % NT + 1


def schedule():
    seq, waiting = [], []

    def product():
        u, j = waiting.pop(0)
        if j == 0:
            seq.append(("linv", u))
        seq.append(("pv", u, j))
        if j == blocks(u) - 1:
            seq.append(("omul", u))

    def lagging(n):
        u, h = divmod(n, H)
        for j in range(-(-h * blocks(u) // H), -(-(h + 1) * blocks(u) // H)):
            seq.append(("ptrans", u, j))
            waiting.append((u, j))
            if len(waiting) > LAG:
                product()
            yield j

    def drain(below):
        while waiting and waiting[0][0] < below:
            product()

    def misc(i, g, h):
        out = {(0, 0): [("qkt", i, 1)], (0, 1): [("proj", i, 2)], (1, 0): [("qkt", i, 2)],
               (1, 1): [("proj", i, 3)], (2, 0): [("qkt", i, 3)]}.get((g, h), [])[:]
        p, n = i - 1, i + 1
        if n < TILES:
            out += {(1, 3): [("xt", n)], (2, 1): [("proj", n, "K")]}.get((g, h), [])
            if n % NT:
                out += {(2, 3): [("qkt", n, "K"), ("proj", n, 0)], (3, 1): [("qkt", n, 0), ("proj", n, 1)],
                        (3, 2): [("proj", n, "V")]}.get((g, h), [])
        if p >= 0:
            out += {(1, 2): [("outproj", p)], (1, 3): [("norm", p)], (2, 0): [("x1t", p)], (2, 1): [("rtr", p)],
                    (2, 2): [("pick", p, 0)], (2, 3): [("ht", p), ("pick", p, 1)], (3, 0): [("sd", p), ("pick", p, 2)],
                    (3, 1): [("pick", p, 3)], (3, 2): [("pick", p, 4)], (3, 3): [("pick", p, 5)]}.get((g, h), [])
        if p >= 1:
            out += {(0, 0): [("pick", p - 1, 6)], (0, 1): [("pick", p - 1, 7)], (0, 2): [("count", p - 1)],
                    (0, 3): [("place", p - 1)]}.get((g, h), [])
        return out

    late = H + 1
    for n in range(HEADS):
        u, h = divmod(n, H)
        i, g = divmod(u, G)
        if n % (NT * G * H) == 0:
            if i == 0:
                seq += [("xt", 0), ("proj", 0, "K")]
            seq += [("qkt", i, "K"), ("proj", i, 0)]
            if i:
                for m in range(n - late, n):
                    for _ in lagging(m):
                        pass
                drain(u)
            seq += [("qkt", i, 0), ("proj", i, 1), ("proj", i, "V")]
        seq.append(("score", u, h))
        before = n - late
        first = True
        if before >= 0 and before // (NT * G * H) == n // (NT * G * H):
            for _ in lagging(before):
                if first:
                    seq.append(("exp", u, h))
                first = False
        if first:
            seq.append(("exp", u, h))
        if (g, h) == (1, 2):
            drain(i * G)
        seq += misc(i, g, h)
    for m in range(HEADS - late, HEADS):
        for _ in lagging(m):
            pass
    drain(UNITS)
    p = TILES - 1
    seq += [("pick", p - 1, 6), ("pick", p - 1, 7), ("count", p - 1), ("place", p - 1)]
    seq += [(s, p) for s in ("outproj", "norm", "x1t", "rtr")] + [("pick", p, 0), ("ht", p), ("pick", p, 1), ("sd", p)]
    seq += [("pick", p, n) for n in range(2, 8)] + [("count", p), ("place", p)]
    return seq


RINGED = ("xt", "proj", "qkt", "ptrans", "linv", "outproj", "x1t", "rtr", "ht", "count", "sd")


def ring_places(seq):
    places, n = {}, 0
    for s in seq:
        if s[0] in RINGED:
            places[s] = (n % RING, n // RING)
            n += 1
    return places, [len(range(r, n, RING)) for r in range(RING)]


SEQ = schedule()
PLACE, TURNS = ring_places(SEQ)
PT_AT = {s[1:]: n for n, s in enumerate(s for s in SEQ if s[0] == "ptrans")}
PT_ALL = len(PT_AT)
PROJ_AT = {s[1:]: n for n, s in enumerate(s for s in SEQ if s[0] == "proj")}
ROPE_AT = {k: n for n, k in enumerate(k for k in PROJ_AT if k[1] != "V")}
QKT_AT = {s[1:]: n for n, s in enumerate(s for s in SEQ if s[0] == "qkt")}
assert [s[1:] for s in SEQ if s[0] == "qkt"] == list(ROPE_AT)


def build(nc, x, w_aq, w_ak, w_av, w_ao, gate_w, bias, w_gate, w_up, w_down, ws_gate, ws_up, ws_down,
          rope_cos, rope_sin, out):
    slot_rows = nc.dram_tensor("slot_rows", (E * CAP, ROW), F32, kind="Internal").ap()
    expert_rows = nc.dram_tensor("expert_rows", (TOKENS * K, M), F32, kind="Internal").ap()
    z_rows = nc.dram_tensor("z_rows", (TOKENS, M), F32, kind="Internal").ap()
    xf = x.rearrange("b t m -> (b t) m")
    of = out.rearrange("b t m -> (b t) m")

    with ExitStack() as ctx:
        def sb(name, shape, dt, where=ctx):
            return where.enter_context(nc.sbuf_tensor(name, shape, dt))

        def sem(name):
            return ctx.enter_context(nc.semaphore(name))

        ident = sb("ident", [P, P], F32)
        ident_bf = sb("ident_bf", [P, P], BF16)
        causal_bf = sb("causal_bf", [P, P], BF16)
        before_bf = sb("before_bf", [P, P], BF16)
        ones_bf = sb("ones_bf", [P, P], BF16)
        minus_half = sb("minus_half", [P, 1], F32)
        iota_e = sb("iota_e", [P, E], F32)
        choice_far = sb("choice_far", [P, K], F32)
        pool_cell = sb("pool_cell", [P, 1], F32)
        dve_cell = sb("dve_cell", [P, 1], F32)
        held = sb("held", [1, 8], F32)
        bias_sb = sb("bias_sb", [P, E], F32)
        blank = sb("blank", [P, ROW], F32)
        token = sb("token", [P, 1], F32)
        taken = sb("taken", [P, E], BF16)
        wr_hi = sb("wr_hi", [P, MC, 256], F32R)
        wr_lo = sb("wr_lo", [P, MC, 256], F32R)
        wsd_hi = sb("wsd_hi", [F, M], F32R)
        wsd_lo = sb("wsd_lo", [F, M], F32R)

        att = ExitStack()
        w_hi = sb("w_hi", [P, 6, H, MC, D], F32R, att)
        w_lo = sb("w_lo", [P, 6, H, MC, D], F32R, att)
        wo = sb("wo", [P, G * H, M], F32, att)
        kt_hi = sb("kt_hi", [P, G, T], F32R, att)
        kt_lo = sb("kt_lo", [P, G, T], F32R, att)
        v_sb = sb("v_sb", [P, NT, G * D], F32, att)
        probs = sb("probs", [P, 2, H, T], F32, att)
        pt = sb("pt", [P, PTB, HD], F32, att)
        qt_hi = sb("qt_hi", [P, 2, HD], F32R, att)
        qt_lo = sb("qt_lo", [P, 2, HD], F32R, att)
        cos_sb = sb("cos_sb", [P, NT, D // 2], F32, att)
        sin_sb = sb("sin_sb", [P, NT, D // 2], F32, att)
        x_sb = sb("x_sb", [P, XB, M], F32, att)
        xt_hi = sb("xt_hi", [P, MC, P], F32R, att)
        xt_lo = sb("xt_lo", [P, MC, P], F32R, att)
        q_cos = sb("q_cos", [P, H, 2, D // 2], F32, att)
        q_sin = sb("q_sin", [P, H, 2, D // 2], F32, att)
        q_rot = sb("q_rot", [P, H, 2, D // 2], F32, att)
        neg_max = sb("neg_max", [P, 8], F32, att)
        row_sum = sb("row_sum", [P, 2, H], F32, att)
        inv_sum = sb("inv_sum", [P, 2, H], F32, att)
        inv_row = sb("inv_row", [P, HD], F32, att)
        ot = sb("ot", [P, G, HD], F32, att)
        row = sb("row", [P, 2, ROW], F32, att)
        y_sb = sb("y_sb", [P, M], F32, att)
        stats = sb("stats", [P, 6], F32, att)
        mean_var = sb("mean_var", [P, 2], F32, att)
        var_eps = sb("var_eps", [P, 1], F32, att)
        rstd = sb("rstd", [P, 1], F32, att)
        x1t_hi = sb("x1t_hi", [P, MC, P], F32R, att)
        x1t_lo = sb("x1t_lo", [P, MC, P], F32R, att)
        sig = sb("sig", [P, E + F], F32, att)
        hid = sb("hid", [P, F], F32, att)
        ht_hi = sb("ht_hi", [F, P], F32R, att)
        ht_lo = sb("ht_lo", [F, P], F32R, att)
        z_sb = sb("z_sb", [P, M], F32, att)
        biased = sb("biased", [P, E], F32, att)
        top2 = sb("top2", [P, EG, 8], F32, att)
        group = sb("group", [P, EG], F32, att)
        group_top = sb("group_top", [P, 8], F32, att)
        group_at = sb("group_at", [P, 8], U32, att)
        group_atf = sb("group_atf", [P, 8], F32, att)
        kept4 = sb("kept4", [P, EG, KG], F32, att)
        kept = sb("kept", [P, EG], F32, att)
        barred = sb("barred", [P, EG], F32, att)
        open_ = sb("open_", [P, E], F32, att)
        top8 = sb("top8", [P, 8], F32, att)
        top_at = sb("top_at", [P, 8], U32, att)
        top_atf = sb("top_atf", [P, 8], F32, att)
        onehot = sb("onehot", [P, K, E], F32, att)
        onehot_s = sb("onehot_s", [P, K, E], F32, att)
        chose = sb("chose", [P, E], BF16, att)
        top_s = sb("top_s", [P, K], F32, att)
        top_sum = sb("top_sum", [P, 1], F32, att)
        top_inv = sb("top_inv", [P, 1], F32, att)
        pos6 = sb("pos6", [P, K], F32, att)
        over = sb("over", [P, K], F32, att)
        slot_u = sb("slot_u", [P, 2, K], U32, att)
        att.close()

        exp = ExitStack()
        wgu = sb("wgu", [P, WB, 2, 2, MC, F], F32, exp)
        wdn = sb("wdn", [F, WB, 2, M], F32, exp)
        srow = sb("srow", [SLOTS, WB, ROW], F32, exp)
        sxt = sb("sxt", [P, 2, MC, SLOTS], F32, exp)
        gexp = sb("gexp", [F, SLOTS], F32, exp)
        gsig = sb("gsig", [F, SLOTS], F32, exp)
        gact = sb("gact", [F, SLOTS], F32, exp)
        hid_t = sb("hid_t", [F, 2, 2, SLOTS], F32, exp)
        slot_now = sb("slot_now", [SLOTS, 1], F32, exp)
        mine = sb("mine", [SLOTS, K], F32, exp)
        mine_k = sb("mine_k", [SLOTS, K], F32, exp)
        slot_w = sb("slot_w", [SLOTS, WB], F32, exp)
        which = sb("which", [SLOTS, 1], F32, exp)
        goal = sb("goal", [SLOTS, 1], F32, exp)
        goal_u = sb("goal_u", [SLOTS, EB], U32, exp)
        nmr = sb("nmr", [P, FB, 1], F32, exp)
        erow = sb("erow", [SLOTS, EB, M], F32, exp)
        yk = sb("yk", [P, FB, K, M], F32, exp)
        zf = sb("zf", [P, FB, M], F32, exp)
        ysum = sb("ysum", [P, FB, M], F32, exp)
        fstats = sb("fstats", [P, 6], F32, exp)
        fmv = sb("fmv", [P, FB, 2], F32, exp)
        fve = sb("fve", [P, FB, 1], F32, exp)
        frs = sb("frs", [P, FB, 1], F32, exp)
        fout = sb("fout", [P, FB, M], F32, exp)
        exp.close()

        s_ps = ctx.enter_context(nc.psum_tensor("s_ps", [P, 2, T], F32))
        o_ps = ctx.enter_context(nc.psum_tensor("o_ps", [P, 512], F32))
        ring = ctx.enter_context(nc.psum_tensor("ring", [P, RING, 512], F32))

        const_ready = sem("const_ready")
        pool_own = sem("pool_own")
        w_loaded = [sem(f"w_loaded{n}") for n in range(6)]
        wo_loaded = sem("wo_loaded")
        wr_loaded = sem("wr_loaded")
        wsd_loaded = sem("wsd_loaded")
        table_loaded = sem("table_loaded")
        bias_loaded = sem("bias_loaded")
        whi_ready = sem("whi_ready")
        wlo_ready = sem("wlo_ready")
        wlo_pool_ready = sem("wlo_pool_ready")
        wmisc_hi_ready = sem("wmisc_hi_ready")
        wmisc_lo_ready = sem("wmisc_lo_ready")
        picked = sem("picked")
        slot_now_ready = sem("slot_now_ready")
        dve_own2 = sem("dve_own2")
        blank_stored = sem("blank_stored")
        experts_blank = sem("experts_blank")
        attention_left = sem("attention_left")
        x_loaded = [sem(f"x_loaded{n}") for n in range(XB)]
        ring_read = [sem(f"ring_read{r}") for r in range(RING)]
        xt_ready = sem("xt_ready")
        xt_hi_ready = sem("xt_hi_ready")
        proj_ready = sem("proj_ready")
        rot_ready = sem("rot_ready")
        qkt_ready = sem("qkt_ready")
        qk_hi_ready = sem("qk_hi_ready")
        scores_ready = sem("scores_ready")
        max_ready = sem("max_ready")
        probs_ready = sem("probs_ready")
        ptrans_ready = sem("ptrans_ready")
        pv_done = sem("pv_done")
        inv_ready = sem("inv_ready")
        linv_ready = sem("linv_ready")
        o_ready = sem("o_ready")
        attn_ready = sem("attn_ready")
        var_ready = sem("var_ready")
        rstd_ready = sem("rstd_ready")
        x1_ready = sem("x1_ready")
        x1t_ready = sem("x1t_ready")
        x1t_hi_ready = sem("x1t_hi_ready")
        rtr_ready = sem("rtr_ready")
        exp_ready = sem("exp_ready")
        ht_ready = sem("ht_ready")
        ht_hi_ready = sem("ht_hi_ready")
        sd_ready = sem("sd_ready")
        z_stored = sem("z_stored")
        chose_ready = sem("chose_ready")
        count_ready = sem("count_ready")
        placed = sem("placed")
        scattered = [sem(f"scattered{n}") for n in range(2)]
        stood = sem("stood")
        dve_own = sem("dve_own")

        experts_loaded = [sem(f"experts_loaded{n}") for n in range(WB)]
        srow_loaded = [sem(f"srow_loaded{n}") for n in range(WB)]
        st_ready = sem("st_ready")
        sxt_ready = sem("sxt_ready")
        gu_ready = sem("gu_ready")
        gexp_ready = sem("gexp_ready")
        hid_t_ready = sem("hid_t_ready")
        dn_ready = sem("dn_ready")
        goal_ready = sem("goal_ready")
        erow_ready = sem("erow_ready")
        erow_sent = [sem(f"erow_sent{n}") for n in range(EB)]
        yk_loaded = [sem(f"yk_loaded{n}") for n in range(FB)]
        zf_loaded = [sem(f"zf_loaded{n}") for n in range(FB)]
        fvar_ready = sem("fvar_ready")
        frs_ready = sem("frs_ready")
        nmr_ready = sem("nmr_ready")
        half_ready = sem("half_ready")
        fout_ready = sem("fout_ready")
        fin_own = sem("fin_own")
        out_stored = [sem(f"out_stored{n}") for n in range(FB)]

        block = ctx.enter_context(nc.Block())

        def score_cols(n):
            few = blocks(n // H) <= 4
            start = 512 * (n // 2 % 2) if few else 0
            return slice(start, start + blocks(n // H) * P)

        def scores_used(n):
            few = blocks(n // H) <= 4 and (n < 2 or blocks((n - 2) // H) <= 4)
            return n - 3 if few else n - 1

        def at(b, per, n):
            return b * per + n

        w_raw = probs[:, :, :, :].rearrange("p s h t -> p (s h t)")[:, 0:6 * H * MC * D].rearrange(
            "p (n x) -> p n x", n=6)
        w_hi_f = w_hi[:, :, :, :, :].rearrange("p n h c d -> p n (h c d)")
        w_lo_f = w_lo[:, :, :, :, :].rearrange("p n h c d -> p n (h c d)")
        raw_r = v_sb[:, 0, :].rearrange("p (c n) -> p c n", c=MC)
        raw_d = v_sb[0:F, 1, 0:M]

        PASSES = ((0, 0), (0, 1), (1, 0))

        def read(eng, step):
            r, turn = PLACE[step]
            eng.wait_ge(ring_read[r], turn + 1)

        def reader(ins, step):
            ins.then_inc(ring_read[PLACE[step][0]], 1)

        def bank(step):
            return ring[:, PLACE[step][0], :]

        def used(eng, semaphore, n):
            if not (isinstance(n, int) and n <= 0):
                eng.wait_ge(semaphore, n)

        @block.sync
        def _(sp):
            def load_x(i):
                sp.dma_start(x_sb[:, i % XB, :], xf[i * P:(i + 1) * P, :]).then_inc(x_loaded[i % XB], 16)

            load_x(0)
            for n, name in enumerate(BLOCKS):
                src = {"K": w_ak, "V": w_av}.get(name)
                src = w_aq[name] if src is None else src
                sp.dma_start(w_raw[:, n, :].rearrange("p (h y) -> p h y", h=H),
                             src.rearrange("h (p c) d -> p h (c d)", c=MC)).then_inc(w_loaded[n], 16)
                if n == 0:
                    sp.dma_start(cos_sb[:, :, :], rope_cos.rearrange("(n p) d -> p n d", p=P)).then_inc(table_loaded, 16)
                    sp.dma_start(sin_sb[:, :, :], rope_sin.rearrange("(n p) d -> p n d", p=P)).then_inc(table_loaded, 16)
            sp.dma_start(raw_r[:, :, 0:E], gate_w.rearrange("(p c) e -> p c e", c=MC)).then_inc(wr_loaded, 16)
            sp.dma_start(raw_r[:, :, E:E + F], ws_gate.rearrange("(p c) e -> p c e", c=MC)).then_inc(wr_loaded, 16)
            sp.dma_start(raw_r[:, :, E + F:], ws_up.rearrange("(p c) e -> p c e", c=MC)).then_inc(wr_loaded, 16)
            sp.dma_start(raw_d, ws_down).then_inc(wsd_loaded, 16)
            load_x(1)
            sp.dma_start(wo[:, :, :], w_ao.rearrange("g h d m -> d (g h) m")).then_inc(wo_loaded, 16)
            sp.dma_start(bias_sb[:, :], bias.rearrange("(a e) -> a e", a=1).to_broadcast([P, E])).then_inc(bias_loaded, 16)
            sp.wait_ge(const_ready, 1)
            sp.dma_start(slot_rows.rearrange("(p n) r -> p n r", p=P),
                         blank[:, :].rearrange("p (a r) -> p a r", a=1).to_broadcast([P, E * CAP // P, ROW])
                         ).then_inc(blank_stored, 16)

            def blank_experts(i):
                sp.dma_start(expert_rows[i * P * K:(i + 1) * P * K, :].rearrange("(p n) m -> p n m", p=P),
                             blank[:, 0:M].rearrange("p (a r) -> p a r", a=1).to_broadcast([P, K, M])
                             ).then_inc(experts_blank, 16)

            for s in SEQ:
                if s[0] == "xt" and 1 <= s[1] < TILES - 1:
                    i = s[1] + 1
                    if i >= XB:
                        sp.wait_ge(var_ready, i - XB + 1)
                    load_x(i)
                if s[0] == "proj" and s[2] == 3:
                    sp.wait_ge(proj_ready, PROJ_AT[s[1:]] + 1)
                    blank_experts(s[1])
                if s[0] == "sd":
                    i = s[1]
                    read(sp, s)
                    sp.dma_start(z_rows[i * P:(i + 1) * P, :], z_sb[:, :]).then_inc(z_stored, 16)
            sp.wait_ge(z_stored, 16 * TILES)

            sp.wait_ge(proj_ready, len(PROJ_AT))

            def load_pair(n, k):
                for a, w in enumerate((w_gate, w_up)):
                    for e in range(2):
                        sp.dma_start(wgu[:, k, e, a, :, :],
                                     w[bass.ds(2 * n + e, 1), :, :].rearrange("a (p c) f -> p (a c) f", c=MC)
                                     ).then_inc(experts_loaded[k], 16)
                sp.dma_start(wdn[:, k, :, :], w_down[bass.ds(2 * n, 2), :, :].rearrange("e f m -> f e m")
                             ).then_inc(experts_loaded[k], 16)

            def load_slots(n, k):
                sp.dma_start(srow[:, k, :], slot_rows[bass.ds(n * SLOTS, SLOTS), :]).then_inc(srow_loaded[k], 16)

            for k in range(WB):
                load_pair(k, k)
            sp.wait_ge(attention_left, 1)
            for n in range(2):
                sp.wait_ge(scattered[n], 8 * K * TILES)
            for k in range(WB):
                load_slots(k, k)
            with sp.Fori(1, PAIRS // WB) as r:
                for k in range(WB):
                    sp.wait_ge(dn_ready, at(r, WB, k + 1 - WB))
                    load_slots(r * WB + k, k)
                    load_pair(r * WB + k, k)
            for n in range(EB):
                sp.wait_ge(erow_sent[n], 16 * (PAIRS // EB))

            def sums(t, k):
                used(sp, fvar_ready, t - FB + 1)
                sp.dma_start(yk[:, k, :, :], expert_rows[bass.ds(t * P * K, P * K), :].rearrange(
                    "(p k) m -> p k m", k=K)).then_inc(yk_loaded[k], 16)
                sp.dma_start(zf[:, k, :], z_rows[bass.ds(t * P, P), :]).then_inc(zf_loaded[k], 16)

            def store(t, k):
                sp.wait_ge(fout_ready, t + 1)
                sp.dma_start(of[bass.ds(t * P, P), :], fout[:, k, :]).then_inc(out_stored[k], 16)

            for k in range(FB):
                sums(k, k)
            with sp.Fori(1, TILES // FB) as r:
                for k in range(FB):
                    sums(r * FB + k, k)
                    store(r * FB + k - FB, k)
            for k in range(FB):
                store(TILES - FB + k, k)
            for k in range(FB):
                sp.wait_ge(out_stored[k], 16 * (TILES // FB))

        @block.gpsimd
        def _(pool):
            own = [0]

            def link(ins):
                own[0] += 1
                ins.then_inc(pool_own, 1)
                pool.wait_ge(pool_own, own[0])

            link(pool.memset(blank[:, :], 0.0))
            pool.memset(blank[:, S_AT:S_AT + K], -1.0).then_inc(const_ready, 1)
            link(pool.memset(ident[:, :], 0.0))
            link(pool.affine_select(out=ident[:, :], in_=ident[:, :], compare_op=ALU.not_equal, fill=1.0, base=0,
                                    pattern=[[-1, P]], channel_multiplier=1))
            link(pool.tensor_copy(ident_bf[:, :], ident[:, :]))
            link(pool.memset(causal_bf[:, :], 0.0))
            link(pool.affine_select(out=causal_bf[:, :], in_=causal_bf[:, :], compare_op=ALU.is_ge, fill=NEG, base=0,
                                    pattern=[[-1, P]], channel_multiplier=1))
            link(pool.memset(before_bf[:, :], 0.0))
            link(pool.affine_select(out=before_bf[:, :], in_=before_bf[:, :], compare_op=ALU.is_ge, fill=1.0, base=0,
                                    pattern=[[-1, P]], channel_multiplier=1))
            link(pool.memset(ones_bf[:, :], 1.0))
            link(pool.memset(minus_half[:, :], -0.5))
            link(pool.memset(taken[:, :], 0.0))
            link(pool.memset(row[:, :, :], 0.0))
            link(pool.iota(iota_e[:, :], pattern=[[1, E]], base=0, channel_multiplier=0,
                           allow_small_or_imprecise_dtypes=True))
            link(pool.iota(choice_far[:, :], pattern=[[1, K]], base=-int(FAR), channel_multiplier=0,
                           allow_small_or_imprecise_dtypes=True))
            pool.iota(token[:, :], pattern=[[0, 1]], base=-P, channel_multiplier=1,
                      allow_small_or_imprecise_dtypes=True).then_inc(const_ready, 1)
            for n in (4, 5):
                pool.wait_ge(whi_ready, n + 1)
                pool.tensor_tensor(w_lo_f[:, n, :], w_raw[:, n, :], w_hi_f[:, n, :].bitcast(F32), ALU.subtract
                                   ).then_inc(wlo_pool_ready, 1)

            def stand(n):
                used(pool, stood, n)
                pool.tensor_tensor(pool_cell[:, 0:1], minus_half[:, :], minus_half[:, :], ALU.mult).then_inc(stood, 1)

            for s in SEQ:
                if s[0] == "proj" and s[2] != "V":
                    n = ROPE_AT[s[1:]]
                    read(pool, s)
                    if n >= 1:
                        pool.wait_ge(qkt_ready, n)
                    pool.tensor_tensor(q_rot[:, :, 0, :], q_cos[:, :, 0, :], q_sin[:, :, 1, :], ALU.subtract)
                    pool.tensor_tensor(q_rot[:, :, 1, :], q_cos[:, :, 1, :], q_sin[:, :, 0, :], ALU.add
                                       ).then_inc(rot_ready, 1)
                if s[0] == "outproj":
                    pool.wait_ge(var_ready, s[1] + 1)
                    pool.tensor_tensor(rstd[:, :], var_eps[:, :], minus_half[:, :], ALU.pow).then_inc(rstd_ready, 1)
                if s[0] == "place":
                    i = s[1]
                    if i == 0:
                        pool.wait_ge(blank_stored, 16)
                    pool.wait_ge(placed, i + 1)
                    for k in range(K):
                        pool.indirect_dma_start(
                            slot_rows[:, :], bass.IndirectOffsetOnAxis(ap=slot_u[:, i % 2, k:k + 1], axis=0),
                            row[:, i % 2, :], None, bounds_check=E * CAP - 1, oob_is_err=False
                        ).then_inc(scattered[i % 2], 16)

            def send(n, k):
                pool.wait_ge(goal_ready, n + 1)
                pool.wait_ge(erow_ready, n + 1)
                stand(n)
                pool.indirect_dma_start(
                    expert_rows[:, :], bass.IndirectOffsetOnAxis(ap=goal_u[:, k % EB:k % EB + 1], axis=0),
                    erow[:, k % EB, :], None, bounds_check=TOKENS * K - 1, oob_is_err=False
                ).then_inc(erow_sent[k % EB], 16)

            pool.wait_ge(attention_left, 1)
            pool.wait_ge(experts_blank, 16 * TILES)
            pool.iota(slot_now[:, :], pattern=[[0, 1]], base=-SLOTS, channel_multiplier=1,
                      allow_small_or_imprecise_dtypes=True).then_inc(slot_now_ready, 1)
            pool.memset(hid_t[:, :, :, :], 0.0).then_inc(slot_now_ready, 1)
            with pool.Fori(0, PAIRS // WB) as r:
                for k in range(WB):
                    send(r * WB + k, k)

            def half(r, k):
                pool.wait_ge(yk_loaded[k], at(r, 16, 16))
                pool.tensor_tensor(yk[:, k, 0:3, :], yk[:, k, 0:3, :], yk[:, k, 3:6, :], ALU.add).then_inc(half_ready, 1)

            def deviation(r, k):
                pool.wait_ge(fvar_ready, at(r, FB, k + 1))
                pool.tensor_tensor(frs[:, k, :], fve[:, k, :], minus_half[:, :], ALU.pow).then_inc(frs_ready, 1)

            with pool.Fori(0, TILES // FB) as r:
                for k in range(FB):
                    half(r, k)
                    if k:
                        deviation(r, k - 1)
                deviation(r, FB - 1)

        @block.scalar
        def _(act):
            def split(hi, raw):
                return act.activation(hi, raw, ACT.Copy)

            for n in range(6):
                act.wait_ge(w_loaded[n], 16)
                split(w_hi_f[:, n, :], w_raw[:, n, :]).then_inc(whi_ready, 1)
            act.wait_ge(wr_loaded, 48)
            split(wr_hi[:, :, :], raw_r).then_inc(wmisc_hi_ready, 1)
            act.wait_ge(wsd_loaded, 16)
            split(wsd_hi[:, :], raw_d).then_inc(wmisc_hi_ready, 1)
            act.wait_ge(wmisc_lo_ready, 2)

            for s in SEQ:
                kind = s[0]
                if kind == "xt":
                    act.wait_ge(xt_ready, s[1] + 1)
                    if s[1] >= 1:
                        act.wait_ge(proj_ready, 6 * s[1])
                    split(xt_hi[:, :, :], bank(s)[:, 0:MC * P].rearrange("p (c t) -> p c t", c=MC)
                          ).then_inc(xt_hi_ready, 1)
                if kind == "proj" and s[2] == "V":
                    act.wait_ge(proj_ready, PROJ_AT[s[1:]] + 1)
                    if s[1] == NT:
                        act.wait_ge(pv_done, PT_ALL // B)
                    reader(act.activation(v_sb[:, s[1] % NT, :], bank(s), ACT.Copy), s)
                if kind == "qkt":
                    i, name = s[1:]
                    act.wait_ge(qkt_ready, QKT_AT[s[1:]] + 1)
                    if name == "K":
                        if i == NT:
                            act.wait_ge(scores_ready, HEADS // B)
                        c = i % NT * P
                        dst, src = kt_hi[:, :, c:c + P], bank(s).rearrange("p (g t) -> p g t", g=G)
                    else:
                        u = i * G + name
                        dst, src = qt_hi[:, u % 2, :], bank(s)
                        if u >= 2:
                            act.wait_ge(scores_ready, H * (u - 1))
                    split(dst, src).then_inc(qk_hi_ready, 1)
                if kind == "exp":
                    u, h = s[1:]
                    n = u * H + h
                    act.wait_ge(max_ready, n + 1)
                    if u < 2:
                        act.wait_ge(wlo_ready, 4)
                        act.wait_ge(wlo_pool_ready, 2)
                    else:
                        act.wait_ge(ptrans_ready, PT_AT[(u - 2, blocks(u - 2) - 1)] + 1)
                        act.wait_ge(inv_ready, u - 1)
                    act.activation(probs[:, u % 2, h, 0:blocks(u) * P], s_ps[:, n % 2, score_cols(n)], ACT.Exp,
                                   bias=neg_max[:, n % 8:n % 8 + 1],
                                   accum_out=row_sum[:, u % 2, h:h + 1]).then_inc(probs_ready, 1)
                if kind == "ptrans":
                    n = PT_AT[s[1:]]
                    act.wait_ge(ptrans_ready, n + 1)
                    if n >= PTB:
                        act.wait_ge(pv_done, n - PTB + 1)
                    reader(act.activation(pt[:, n % PTB, :], bank(s), ACT.Copy), s)
                if kind == "linv":
                    u = s[1]
                    act.wait_ge(linv_ready, u + 1)
                    if u >= 1:
                        act.wait_ge(o_ready, u)
                    reader(act.activation(inv_row[:, :], bank(s), ACT.Copy), s)
                if kind == "x1t":
                    act.wait_ge(x1t_ready, s[1] + 1)
                    if s[1] >= 1:
                        act.wait_ge(rtr_ready, s[1])
                    split(x1t_hi[:, :, :], bank(s)[:, 0:MC * P].rearrange("p (c t) -> p c t", c=MC)
                          ).then_inc(x1t_hi_ready, 1)
                if kind == "rtr":
                    act.wait_ge(rtr_ready, s[1] + 1)
                    if s[1] >= 1:
                        act.wait_ge(picked, s[1])
                    act.activation(sig[:, :], bank(s)[:, 0:E + F], ACT.Exp, scale=-1.0).then_inc(exp_ready, 1)
                if kind == "ht":
                    act.wait_ge(ht_ready, s[1] + 1)
                    if s[1] >= 1:
                        act.wait_ge(sd_ready, s[1])
                    split(ht_hi[:, :], bank(s)[0:F, 0:P]).then_inc(ht_hi_ready, 1)

            act.wait_ge(attention_left, 1)

            def slots_in(n, k):
                act.wait_ge(st_ready, n + 1)
                used(act, gu_ready, n - 1)
                act.activation(sxt[:, k % 2, :, :], s_ps[:, k % 2, 0:MC * SLOTS].rearrange("p (c s) -> p c s", c=MC),
                               ACT.Copy).then_inc(sxt_ready, 1)

            def gate_exp(n, k):
                act.wait_ge(gu_ready, n + 1)
                used(act, hid_t_ready, n)
                act.activation(gexp[:, :], s_ps[0:F, k % 2, 512:512 + SLOTS], ACT.Exp, scale=-1.0
                               ).then_inc(gexp_ready, 1)

            def rows_out(r, k):
                n, r, k = at(r, WB, k), r + k // WB, k % WB
                act.wait_ge(dn_ready, n + 1)
                used(act, erow_sent[k % EB], at(r, 16 * WB // EB, 16 * (k // EB)))
                act.activation(erow[:, k % EB, :], ring[0:SLOTS, k % 2, 0:M], ACT.Copy, scale=slot_w[:, k:k + 1]
                               ).then_inc(erow_ready, 1)

            def expert_round(r, last=False):
                for k in range(WB):
                    n = at(r, WB, k)
                    if not (last and k == WB - 1):
                        slots_in(n + 1, k + 1)
                    gate_exp(n, k)
                    if k >= 2 or not isinstance(r, int) or r > 0:
                        rows_out(r, k - 2)

            slots_in(0, 0)
            expert_round(0)
            with act.Fori(1, ROUNDS - 1) as r:
                expert_round(r)
            expert_round(ROUNDS - 1, last=True)
            rows_out(ROUNDS - 1, WB - 2)
            rows_out(ROUNDS - 1, WB - 1)

            def scale(r, k):
                n = at(r, FB, k)
                act.wait_ge(nmr_ready, n + 1)
                used(act, out_stored[k], at(r, 16, 0))
                act.activation(fout[:, k, :], ysum[:, k, :], ACT.Identity, bias=nmr[:, k, :], scale=frs[:, k, :]
                               ).then_inc(fout_ready, 1)

            for k in range(FB):
                scale(0, k)
            with act.Fori(1, TILES // FB) as r:
                for k in range(FB):
                    scale(r, k)

        @block.tensor
        def _(pe):
            def begin(step):
                r, turn = PLACE[step]
                if turn >= 1:
                    pe.wait_ge(ring_read[r], turn)

            pe.wait_ge(const_ready, 2)
            for s in SEQ:
                kind = s[0]
                if kind in RINGED:
                    begin(s)
                if kind == "xt":
                    i = s[1]
                    pe.wait_ge(x_loaded[i % XB], 16 * (i // XB + 1))
                    xc = x_sb[:, i % XB, :].rearrange("t (p c) -> t c p", c=MC)
                    for c in range(MC):
                        ins = pe.transpose(bank(s)[:, c * P:(c + 1) * P], xc[:, c, :], ident[:, :])
                    ins.then_inc(xt_ready, 1)
                if kind == "proj":
                    i, name = s[1:]
                    n = BLOCKS.index(name)
                    read(pe, ("xt", i))
                    pe.wait_ge(whi_ready, n + 1)
                    if n < 4:
                        pe.wait_ge(wlo_ready, n + 1)
                    else:
                        pe.wait_ge(wlo_pool_ready, n - 3)
                    for c in range(MC):
                        for xp, wp in PASSES:
                            ins = pe.matmul(bank(s), (xt_hi, xt_lo)[xp][:, c, :], (w_hi, w_lo)[wp][:, n, :, c, :],
                                            start=(c == 0 and xp == wp == 0), stop=(c == MC - 1 and xp == 1))
                    ins.then_inc(proj_ready, 1)
                if kind == "qkt":
                    pe.wait_ge(rot_ready, QKT_AT[s[1:]] + 1)
                    for h in range(H):
                        ins = pe.transpose(bank(s)[:, h * P:(h + 1) * P],
                                           q_rot[:, h, :, :].rearrange("p a d -> p (a d)"), ident[:, :])
                    ins.then_inc(qkt_ready, 1)
                if kind == "score":
                    u, h = s[1:]
                    (i, g), n = divmod(u, G), u * H + h
                    read(pe, ("qkt", i, g))
                    if h == 0:
                        read(pe, ("qkt", i, "K"))
                    heads_done = scores_used(n)
                    if heads_done > 0:
                        pe.wait_ge(probs_ready, heads_done)
                    q = [z[:, u % 2, h * P:(h + 1) * P] for z in (qt_hi, qt_lo)]
                    k = [z[:, g, :] for z in (kt_hi, kt_lo)]
                    width, c = blocks(u) * P, score_cols(n).start
                    for a in range(0, width, 512):
                        e = min(a + 512, width)
                        last = e == width
                        for qp, kp in PASSES:
                            pe.matmul(s_ps[:, n % 2, c + a:c + e], q[qp], k[kp][:, a:e],
                                      start=(qp == kp == 0), stop=(qp == 1 and not last))
                        if last:
                            ins = pe.matmul(s_ps[:, n % 2, c + e - P:c + e], ident_bf[:, :], causal_bf[:, :],
                                            start=False, stop=True)
                    ins.then_inc(scores_ready, 1)
                if kind == "ptrans":
                    u, j = s[1:]
                    pe.wait_ge(probs_ready, H * (u + 1))
                    for h in range(H):
                        ins = pe.transpose(bank(s)[:, h * P:(h + 1) * P], probs[:, u % 2, h, j * P:(j + 1) * P],
                                           ident[:, :])
                    ins.then_inc(ptrans_ready, 1)
                if kind == "pv":
                    u, j = s[1:]
                    (i, g), n = divmod(u, G), PT_AT[s[1:]]
                    read(pe, ("ptrans", u, j))
                    if g == 0 and j == blocks(u) - 1:
                        read(pe, ("proj", i, "V"))
                    if j == 0 and u >= 1:
                        pe.wait_ge(o_ready, u)
                    pe.matmul(o_ps[:, :], v_sb[:, j, g * D:(g + 1) * D], pt[:, n % PTB, :],
                              start=(j == 0), stop=(j == blocks(u) - 1)).then_inc(pv_done, 1)
                if kind == "linv":
                    u = s[1]
                    pe.wait_ge(inv_ready, u + 1)
                    for h in range(H):
                        ins = pe.transpose(bank(s)[:, h * P:(h + 1) * P],
                                           inv_sum[:, u % 2, h:h + 1].to_broadcast([P, P]), ident[:, :])
                    ins.then_inc(linv_ready, 1)
                if kind == "outproj":
                    i = s[1]
                    pe.wait_ge(wo_loaded, 16)
                    pe.wait_ge(o_ready, G * (i + 1))
                    for h in range(G * H):
                        ins = pe.matmul(bank(s)[:, 0:M], ot[:, h // H, (h % H) * P:(h % H + 1) * P], wo[:, h, :],
                                        start=(h == 0), stop=(h == G * H - 1))
                    ins.then_inc(attn_ready, 1)
                if kind == "x1t":
                    i = s[1]
                    pe.wait_ge(x1_ready, i + 1)
                    xc = row[:, i % 2, 0:M].rearrange("t (p c) -> t c p", c=MC)
                    for c in range(MC):
                        ins = pe.transpose(bank(s)[:, c * P:(c + 1) * P], xc[:, c, :], ident[:, :])
                    ins.then_inc(x1t_ready, 1)
                if kind == "rtr":
                    read(pe, ("x1t", s[1]))
                    pe.wait_ge(wmisc_lo_ready, 2)
                    for c in range(MC):
                        for xp, wp in PASSES:
                            ins = pe.matmul(bank(s)[:, 0:E + 2 * F], (x1t_hi, x1t_lo)[xp][:, c, :],
                                            (wr_hi, wr_lo)[wp][:, c, :],
                                            start=(c == 0 and xp == wp == 0), stop=(c == MC - 1 and xp == 1))
                    ins.then_inc(rtr_ready, 1)
                if kind == "ht":
                    read(pe, ("rtr", s[1]))
                    pe.transpose(bank(s)[0:F, 0:P], hid[:, :], ident[:, :]).then_inc(ht_ready, 1)
                if kind == "count":
                    pe.wait_ge(chose_ready, s[1] + 1)
                    pe.matmul(bank(s)[:, 0:E], before_bf[:, :], chose[:, :], start=True, stop=False)
                    pe.matmul(bank(s)[:, 0:E], ones_bf[:, :], taken[:, :], start=False, stop=True
                              ).then_inc(count_ready, 1)
                if kind == "sd":
                    read(pe, ("ht", s[1]))
                    for n, (hp, wp) in enumerate(PASSES):
                        ins = pe.matmul(bank(s)[:, 0:M], (ht_hi, ht_lo)[hp][:, :], (wsd_hi, wsd_lo)[wp][:, :],
                                        start=(n == 0), stop=(n == 2))
                    ins.then_inc(sd_ready, 1)

            pe.wait_ge(attention_left, 1)

            def slots_t(r, k):
                n, r, k = at(r, WB, k), r + k // WB, k % WB
                pe.wait_ge(srow_loaded[k], at(r, 16, 16))
                used(pe, sxt_ready, n - 1)
                xc = srow[:, k, 0:M].rearrange("t (p c) -> t c p", c=MC)
                for c in range(MC):
                    ins = pe.transpose(s_ps[:, k % 2, c * SLOTS:(c + 1) * SLOTS], xc[:, c, :],
                                       ident[0:SLOTS, 0:SLOTS])
                ins.then_inc(st_ready, 1)

            def gate_up(r, k):
                n = at(r, WB, k)
                pe.wait_ge(experts_loaded[k], at(r, 80, 80))
                pe.wait_ge(sxt_ready, n + 1)
                used(pe, hid_t_ready, n - 1)
                for a in range(2):
                    for e in range(2):
                        for c in range(MC):
                            ins = pe.matmul(s_ps[0:F, k % 2, 512 + a * SLOTS + e * CAP:512 + a * SLOTS + (e + 1) * CAP],
                                            wgu[:, k, e, a, c, :], sxt[:, k % 2, c, e * CAP:(e + 1) * CAP],
                                            start=(c == 0), stop=(c == MC - 1))
                ins.then_inc(gu_ready, 1)

            def down(r, k):
                n, k = at(r, WB, k), k % WB
                pe.wait_ge(hid_t_ready, n + 1)
                used(pe, erow_ready, n - 1)
                for e in range(2):
                    ins = pe.matmul(ring[0:SLOTS, k % 2, 0:M], hid_t[:, k % 2, e, :], wdn[:, k, e, :],
                                    start=(e == 0), stop=(e == 1))
                ins.then_inc(dn_ready, 1)

            def expert_round(r, last=False):
                for k in range(WB):
                    if not (last and k == WB - 1):
                        slots_t(r, k + 1)
                    gate_up(r, k)
                    if k >= 2 or not isinstance(r, int) or r > 0:
                        down(r, k - 2)

            slots_t(0, 0)
            expert_round(0)
            with pe.Fori(1, ROUNDS - 1) as r:
                expert_round(r)
            expert_round(ROUNDS - 1, last=True)
            down(ROUNDS - 1, WB - 2)
            down(ROUNDS - 1, WB - 1)

        @block.vector
        def _(dve):
            def low(lo, raw, hi):
                return dve.tensor_tensor(lo, raw, hi.bitcast(F32), ALU.subtract)

            for n in range(4):
                dve.wait_ge(whi_ready, n + 1)
                low(w_lo_f[:, n, :], w_raw[:, n, :], w_hi_f[:, n, :]).then_inc(wlo_ready, 1)
            dve.wait_ge(wmisc_hi_ready, 2)
            low(wr_lo[:, :, :], raw_r, wr_hi[:, :, :]).then_inc(wmisc_lo_ready, 1)
            low(wsd_lo[:, :], raw_d, wsd_hi[:, :]).then_inc(wmisc_lo_ready, 1)
            dve.wait_ge(bias_loaded, 16)
            dve.wait_ge(const_ready, 2)
            dve.wait_ge(table_loaded, 32)

            links = [0]

            def later(ins):
                links[0] += 1
                ins.then_inc(dve_own, 1)

            def settled():
                dve.wait_ge(dve_own, links[0])

            def after(ins):
                later(ins)
                settled()

            def hold(n):
                dve.tensor_copy(held[0:1, n:n + 1], minus_half[0:1, :])

            def wide(ap, n):
                return ap.rearrange("p (a x) -> p a x", a=1).to_broadcast([P, n, ap.shape[1]])

            def each(ap, n):
                return ap.rearrange("p (x a) -> p x a", a=1).to_broadcast([P, ap.shape[1], n])

            for s in SEQ:
                kind = s[0]
                if kind == "xt":
                    dve.wait_ge(xt_hi_ready, s[1] + 1)
                    reader(low(xt_lo[:, :, :], bank(s)[:, 0:MC * P].rearrange("p (c t) -> p c t", c=MC),
                               xt_hi[:, :, :]), s)
                if kind == "proj" and s[2] != "V":
                    i, n = s[1], ROPE_AT[s[1:]]
                    dve.wait_ge(proj_ready, PROJ_AT[s[1:]] + 1)
                    if n >= 1:
                        dve.wait_ge(rot_ready, n)
                    src = bank(s).rearrange("p (x d) -> p x d", d=D // 2)
                    dve.tensor_tensor(q_cos[:, :, :, :].rearrange("p h a d -> p (h a) d"), src,
                                      wide(cos_sb[:, i % NT, :], 2 * H), ALU.mult)
                    reader(dve.tensor_tensor(q_sin[:, :, :, :].rearrange("p h a d -> p (h a) d"), src,
                                             wide(sin_sb[:, i % NT, :], 2 * H), ALU.mult), s)
                if kind == "qkt":
                    i, name = s[1:]
                    dve.wait_ge(qk_hi_ready, QKT_AT[s[1:]] + 1)
                    if name == "K":
                        kt_cols = slice(i % NT * P, (i % NT + 1) * P)
                        reader(low(kt_lo[:, :, kt_cols], bank(s).rearrange("p (g t) -> p g t", g=G),
                                   kt_hi[:, :, kt_cols]), s)
                    else:
                        u = i * G + name
                        reader(low(qt_lo[:, u % 2, :], bank(s), qt_hi[:, u % 2, :]), s)
                if kind == "score":
                    u, h = s[1:]
                    n = u * H + h
                    dve.wait_ge(scores_ready, n + 1)
                    dve.tensor_reduce(neg_max[:, n % 8:n % 8 + 1], s_ps[:, n % 2, score_cols(n)], AX_X, ALU.max,
                                      negate=True).then_inc(max_ready, 1)
                if kind == "ptrans" and s[2] == 0:
                    u = s[1]
                    dve.wait_ge(probs_ready, H * (u + 1))
                    if u >= 2:
                        dve.wait_ge(linv_ready, u - 1)
                    dve.reciprocal(inv_sum[:, u % 2, :], row_sum[:, u % 2, :]).then_inc(inv_ready, 1)
                if kind == "omul":
                    u = s[1]
                    i, g = divmod(u, G)
                    read(dve, ("linv", u))
                    dve.wait_ge(pv_done, PT_AT[(u, blocks(u) - 1)] + 1)
                    if i >= 1:
                        dve.wait_ge(attn_ready, i)
                    dve.tensor_tensor(ot[:, g, :], o_ps[:, :], inv_row[:, :], ALU.mult).then_inc(o_ready, 1)
                if kind == "outproj":
                    i = s[1]
                    dve.wait_ge(attn_ready, i + 1)
                    reader(dve.tensor_tensor(y_sb[:, :], bank(s)[:, 0:M], x_sb[:, i % XB, :], ALU.add), s)
                    read(dve, s)
                    after(dve.bn_stats(stats[:, :], y_sb[:, :]))
                    after(dve.bn_aggr(mean_var[:, :], stats[:, :]))
                    dve.tensor_scalar(var_eps[:, :], mean_var[:, 1:2], EPS, None, ALU.add).then_inc(var_ready, 1)
                if kind == "norm":
                    i = s[1]
                    dve.wait_ge(rstd_ready, i + 1)
                    if i >= 2:
                        dve.wait_ge(scattered[i % 2], 16 * K * (i // 2))
                    dve.tensor_scalar(row[:, i % 2, 0:M], y_sb[:, :], mean_var[:, 0:1], rstd[:, 0:1],
                                      ALU.subtract, ALU.mult).then_inc(x1_ready, 1)
                    after(dve.tensor_scalar(token[:, :], token[:, :], float(P), None, ALU.add))
                    dve.tensor_copy(row[:, i % 2, T_AT:T_AT + 1], token[:, :])
                if kind == "x1t":
                    dve.wait_ge(x1t_hi_ready, s[1] + 1)
                    reader(low(x1t_lo[:, :, :], bank(s)[:, 0:MC * P].rearrange("p (c t) -> p c t", c=MC),
                               x1t_hi[:, :, :]), s)
                if kind == "rtr":
                    dve.wait_ge(exp_ready, s[1] + 1)
                    if s[1] >= 1:
                        dve.wait_ge(ht_ready, s[1])
                    after(dve.tensor_scalar(sig[:, :], sig[:, :], 1.0, None, ALU.add))
                    after(dve.reciprocal(sig[:, :], sig[:, :]))
                    after(dve.tensor_tensor(hid[:, :], bank(s)[:, E:E + F], sig[:, E:], ALU.mult))
                    reader(dve.tensor_tensor(hid[:, :], bank(s)[:, E + F:E + 2 * F], hid[:, :], ALU.mult), s)
                if kind == "pick":
                    i, part = s[1:]
                    settled()
                if kind == "pick" and part == 0:
                    after(dve.tensor_tensor(biased[:, :], sig[:, 0:E], bias_sb[:, :], ALU.add))
                    for n in range(EG - 1):
                        dve.max(top2[:, n, :], biased[:, n * 8:(n + 1) * 8])
                    later(dve.max(top2[:, EG - 1, :], biased[:, E - 8:]))
                if kind == "pick" and part == 1:
                    after(dve.tensor_tensor(group[:, :], top2[:, :, 0], top2[:, :, 1], ALU.add))
                    later(dve.max(group_top[:, :], group[:, :]))
                if kind == "pick" and part == 2:
                    after(dve.max_index(group_at[:, :], group_top[:, :], group[:, :]))
                    later(dve.tensor_copy(group_atf[:, :], group_at[:, :]))
                if kind == "pick" and part == 3:
                    after(dve.tensor_tensor(kept4[:, :, :], each(iota_e[:, 0:EG], KG),
                                            wide(group_atf[:, 0:KG], EG), ALU.is_equal))
                    later(dve.tensor_reduce(kept[:, :], kept4[:, :, :], AX_X, ALU.add))
                if kind == "pick" and part == 4:
                    dve.tensor_tensor(open_[:, :].rearrange("p (g e) -> p g e", g=EG),
                                      biased[:, :].rearrange("p (g e) -> p g e", g=EG),
                                      each(kept[:, :], E // EG), ALU.mult)
                    after(dve.tensor_scalar(barred[:, :], kept[:, :], 1.0, -NEG, ALU.subtract, ALU.mult))
                    later(dve.tensor_tensor(open_[:, :].rearrange("p (g e) -> p g e", g=EG),
                                            open_[:, :].rearrange("p (g e) -> p g e", g=EG),
                                            each(barred[:, :], E // EG), ALU.add))
                if kind == "pick" and part == 5:
                    after(dve.max(top8[:, :], open_[:, :]))
                    after(dve.max_index(top_at[:, :], top8[:, :], open_[:, :]))
                    later(dve.tensor_copy(top_atf[:, :], top_at[:, :]))
                if kind == "pick" and part == 6:
                    after(dve.tensor_tensor(onehot[:, :, :], wide(iota_e[:, :], K),
                                            each(top_atf[:, 0:K], E), ALU.is_equal))
                    if i >= 1:
                        dve.wait_ge(count_ready, i)
                    with nc.allow_low_precision("zeros and ones"):
                        dve.tensor_reduce(chose[:, :], onehot[:, :, :].rearrange("p k e -> p e k"), AX_X, ALU.add
                                          ).then_inc(chose_ready, 1)
                if kind == "pick" and part == 7:
                    after(dve.tensor_tensor(onehot_s[:, :, :], onehot[:, :, :], wide(sig[:, 0:E], K), ALU.mult))
                    dve.tensor_reduce(top_s[:, :], onehot_s[:, :, :], AX_X, ALU.add).then_inc(picked, 1)
                    dve.wait_ge(picked, i + 1)
                    after(dve.tensor_reduce(top_sum[:, :], top_s[:, :], AX_X, ALU.add))
                    after(dve.reciprocal(top_inv[:, :], top_sum[:, :]))
                    dve.tensor_scalar(row[:, i % 2, W_AT:W_AT + K], top_s[:, :], top_inv[:, 0:1], SCALE,
                                      ALU.mult, ALU.mult)
                if kind == "ht":
                    dve.wait_ge(ht_hi_ready, s[1] + 1)
                    reader(low(ht_lo[:, :], bank(s)[0:F, 0:P], ht_hi[:, :]), s)
                if kind == "count":
                    dve.wait_ge(count_ready, s[1] + 1)
                    reader(dve.tensor_tensor(onehot_s[:, :, :], onehot[:, :, :], wide(bank(s)[:, 0:E], K), ALU.mult), s)
                if kind == "sd":
                    i = s[1]
                    dve.wait_ge(sd_ready, i + 1)
                    if i >= 1:
                        dve.wait_ge(z_stored, 16 * i)
                    reader(dve.tensor_tensor(z_sb[:, :], bank(s)[:, 0:M], row[:, i % 2, 0:M], ALU.add), s)
                if kind == "place":
                    i = s[1]
                    read(dve, ("count", i))
                    after(dve.tensor_reduce(pos6[:, :], onehot_s[:, :, :], AX_X, ALU.add))
                    with nc.allow_low_precision("at most one a tile"):
                        dve.tensor_tensor(taken[:, :], taken[:, :], chose[:, :], ALU.add)
                    after(dve.tensor_scalar(over[:, :], pos6[:, :], float(CAP), FAR, ALU.is_ge, ALU.mult))
                    after(dve.tensor_tensor(pos6[:, :], pos6[:, :], over[:, :], ALU.add))
                    after(dve.scalar_tensor_tensor(row[:, i % 2, S_AT:S_AT + K], top_atf[:, 0:K], float(CAP),
                                                             pos6[:, :], ALU.mult, ALU.add))
                    dve.tensor_copy(slot_u[:, i % 2, :], row[:, i % 2, S_AT:S_AT + K]).then_inc(placed, 1)
            dve.wait_ge(placed, TILES)
            dve.tensor_copy(dve_cell[:, :], pos6[:, 0:1]).then_inc(attention_left, 1)

            dve.wait_ge(slot_now_ready, 2)
            links[0] = 0

            def after2(r, ins):
                links[0] += 1
                ins.then_inc(dve_own2, 1)
                return at(r, EXPERT_LINKS * WB, links[0])

            def need(mark):
                dve.wait_ge(dve_own2, mark)

            def expert_round(r):
                links[0] = 0
                for k in range(WB):
                    n = at(r, WB, k)
                    half = s_ps[0:F, k % 2, 512:512 + 2 * SLOTS]
                    dve.wait_ge(srow_loaded[k], at(r, 16, 16))
                    now = after2(r, dve.tensor_scalar(slot_now[:, :], slot_now[:, :], float(SLOTS), None, ALU.add))
                    dve.wait_ge(gexp_ready, n + 1)
                    plus = after2(r, dve.tensor_scalar(gsig[:, :], gexp[:, :], 1.0, None, ALU.add))
                    need(now)
                    used(dve, erow_ready, at(r, WB, k - WB + 1))
                    dve.scalar_tensor_tensor(mine[:, :], srow[:, k, S_AT:S_AT + K], slot_now[:, 0:1],
                                             srow[:, k, W_AT:W_AT + K], ALU.is_equal, ALU.mult,
                                             accum_out=slot_w[:, k:k + 1])
                    place = after2(r, dve.scalar_tensor_tensor(mine_k[:, :], srow[:, k, S_AT:S_AT + K],
                                                               slot_now[:, 0:1], choice_far[0:SLOTS, :],
                                                               ALU.is_equal, ALU.mult, accum_out=which[:, :]))
                    need(plus)
                    inverse = after2(r, dve.reciprocal(gact[:, :], gsig[:, :]))
                    need(place)
                    goal_at = after2(r, dve.tensor_scalar(goal[:, :], srow[:, k, T_AT:T_AT + 1], float(K), which[:, 0:1],
                                                          ALU.mult, ALU.add))
                    need(inverse)
                    gated = after2(r, dve.tensor_tensor(gsig[:, :], half[:, 0:SLOTS], gact[:, :], ALU.mult))
                    need(goal_at)
                    used(dve, erow_sent[k % EB], at(r, 16 * WB // EB, 16 * (k // EB)))
                    dve.tensor_scalar(goal_u[:, k % EB:k % EB + 1], goal[:, :], FAR, None, ALU.add
                                      ).then_inc(goal_ready, 1)
                    need(gated)
                    used(dve, dn_ready, n - 1)
                    for e in range(2):
                        cols = slice(e * CAP, (e + 1) * CAP)
                        ins = dve.tensor_tensor(hid_t[:, k % 2, e, cols], half[:, SLOTS + e * CAP:SLOTS + (e + 1) * CAP],
                                                gsig[:, cols], ALU.mult)
                    ins.then_inc(hid_t_ready, 1)
                assert links[0] == EXPERT_LINKS * WB, links[0] / WB

            expert_round(0)
            with dve.Fori(1, ROUNDS) as r:
                expert_round(r)

            def add(r, ins):
                links[0] += 1
                ins.then_inc(fin_own, 1)
                dve.wait_ge(fin_own, at(r, SUM_LINKS * FB, links[0]))

            def add_up(r, k):
                t = at(r, FB, k)
                dve.wait_ge(half_ready, t + 1)
                dve.wait_ge(zf_loaded[k], at(r, 16, 16))
                used(dve, fout_ready, t - FB + 1)
                dve.tensor_tensor(ysum[:, k, :], yk[:, k, 0, :], zf[:, k, :], ALU.add)
                add(r, dve.tensor_tensor(yk[:, k, 1, :], yk[:, k, 1, :], yk[:, k, 2, :], ALU.add))
                add(r, dve.tensor_tensor(ysum[:, k, :], ysum[:, k, :], yk[:, k, 1, :], ALU.add))
                add(r, dve.bn_stats(fstats[:, :], ysum[:, k, :]))
                hold(k)
                add(r, dve.bn_aggr(fmv[:, k, :], fstats[:, :]))
                dve.tensor_scalar(fve[:, k, :], fmv[:, k, 1:2], EPS, None, ALU.add).then_inc(fvar_ready, 1)

            def shift(r, k):
                dve.wait_ge(frs_ready, at(r, FB, k + 1))
                dve.tensor_scalar(nmr[:, k, :], fmv[:, k, 0:1], -1.0, frs[:, k, 0:1], ALU.mult, ALU.mult
                                  ).then_inc(nmr_ready, 1)

            def final_round(r):
                links[0] = 0
                for k in range(FB):
                    add_up(r, k)
                    if k:
                        shift(r, k - 1)
                shift(r, FB - 1)
                assert links[0] == SUM_LINKS * FB, links

            final_round(0)
            with dve.Fori(1, TILES // FB) as r:
                final_round(r)


_INS = ["L0_attn_x", "L0_attn_w_aq", "L0_attn_w_ak", "L0_attn_w_av", "L0_attn_w_ao", "L0_ffn_gate_w", "L0_ffn_bias",
        "L0_ffn_w_gate", "L0_ffn_w_up", "L0_ffn_w_down", "L0_ffn_ws_gate", "L0_ffn_ws_up", "L0_ffn_ws_down"]


def rope_tables():
    half = D // 2
    freqs = np.power(10000.0, -np.arange(half) / half).astype(np.float32)
    angles = (np.arange(T, dtype=np.float32)[:, None] * freqs[None, :]).astype(np.float64)
    scale = float(D) ** -0.25
    return (np.cos(angles) * scale).astype(np.float32), (np.sin(angles) * scale).astype(np.float32)


def kernel(**inputs):
    import concourse.bacc as _bacc
    from concourse import mybir as _mybir
    from concourse.bass_utils import run_bass_kernel_spmd as _run

    nc = _bacc.Bacc("TRN2", target_bir_lowering=False, num_devices=1)
    arrays, args = {}, []
    cos, sin = rope_tables()
    for name, a in [(n, np.ascontiguousarray(inputs[n])) for n in _INS] + [("rope_cos", cos), ("rope_sin", sin)]:
        arrays[f"in_{name}_dram"] = a
        args.append(nc.dram_tensor(f"in_{name}_dram", a.shape, _mybir.dt.from_np(a.dtype), kind="ExternalInput").ap())
    args.append(nc.dram_tensor("out_0_dram", (B, T, M), F32, kind="ExternalOutput").ap())
    build(nc, *args)
    r = _run(nc, [arrays], core_ids=[0])
    return r.results[0]["out_0_dram"]
```

```python
from contextlib import ExitStack

import numpy as np

import concourse.bass as bass
from concourse import mybir

ALU = mybir.AluOpType
ACT = mybir.ActivationFunctionType
AX_X = mybir.AxisListType.X
F32 = mybir.dt.float32
F32R = mybir.dt.float32r
BF16 = mybir.dt.bfloat16
U32 = mybir.dt.uint32

P = 128
B, T, M = 2, 1024, 256
G, H, D = 4, 4, 128
NT = T // P
TILES = B * NT
MC = M // P
HD = H * D
NEG = -1e30
EPS = 1e-5
E, K, F = 64, 6, 96
EG, KG = 8, 4
SCALE = 2.5
CAP = 2 * (256 * K // E)
PAIRS = E // 2
WB = 8
ROUNDS = PAIRS // WB
EB = 4
FB = 4
HALF = P // 2
TOKENS = B * T
W_AT, S_AT, T_AT, ROW = M, M + K, M + 2 * K, M + 16
FAR = 1.0e5

UNITS = TILES * G
HEADS = UNITS * H
PTB = 3
LAG = 2
SUM_LINKS = 4
EXPERT_LINKS = 6
RING = 3
XB = 3
SCALED_FROM = 6
POOL_TILES = range(4, NT)
BLOCKS = ["K", "V", 0, 1, 2, 3]
SPLIT_AT = {("xt", 0): ["K"], ("qkt", 0, "K"): [0], ("qkt", 0, 0): [1, "V"], ("score", 0, 0): [2, 3]}
BLOCKS_IN_TURN = [n for names in SPLIT_AT.values() for n in names]


def scaled_first(u):
    return blocks(u) >= SCALED_FROM


def blocks(u):
    return u // G % NT + 1


BETWEEN = [
    (("qkt", 1), 0, (1, 0, 0, 0)),
    (("proj", 2), 0, (2, 1, 1, 1)),
    (("qkt", 2), 0, (6, 5, 4, 4)),
    (("proj", 3), 0, (6, 6, 5, 5)),
    (("qkt", 3), 0, (8, 8, 8, 8)),
    (("xt",), 1, (6, 7, 7, 6)),
    (("proj", "K"), 1, (10, 9, 9, 9)),
    (("qkt", "K"), 1, (12, 11, 11, 11)),
    (("proj", 0), 1, (12, 11, 12, 11)),
    (("qkt", 0), 1, (13, 13, 14, 14)),
    (("proj", 1), 1, (13, 13, 14, 14)),
    (("proj", "V"), 1, (14, 12, 14, 14)),
    (("pick", 6), -2, (1, 1, 0, 0)),
    (("pick", 7), -2, (1, 1, 1, 1)),
    (("count",), -2, (2, 1, 2, 2)),
    (("place",), -2, (3, 3, 3, 3)),
    (("outproj",), -1, (6, 7, 6, 6)),
    (("norm",), -1, (7, 7, 7, 7)),
    (("x1t",), -1, (8, 8, 8, 8)),
    (("rtr",), -1, (9, 9, 9, 9)),
    (("pick", 0), -1, (11, 10, 10, 10)),
    (("ht",), -1, (11, 11, 11, 11)),
    (("pick", 1), -1, (11, 12, 11, 12)),
    (("sd",), -1, (12, 12, 12, 12)),
    (("pick", 2), -1, (12, 12, 12, 12)),
    (("pick", 3), -1, (12, 13, 13, 13)),
    (("pick", 4), -1, (14, 14, 14, 13)),
    (("pick", 5), -1, (14, 14, 15, 13)),
]
AT_START = [("qkt", "K"), ("proj", 0), ("qkt", 0), ("proj", 1), ("proj", "V")]


def schedule():
    seq, waiting = [], []

    def product():
        u, j = waiting.pop(0)
        if j == blocks(u) - 1:
            seq.extend([] if scaled_first(u) else [("linv", u)])
        seq.append(("pv", u, j))
        if j == blocks(u) - 1:
            seq.append(("omul", u))

    def lagging(n):
        u, h = divmod(n, H)
        for j in range(-(-h * blocks(u) // H), -(-(h + 1) * blocks(u) // H)):
            seq.append(("ptrans", u, j))
            waiting.append((u, j))
            if len(waiting) > LAG:
                product()
            yield j

    def scale(n):
        if scaled_first(n // H):
            seq.append(("scale", n))

    def drain(below):
        while waiting and waiting[0][0] < below:
            product()

    def misc(i, at):
        out = []
        for step, ahead, heads in BETWEEN:
            tile = i + ahead
            if heads[min(i % NT, len(heads) - 1)] != at or not 0 <= tile < TILES:
                continue
            if not (ahead == 1 and tile % NT == 0 and step in AT_START):
                out.append((step[0], tile) + step[1:])
        return out

    late = H + 1
    for n in range(HEADS):
        u, h = divmod(n, H)
        i, g = divmod(u, G)
        if n % (NT * G * H) == 0:
            if i == 0:
                seq += [("xt", 0), ("proj", 0, "K")]
            seq += [("qkt", i, "K"), ("proj", i, 0)]
            if i:
                scale(n - 1)
                for m in range(n - late, n):
                    for _ in lagging(m):
                        pass
                drain(u)
            seq += [("qkt", i, 0), ("proj", i, 1), ("proj", i, "V")]
        seq.append(("score", u, h))
        if n % (NT * G * H):
            scale(n - 1)
        before = n - late
        first = True
        if before >= 0 and before // (NT * G * H) == n // (NT * G * H):
            for _ in lagging(before):
                if first:
                    seq.append(("exp", u, h))
                first = False
        if first:
            seq.append(("exp", u, h))
        if (g, h) == (1, 2):
            drain(i * G)
        seq += misc(i, n % (G * H))
    p = TILES - 1
    seq += [("pick", p - 1, 6), ("pick", p - 1, 7), ("count", p - 1), ("place", p - 1)]
    scale(HEADS - 1)
    for m in range(HEADS - late, HEADS):
        for _ in lagging(m):
            pass
    drain(UNITS)
    seq += [(s, p) for s in ("outproj", "norm", "x1t", "rtr")] + [("pick", p, 0), ("ht", p), ("pick", p, 1), ("sd", p)]
    seq += [("pick", p, n) for n in range(2, 8)] + [("count", p), ("place", p)]
    return seq


def by_pool(step):
    return step[1] % NT in POOL_TILES


RINGED = ("xt", "proj", "qkt", "ptrans", "linv", "outproj", "x1t", "rtr", "ht", "count", "sd")


def ring_places(seq):
    places, n = {}, 0
    for s in seq:
        if s[0] in RINGED:
            places[s] = (n % RING, n // RING)
            n += 1
    return places


SEQ = schedule()
PLACE = ring_places(SEQ)
PT_AT = {s[1:]: n for n, s in enumerate(s for s in SEQ if s[0] == "ptrans")}
PT_ALL = len(PT_AT)
SCALED_AT = {s[1]: n for n, s in enumerate(s for s in SEQ if s[0] == "scale")}
INV_AT = {s[1]: n for n, s in enumerate(s for s in SEQ if s[0] == "linv")}
PROJ_AT = {s[1:]: n for n, s in enumerate(s for s in SEQ if s[0] == "proj")}
ROPE_AT = {k: n for n, k in enumerate(k for k in PROJ_AT if k[1] != "V")}
QKT_AT = {s[1:]: n for n, s in enumerate(s for s in SEQ if s[0] == "qkt")}
assert [s[1:] for s in SEQ if s[0] == "qkt"] == list(ROPE_AT)


def build(nc, x, w_aq, w_ak, w_av, w_ao, gate_w, bias, w_gate, w_up, w_down, ws_gate, ws_up, ws_down,
          rope_cos, rope_sin, out):
    slot_rows = nc.dram_tensor("slot_rows", (E * HALF, ROW), F32, kind="Internal").ap()
    expert_rows = nc.dram_tensor("expert_rows", (TOKENS * K, M), F32, kind="Internal").ap()
    z_rows = nc.dram_tensor("z_rows", (TOKENS, M), F32, kind="Internal").ap()
    xf = x.rearrange("b t m -> (b t) m")
    of = out.rearrange("b t m -> (b t) m")

    with ExitStack() as ctx:
        def sb(name, shape, dt, where=ctx):
            return where.enter_context(nc.sbuf_tensor(name, shape, dt))

        def sem(name):
            return ctx.enter_context(nc.semaphore(name))

        ident = sb("ident", [P, P], F32)
        ident_bf = sb("ident_bf", [P, P], BF16)
        causal_bf = sb("causal_bf", [P, P], BF16)
        before_bf = sb("before_bf", [P, P], BF16)
        ones_bf = sb("ones_bf", [P, P], BF16)
        minus_half = sb("minus_half", [P, 1], F32)
        iota_e = sb("iota_e", [P, E], F32)
        choice_far = sb("choice_far", [P, K], F32)
        pool_cell = sb("pool_cell", [P, 1], F32)
        dve_cell = sb("dve_cell", [P, 1], F32)
        held = sb("held", [1, FB], F32)
        bias_sb = sb("bias_sb", [P, E], F32)
        blank = sb("blank", [P, ROW], F32)
        token = sb("token", [P, 1], F32)
        taken = sb("taken", [P, E], BF16)
        wr_hi = sb("wr_hi", [P, MC, 256], F32R)
        wr_lo = sb("wr_lo", [P, MC, 256], F32R)
        wsd_hi = sb("wsd_hi", [F, M], F32R)
        wsd_lo = sb("wsd_lo", [F, M], F32R)

        att = ExitStack()
        w_hi = sb("w_hi", [P, 6, H, MC, D], F32R, att)
        w_lo = sb("w_lo", [P, 6, H, MC, D], F32R, att)
        wo = sb("wo", [P, G * H, M], F32, att)
        kt_hi = sb("kt_hi", [P, G, T], F32R, att)
        kt_lo = sb("kt_lo", [P, G, T], F32R, att)
        v_sb = sb("v_sb", [P, NT, G * D], F32, att)
        probs = sb("probs", [P, 2, H, T], F32, att)
        pt = sb("pt", [P, PTB, HD], F32, att)
        qt_hi = sb("qt_hi", [P, 2, HD], F32R, att)
        qt_lo = sb("qt_lo", [P, 2, HD], F32R, att)
        cos_sb = sb("cos_sb", [P, NT, D // 2], F32, att)
        sin_sb = sb("sin_sb", [P, NT, D // 2], F32, att)
        x_sb = sb("x_sb", [P, XB, M], F32, att)
        xt_hi = sb("xt_hi", [P, MC, P], F32R, att)
        xt_lo = sb("xt_lo", [P, MC, P], F32R, att)
        q_cos = sb("q_cos", [P, H, 2, D // 2], F32, att)
        q_sin = sb("q_sin", [P, H, 2, D // 2], F32, att)
        q_rot = sb("q_rot", [P, H, 2, D // 2], F32, att)
        neg_max = sb("neg_max", [P, 8], F32, att)
        row_sum = sb("row_sum", [P, 2, H], F32, att)
        inv_sum = sb("inv_sum", [P, 2, H], F32, att)
        inv_row = sb("inv_row", [P, HD], F32, att)
        ot = sb("ot", [P, G, HD], F32, att)
        row = sb("row", [P, 2, ROW], F32, att)
        y_sb = sb("y_sb", [P, M], F32, att)
        stats = sb("stats", [P, 6], F32, att)
        mean_var = sb("mean_var", [P, 2], F32, att)
        var_eps = sb("var_eps", [P, 1], F32, att)
        rstd = sb("rstd", [P, 1], F32, att)
        x1t_hi = sb("x1t_hi", [P, MC, P], F32R, att)
        x1t_lo = sb("x1t_lo", [P, MC, P], F32R, att)
        sig = sb("sig", [P, E + F], F32, att)
        hid = sb("hid", [P, F], F32, att)
        ht_hi = sb("ht_hi", [F, P], F32R, att)
        ht_lo = sb("ht_lo", [F, P], F32R, att)
        z_sb = sb("z_sb", [P, M], F32, att)
        biased = sb("biased", [P, E], F32, att)
        top2 = sb("top2", [P, EG, 8], F32, att)
        group = sb("group", [P, EG], F32, att)
        group_top = sb("group_top", [P, 8], F32, att)
        group_at = sb("group_at", [P, 8], U32, att)
        group_atf = sb("group_atf", [P, 8], F32, att)
        kept4 = sb("kept4", [P, EG, KG], F32, att)
        kept = sb("kept", [P, EG], F32, att)
        barred = sb("barred", [P, EG], F32, att)
        open_ = sb("open_", [P, E], F32, att)
        top8 = sb("top8", [P, 8], F32, att)
        top_at = sb("top_at", [P, 8], U32, att)
        top_atf = sb("top_atf", [P, 8], F32, att)
        onehot = sb("onehot", [P, K, E], F32, att)
        onehot_s = sb("onehot_s", [P, K, E], F32, att)
        chose = sb("chose", [P, E], BF16, att)
        top_s = sb("top_s", [P, K], F32, att)
        top_sum = sb("top_sum", [P, 1], F32, att)
        top_inv = sb("top_inv", [P, 1], F32, att)
        pos6 = sb("pos6", [P, K], F32, att)
        over = sb("over", [P, K], F32, att)
        slot_u = sb("slot_u", [P, 2, K], U32, att)
        att.close()

        exp = ExitStack()
        wgu = sb("wgu", [P, WB, 2, 2, MC, F], F32, exp)
        wdn = sb("wdn", [F, WB, 2, M], F32, exp)
        srow = sb("srow", [P, WB, ROW], F32, exp)
        sxt = sb("sxt", [P, 2, MC, P], F32, exp)
        gexp = sb("gexp", [P, F], F32, exp)
        gsig = sb("gsig", [P, F], F32, exp)
        gact = sb("gact", [P, F], F32, exp)
        hid_t = sb("hid_t", [F, 2, P], F32, exp)
        hid_e = sb("hid_e", [P, 2, F], F32, exp)
        slot_now = sb("slot_now", [P, 1], F32, exp)
        mine = sb("mine", [P, K], F32, exp)
        mine_k = sb("mine_k", [P, K], F32, exp)
        slot_w = sb("slot_w", [P, WB], F32, exp)
        which = sb("which", [P, 1], F32, exp)
        goal = sb("goal", [P, 1], F32, exp)
        goal_u = sb("goal_u", [P, EB], U32, exp)
        nmr = sb("nmr", [P, FB, 1], F32, exp)
        erow = sb("erow", [P, EB, M], F32, exp)
        yk = sb("yk", [P, FB, K, M], F32, exp)
        zf = sb("zf", [P, FB, M], F32, exp)
        ysum = sb("ysum", [P, FB, M], F32, exp)
        fstats = sb("fstats", [P, 6], F32, exp)
        fmv = sb("fmv", [P, FB, 2], F32, exp)
        fve = sb("fve", [P, FB, 1], F32, exp)
        frs = sb("frs", [P, FB, 1], F32, exp)
        fout = sb("fout", [P, FB, M], F32, exp)
        exp.close()

        s_ps = ctx.enter_context(nc.psum_tensor("s_ps", [P, 2, T], F32))
        o_ps = ctx.enter_context(nc.psum_tensor("o_ps", [P, 512], F32))
        ring = ctx.enter_context(nc.psum_tensor("ring", [P, RING, 512], F32))

        const_ready = sem("const_ready")
        ident_ready = sem("ident_ready")
        pool_own = sem("pool_own")
        w_loaded = [sem(f"w_loaded{n}") for n in range(6)]
        wo_loaded = sem("wo_loaded")
        wr_loaded = sem("wr_loaded")
        wsd_loaded = sem("wsd_loaded")
        table_loaded = sem("table_loaded")
        bias_loaded = sem("bias_loaded")
        whi_ready = [sem(f"whi_ready{n}") for n in range(6)]
        wlo_ready = [sem(f"wlo_ready{n}") for n in range(6)]
        wmisc_hi_ready = sem("wmisc_hi_ready")
        wmisc_lo_ready = sem("wmisc_lo_ready")
        picked = sem("picked")
        slot_now_ready = sem("slot_now_ready")
        hid_e_ready = sem("hid_e_ready")
        htr_ready = sem("htr_ready")
        dve_own2 = sem("dve_own2")
        blank_stored = sem("blank_stored")
        experts_blank = sem("experts_blank")
        attention_left = sem("attention_left")
        x_loaded = [sem(f"x_loaded{n}") for n in range(XB)]
        ring_read = [sem(f"ring_read{r}") for r in range(RING)]
        xt_ready = sem("xt_ready")
        xt_hi_ready = sem("xt_hi_ready")
        proj_ready = sem("proj_ready")
        rot_ready = sem("rot_ready")
        qkt_ready = sem("qkt_ready")
        qk_hi_ready = sem("qk_hi_ready")
        scores_ready = sem("scores_ready")
        max_ready = sem("max_ready")
        probs_ready = sem("probs_ready")
        ptrans_ready = sem("ptrans_ready")
        pv_done = sem("pv_done")
        inv_ready = sem("inv_ready")
        scaled_ready = sem("scaled_ready")
        linv_ready = sem("linv_ready")
        o_ready = sem("o_ready")
        attn_ready = sem("attn_ready")
        var_ready = sem("var_ready")
        rstd_ready = sem("rstd_ready")
        x1_ready = sem("x1_ready")
        x1t_ready = sem("x1t_ready")
        x1t_hi_ready = sem("x1t_hi_ready")
        rtr_ready = sem("rtr_ready")
        exp_ready = sem("exp_ready")
        ht_ready = sem("ht_ready")
        ht_hi_ready = sem("ht_hi_ready")
        sd_ready = sem("sd_ready")
        z_stored = sem("z_stored")
        chose_ready = sem("chose_ready")
        count_ready = sem("count_ready")
        placed = sem("placed")
        scattered = [sem(f"scattered{n}") for n in range(2)]
        stood = sem("stood")
        dve_own = sem("dve_own")

        experts_loaded = [sem(f"experts_loaded{n}") for n in range(WB)]
        srow_loaded = [sem(f"srow_loaded{n}") for n in range(WB)]
        st_ready = sem("st_ready")
        sxt_ready = sem("sxt_ready")
        gu_ready = sem("gu_ready")
        gexp_ready = sem("gexp_ready")
        hid_t_ready = sem("hid_t_ready")
        dn_ready = sem("dn_ready")
        goal_ready = sem("goal_ready")
        erow_ready = sem("erow_ready")
        erow_sent = [sem(f"erow_sent{n}") for n in range(EB)]
        yk_loaded = [sem(f"yk_loaded{n}") for n in range(FB)]
        zf_loaded = [sem(f"zf_loaded{n}") for n in range(FB)]
        fvar_ready = sem("fvar_ready")
        frs_ready = sem("frs_ready")
        nmr_ready = sem("nmr_ready")
        half_ready = sem("half_ready")
        fout_ready = sem("fout_ready")
        fin_own = sem("fin_own")
        out_stored = [sem(f"out_stored{n}") for n in range(FB)]

        block = ctx.enter_context(nc.Block())

        def score_cols(n):
            few = blocks(n // H) <= 4
            start = 512 * (n // 2 % 2) if few else 0
            return slice(start, start + blocks(n // H) * P)

        def scores_used(n):
            few = blocks(n // H) <= 4 and (n < 2 or blocks((n - 2) // H) <= 4)
            return n - 3 if few else n - 1

        def at(b, per, n):
            return b * per + n

        w_raw = probs[:, :, :, :].rearrange("p s h t -> p (s h t)")[:, 0:6 * H * MC * D].rearrange(
            "p (n x) -> p n x", n=6)
        w_hi_f = w_hi[:, :, :, :, :].rearrange("p n h c d -> p n (h c d)")
        w_lo_f = w_lo[:, :, :, :, :].rearrange("p n h c d -> p n (h c d)")
        raw_r = ot[:, 0, :].rearrange("p (c n) -> p c n", c=MC)
        raw_d = ot[0:F, 1, 0:M]

        PASSES = ((0, 0), (0, 1), (1, 0))

        def read(eng, step):
            r, turn = PLACE[step]
            eng.wait_ge(ring_read[r], turn + 1)

        def reader(ins, step):
            ins.then_inc(ring_read[PLACE[step][0]], 1)

        def bank(step):
            return ring[:, PLACE[step][0], :]

        def wide(ap, n):
            return ap.rearrange("p (a x) -> p a x", a=1).to_broadcast([P, n, ap.shape[1]])

        def used(eng, semaphore, n):
            if not (isinstance(n, int) and n <= 0):
                eng.wait_ge(semaphore, n)

        @block.sync
        def _(sp):
            def load_x(i):
                sp.dma_start(x_sb[:, i % XB, :], xf[i * P:(i + 1) * P, :]).then_inc(x_loaded[i % XB], 16)

            load_x(0)
            for name in BLOCKS_IN_TURN:
                n = BLOCKS.index(name)
                src = {"K": w_ak, "V": w_av}.get(name)
                src = w_aq[name] if src is None else src
                sp.dma_start(w_raw[:, n, :].rearrange("p (h y) -> p h y", h=H),
                             src.rearrange("h (p c) d -> p h (c d)", c=MC)).then_inc(w_loaded[n], 16)
                if n == 0:
                    sp.dma_start(cos_sb[:, :, :], rope_cos.rearrange("(n p) d -> p n d", p=P)
                                 ).then_inc(table_loaded, 16)
                    sp.dma_start(sin_sb[:, :, :], rope_sin.rearrange("(n p) d -> p n d", p=P)
                                 ).then_inc(table_loaded, 16)
            sp.dma_start(raw_r[:, :, 0:E], gate_w.rearrange("(p c) e -> p c e", c=MC)).then_inc(wr_loaded, 16)
            sp.dma_start(raw_r[:, :, E:E + F], ws_gate.rearrange("(p c) e -> p c e", c=MC)).then_inc(wr_loaded, 16)
            sp.dma_start(raw_r[:, :, E + F:], ws_up.rearrange("(p c) e -> p c e", c=MC)).then_inc(wr_loaded, 16)
            sp.dma_start(raw_d, ws_down).then_inc(wsd_loaded, 16)
            sp.dma_start(bias_sb[:, :], bias.rearrange("(a e) -> a e", a=1).to_broadcast([P, E])
                         ).then_inc(bias_loaded, 16)
            load_x(1)
            sp.dma_start(wo[:, :, :], w_ao.rearrange("g h d m -> d (g h) m")).then_inc(wo_loaded, 16)
            sp.wait_ge(const_ready, 1)
            sp.dma_start(slot_rows.rearrange("(p n) r -> p n r", p=P),
                         blank[:, :].rearrange("p (a r) -> p a r", a=1).to_broadcast([P, E * HALF // P, ROW])
                         ).then_inc(blank_stored, 16)

            def load_pair(n, k):
                for a, w in enumerate((w_gate, w_up)):
                    sp.dma_start(wgu[:, k, :, a, :, :].rearrange("p e c f -> p e (c f)"),
                                 w[bass.ds(2 * n, 2), :, :].rearrange("e (p c) f -> p e (c f)", c=MC)
                                 ).then_inc(experts_loaded[k], 16)
                sp.dma_start(wdn[:, k, :, :], w_down[bass.ds(2 * n, 2), :, :].rearrange("e f m -> f e m")
                             ).then_inc(experts_loaded[k], 16)

            def blank_experts(i):
                sp.dma_start(expert_rows[i * P * K:(i + 1) * P * K, :].rearrange("(p n) m -> p n m", p=P),
                             blank[:, 0:M].rearrange("p (a r) -> p a r", a=1).to_broadcast([P, K, M])
                             ).then_inc(experts_blank, 16)

            for s in SEQ:
                if s[0] == "xt" and 1 <= s[1] < TILES - 1:
                    i = s[1] + 1
                    if i >= XB:
                        sp.wait_ge(var_ready, i - XB + 1)
                    load_x(i)
                if s[0] == "proj" and s[2] == 3:
                    sp.wait_ge(proj_ready, PROJ_AT[s[1:]] + 1)
                    blank_experts(s[1])
                if s == ("proj", TILES - 1, 3):
                    sp.wait_ge(proj_ready, len(PROJ_AT))
                    for k in range(WB):
                        load_pair(k, k)
                if s[0] == "sd":
                    i = s[1]
                    read(sp, s)
                    sp.dma_start(z_rows[i * P:(i + 1) * P, :], z_sb[:, :]).then_inc(z_stored, 16)
            sp.wait_ge(z_stored, 16 * TILES)

            def load_slots(n, k):
                sp.dma_start(srow[:, k, :], slot_rows[bass.ds(n * P, P), :]).then_inc(srow_loaded[k], 16)

            sp.wait_ge(attention_left, 1)
            for n in range(2):
                sp.wait_ge(scattered[n], 8 * K * TILES)
            for k in range(WB):
                load_slots(k, k)
            with sp.Fori(1, PAIRS // WB) as r:
                for k in range(WB):
                    sp.wait_ge(dn_ready, at(r, WB, k + 1 - WB))
                    load_slots(r * WB + k, k)
                    load_pair(r * WB + k, k)
            for n in range(EB):
                sp.wait_ge(erow_sent[n], 16 * (PAIRS // EB))

            def sums(t, k):
                used(sp, fvar_ready, t - FB + 1)
                sp.dma_start(yk[:, k, :, :], expert_rows[bass.ds(t * P * K, P * K), :].rearrange(
                    "(p k) m -> p k m", k=K)).then_inc(yk_loaded[k], 16)
                sp.dma_start(zf[:, k, :], z_rows[bass.ds(t * P, P), :]).then_inc(zf_loaded[k], 16)

            def store(t, k):
                sp.wait_ge(fout_ready, t + 1)
                sp.dma_start(of[bass.ds(t * P, P), :], fout[:, k, :]).then_inc(out_stored[k], 16)

            for k in range(FB):
                sums(k, k)
            with sp.Fori(1, TILES // FB) as r:
                for k in range(FB):
                    sums(r * FB + k, k)
                    store(r * FB + k - FB, k)
            for k in range(FB):
                store(TILES - FB + k, k)
            for k in range(FB):
                sp.wait_ge(out_stored[k], 16 * (TILES // FB))

        @block.gpsimd
        def _(pool):
            own = [0]

            def link(ins):
                own[0] += 1
                ins.then_inc(pool_own, 1)
                pool.wait_ge(pool_own, own[0])

            link(pool.memset(ident[:, :], 0.0))
            link(pool.affine_select(out=ident[:, :], in_=ident[:, :], compare_op=ALU.not_equal, fill=1.0, base=0,
                                    pattern=[[-1, P]], channel_multiplier=1))
            pool.memset(pool_cell[:, :], 0.0).then_inc(ident_ready, 1)
            link(pool.memset(blank[:, :], 0.0))
            pool.memset(blank[:, S_AT:S_AT + K], -1.0).then_inc(const_ready, 1)
            link(pool.tensor_copy(ident_bf[:, :], ident[:, :]))
            link(pool.memset(causal_bf[:, :], 0.0))
            link(pool.affine_select(out=causal_bf[:, :], in_=causal_bf[:, :], compare_op=ALU.is_ge, fill=NEG, base=0,
                                    pattern=[[-1, P]], channel_multiplier=1))
            link(pool.memset(before_bf[:, :], 0.0))
            link(pool.affine_select(out=before_bf[:, :], in_=before_bf[:, :], compare_op=ALU.is_ge, fill=1.0, base=0,
                                    pattern=[[-1, P]], channel_multiplier=1))
            link(pool.memset(ones_bf[:, :], 1.0))
            link(pool.memset(minus_half[:, :], -0.5))
            link(pool.memset(taken[:, :], 0.0))
            link(pool.memset(row[:, :, :], 0.0))
            link(pool.iota(iota_e[:, :], pattern=[[1, E]], base=0, channel_multiplier=0,
                           allow_small_or_imprecise_dtypes=True))
            link(pool.iota(choice_far[:, :], pattern=[[1, K]], base=-int(FAR), channel_multiplier=0,
                           allow_small_or_imprecise_dtypes=True))
            pool.iota(token[:, :], pattern=[[0, 1]], base=-P, channel_multiplier=1,
                      allow_small_or_imprecise_dtypes=True).then_inc(const_ready, 1)
            def stand(n):
                used(pool, stood, n)
                pool.tensor_tensor(pool_cell[:, 0:1], minus_half[:, :], minus_half[:, :], ALU.mult).then_inc(stood, 1)

            for s in SEQ:
                if s[0] == "proj" and s[2] != "V":
                    n = ROPE_AT[s[1:]]
                    read(pool, s)
                    if n >= 1:
                        pool.wait_ge(qkt_ready, n)
                    if by_pool(s):
                        i = s[1] % NT
                        raw = q_cos[:, :, :, :].rearrange("p h a d -> p (h a) d")
                        link(pool.tensor_tensor(q_sin[:, :, :, :].rearrange("p h a d -> p (h a) d"), raw,
                                                wide(sin_sb[:, i, :], 2 * H), ALU.mult))
                        link(pool.tensor_tensor(raw, raw, wide(cos_sb[:, i, :], 2 * H), ALU.mult))
                    pool.tensor_tensor(q_rot[:, :, 0, :], q_cos[:, :, 0, :], q_sin[:, :, 1, :], ALU.subtract)
                    pool.tensor_tensor(q_rot[:, :, 1, :], q_cos[:, :, 1, :], q_sin[:, :, 0, :], ALU.add
                                       ).then_inc(rot_ready, 1)
                if s[0] == "outproj":
                    pool.wait_ge(var_ready, s[1] + 1)
                    pool.tensor_tensor(rstd[:, :], var_eps[:, :], minus_half[:, :], ALU.pow).then_inc(rstd_ready, 1)
                if s[0] == "place":
                    i = s[1]
                    if i == 0:
                        pool.wait_ge(blank_stored, 16)
                    pool.wait_ge(placed, i + 1)
                    for k in range(K):
                        pool.indirect_dma_start(
                            slot_rows[:, :], bass.IndirectOffsetOnAxis(ap=slot_u[:, i % 2, k:k + 1], axis=0),
                            row[:, i % 2, :], None, bounds_check=E * HALF - 1, oob_is_err=False
                        ).then_inc(scattered[i % 2], 16)

            def send(n, k):
                pool.wait_ge(goal_ready, n + 1)
                pool.wait_ge(erow_ready, n + 1)
                stand(n)
                pool.indirect_dma_start(
                    expert_rows[:, :], bass.IndirectOffsetOnAxis(ap=goal_u[:, k % EB:k % EB + 1], axis=0),
                    erow[:, k % EB, :], None, bounds_check=TOKENS * K - 1, oob_is_err=False
                ).then_inc(erow_sent[k % EB], 16)

            pool.wait_ge(attention_left, 1)
            pool.iota(slot_now[:, :], pattern=[[0, 1]], base=-P, channel_multiplier=1,
                      allow_small_or_imprecise_dtypes=True).then_inc(slot_now_ready, 1)
            pool.wait_ge(experts_blank, 16 * TILES)
            with pool.Fori(0, PAIRS // WB) as r:
                for k in range(WB):
                    send(r * WB + k, k)

            def half(r, k):
                pool.wait_ge(yk_loaded[k], at(r, 16, 16))
                pool.tensor_tensor(yk[:, k, 0:3, :], yk[:, k, 0:3, :], yk[:, k, 3:6, :], ALU.add
                                   ).then_inc(half_ready, 1)

            def deviation(r, k):
                pool.wait_ge(fvar_ready, at(r, FB, k + 1))
                pool.tensor_tensor(frs[:, k, :], fve[:, k, :], minus_half[:, :], ALU.pow).then_inc(frs_ready, 1)

            with pool.Fori(0, TILES // FB) as r:
                for k in range(FB):
                    half(r, k)
                    if k:
                        deviation(r, k - 1)
                deviation(r, FB - 1)

        @block.scalar
        def _(act):
            def split(hi, raw):
                return act.activation(hi, raw, ACT.Copy)

            for s in SEQ:
                for name in SPLIT_AT.get(s, []):
                    n = BLOCKS.index(name)
                    act.wait_ge(w_loaded[n], 16)
                    split(w_hi_f[:, n, :], w_raw[:, n, :]).then_inc(whi_ready[n], 1)
                if s == ("score", 0, 0):
                    act.wait_ge(wr_loaded, 48)
                    split(wr_hi[:, :, :], raw_r).then_inc(wmisc_hi_ready, 1)
                    act.wait_ge(wsd_loaded, 16)
                    split(wsd_hi[:, :], raw_d).then_inc(wmisc_hi_ready, 1)
                kind = s[0]
                if kind == "xt":
                    act.wait_ge(xt_ready, s[1] + 1)
                    if s[1] >= 1:
                        act.wait_ge(proj_ready, 6 * s[1])
                    split(xt_hi[:, :, :], bank(s)[:, 0:MC * P].rearrange("p (c t) -> p c t", c=MC)
                          ).then_inc(xt_hi_ready, 1)
                if kind == "proj" and s[2] == "V":
                    act.wait_ge(proj_ready, PROJ_AT[s[1:]] + 1)
                    if s[1] == NT:
                        act.wait_ge(pv_done, PT_ALL // B)
                    reader(act.activation(v_sb[:, s[1] % NT, :], bank(s), ACT.Copy), s)
                if kind == "proj" and s[2] != "V" and by_pool(s):
                    n = ROPE_AT[s[1:]]
                    act.wait_ge(proj_ready, PROJ_AT[s[1:]] + 1)
                    if n >= 1:
                        act.wait_ge(rot_ready, n)
                    reader(act.activation(q_cos[:, :, :, :].rearrange("p h a d -> p (h a d)"), bank(s), ACT.Copy), s)
                if kind == "qkt":
                    i, name = s[1:]
                    act.wait_ge(qkt_ready, QKT_AT[s[1:]] + 1)
                    if name == "K":
                        if i == NT:
                            act.wait_ge(scores_ready, HEADS // B)
                        c = i % NT * P
                        dst, src = kt_hi[:, :, c:c + P], bank(s).rearrange("p (g t) -> p g t", g=G)
                    else:
                        u = i * G + name
                        dst, src = qt_hi[:, u % 2, :], bank(s)
                        if u >= 2:
                            act.wait_ge(scores_ready, H * (u - 1))
                    split(dst, src).then_inc(qk_hi_ready, 1)
                if kind == "exp":
                    u, h = s[1:]
                    n = u * H + h
                    act.wait_ge(max_ready, n + 1)
                    if u < 2:
                        for m in range(6):
                            act.wait_ge(wlo_ready[m], 1)
                    else:
                        act.wait_ge(ptrans_ready, PT_AT[(u - 2, blocks(u - 2) - 1)] + 1)
                        if not scaled_first(u - 2):
                            act.wait_ge(inv_ready, INV_AT[u - 2] + 1)
                    act.activation(probs[:, u % 2, h, 0:blocks(u) * P], s_ps[:, n % 2, score_cols(n)], ACT.Exp,
                                   bias=neg_max[:, n % 8:n % 8 + 1],
                                   accum_out=row_sum[:, u % 2, h:h + 1]).then_inc(probs_ready, 1)
                if kind == "ptrans":
                    n = PT_AT[s[1:]]
                    act.wait_ge(ptrans_ready, n + 1)
                    if n >= PTB:
                        act.wait_ge(pv_done, n - PTB + 1)
                    reader(act.activation(pt[:, n % PTB, :], bank(s), ACT.Copy), s)
                if kind == "linv":
                    u = s[1]
                    act.wait_ge(linv_ready, INV_AT[u] + 1)
                    if u >= 1:
                        act.wait_ge(o_ready, u)
                    reader(act.activation(inv_row[:, :], bank(s), ACT.Copy), s)
                if kind == "x1t":
                    act.wait_ge(x1t_ready, s[1] + 1)
                    if s[1] >= 1:
                        act.wait_ge(rtr_ready, s[1])
                    split(x1t_hi[:, :, :], bank(s)[:, 0:MC * P].rearrange("p (c t) -> p c t", c=MC)
                          ).then_inc(x1t_hi_ready, 1)
                if kind == "rtr":
                    act.wait_ge(rtr_ready, s[1] + 1)
                    if s[1] >= 1:
                        act.wait_ge(picked, s[1])
                    act.activation(sig[:, :], bank(s)[:, 0:E + F], ACT.Exp, scale=-1.0).then_inc(exp_ready, 1)
                if kind == "ht":
                    act.wait_ge(ht_ready, s[1] + 1)
                    if s[1] >= 1:
                        act.wait_ge(sd_ready, s[1])
                    split(ht_hi[:, :], bank(s)[0:F, 0:P]).then_inc(ht_hi_ready, 1)

            act.wait_ge(attention_left, 1)

            def slots_in(n, k):
                act.wait_ge(st_ready, n + 1)
                used(act, gu_ready, n - 1)
                act.activation(sxt[:, k % 2, :, :], s_ps[:, k % 2, 0:MC * P].rearrange("p (c s) -> p c s", c=MC),
                               ACT.Copy).then_inc(sxt_ready, 1)

            def gate_exp(n, k):
                act.wait_ge(gu_ready, n + 1)
                used(act, hid_e_ready, n)
                act.activation(gexp[:, :], s_ps[:, k % 2, 512:512 + F], ACT.Exp, scale=-1.0
                               ).then_inc(gexp_ready, 1)

            def hidden_in(r, k):
                n, k = at(r, WB, k), k % WB
                act.wait_ge(htr_ready, n + 1)
                used(act, dn_ready, n - 1)
                act.activation(hid_t[:, k % 2, :], ring[0:F, 2, 0:P], ACT.Copy).then_inc(hid_t_ready, 1)

            def rows_out(r, k):
                n, r, k = at(r, WB, k), r + k // WB, k % WB
                act.wait_ge(dn_ready, n + 1)
                used(act, erow_sent[k % EB], at(r, 16 * WB // EB, 16 * (k // EB)))
                act.activation(erow[:, k % EB, :], ring[:, k % 2, 0:M], ACT.Copy, scale=slot_w[:, k:k + 1]
                               ).then_inc(erow_ready, 1)

            def expert_round(r, last=False):
                for k in range(WB):
                    n = at(r, WB, k)
                    if not (last and k == WB - 1):
                        slots_in(n + 1, k + 1)
                    gate_exp(n, k)
                    if k >= 2 or not isinstance(r, int) or r > 0:
                        rows_out(r, k - 2)
                    if k >= 1 or not isinstance(r, int) or r > 0:
                        hidden_in(r, k - 1)

            slots_in(0, 0)
            expert_round(0)
            with act.Fori(1, ROUNDS - 1) as r:
                expert_round(r)
            expert_round(ROUNDS - 1, last=True)
            rows_out(ROUNDS - 1, WB - 2)
            hidden_in(ROUNDS - 1, WB - 1)
            rows_out(ROUNDS - 1, WB - 1)

            def scale(r, k):
                n = at(r, FB, k)
                act.wait_ge(nmr_ready, n + 1)
                used(act, out_stored[k], at(r, 16, 0))
                act.activation(fout[:, k, :], ysum[:, k, :], ACT.Identity, bias=nmr[:, k, :], scale=frs[:, k, :]
                               ).then_inc(fout_ready, 1)

            for k in range(FB):
                scale(0, k)
            with act.Fori(1, TILES // FB) as r:
                for k in range(FB):
                    scale(r, k)

        @block.tensor
        def _(pe):
            def begin(step):
                r, turn = PLACE[step]
                if turn >= 1:
                    pe.wait_ge(ring_read[r], turn)

            pe.wait_ge(ident_ready, 1)
            for s in SEQ:
                kind = s[0]
                if s == ("score", 0, 0):
                    pe.wait_ge(const_ready, 2)
                if kind in RINGED:
                    begin(s)
                if kind == "xt":
                    i = s[1]
                    pe.wait_ge(x_loaded[i % XB], 16 * (i // XB + 1))
                    xc = x_sb[:, i % XB, :].rearrange("t (p c) -> t c p", c=MC)
                    for c in range(MC):
                        ins = pe.transpose(bank(s)[:, c * P:(c + 1) * P], xc[:, c, :], ident[:, :])
                    ins.then_inc(xt_ready, 1)
                if kind == "proj":
                    i, name = s[1:]
                    n = BLOCKS.index(name)
                    read(pe, ("xt", i))
                    pe.wait_ge(wlo_ready[n], 1)
                    for c in range(MC):
                        for xp, wp in PASSES:
                            ins = pe.matmul(bank(s), (xt_hi, xt_lo)[xp][:, c, :], (w_hi, w_lo)[wp][:, n, :, c, :],
                                            start=(c == 0 and xp == wp == 0), stop=(c == MC - 1 and xp == 1))
                    ins.then_inc(proj_ready, 1)
                if kind == "qkt":
                    pe.wait_ge(rot_ready, QKT_AT[s[1:]] + 1)
                    for h in range(H):
                        ins = pe.transpose(bank(s)[:, h * P:(h + 1) * P],
                                           q_rot[:, h, :, :].rearrange("p a d -> p (a d)"), ident[:, :])
                    ins.then_inc(qkt_ready, 1)
                if kind == "score":
                    u, h = s[1:]
                    (i, g), n = divmod(u, G), u * H + h
                    read(pe, ("qkt", i, g))
                    if h == 0:
                        read(pe, ("qkt", i, "K"))
                    heads_done = scores_used(n)
                    if heads_done > 0:
                        pe.wait_ge(probs_ready, heads_done)
                    q = [z[:, u % 2, h * P:(h + 1) * P] for z in (qt_hi, qt_lo)]
                    k = [z[:, g, :] for z in (kt_hi, kt_lo)]
                    width, c = blocks(u) * P, score_cols(n).start
                    for a in range(0, width, 512):
                        e = min(a + 512, width)
                        last = e == width
                        for qp, kp in PASSES:
                            pe.matmul(s_ps[:, n % 2, c + a:c + e], q[qp], k[kp][:, a:e],
                                      start=(qp == kp == 0), stop=(qp == 1 and not last))
                        if last:
                            ins = pe.matmul(s_ps[:, n % 2, c + e - P:c + e], ident_bf[:, :], causal_bf[:, :],
                                            start=False, stop=True)
                    ins.then_inc(scores_ready, 1)
                if kind == "ptrans":
                    u, j = s[1:]
                    if scaled_first(u):
                        pe.wait_ge(scaled_ready, SCALED_AT[H * u + H - 1] + 1)
                    else:
                        pe.wait_ge(probs_ready, H * (u + 1))
                    for h in range(H):
                        ins = pe.transpose(bank(s)[:, h * P:(h + 1) * P], probs[:, u % 2, h, j * P:(j + 1) * P],
                                           ident[:, :])
                    ins.then_inc(ptrans_ready, 1)
                if kind == "pv":
                    u, j = s[1:]
                    (i, g), n = divmod(u, G), PT_AT[s[1:]]
                    read(pe, ("ptrans", u, j))
                    if g == 0 and j == blocks(u) - 1:
                        read(pe, ("proj", i, "V"))
                    if j == 0 and u >= 1:
                        pe.wait_ge(o_ready, u)
                    pe.matmul(o_ps[:, :], v_sb[:, j, g * D:(g + 1) * D], pt[:, n % PTB, :],
                              start=(j == 0), stop=(j == blocks(u) - 1)).then_inc(pv_done, 1)
                if kind == "linv":
                    u = s[1]
                    pe.wait_ge(inv_ready, INV_AT[u] + 1)
                    for h in range(H):
                        ins = pe.transpose(bank(s)[:, h * P:(h + 1) * P],
                                           inv_sum[:, u % 2, h:h + 1].to_broadcast([P, P]), ident[:, :])
                    ins.then_inc(linv_ready, 1)
                if kind == "outproj":
                    i = s[1]
                    pe.wait_ge(wo_loaded, 16)
                    pe.wait_ge(o_ready, G * (i + 1))
                    for h in range(G * H):
                        ins = pe.matmul(bank(s)[:, 0:M], ot[:, h // H, (h % H) * P:(h % H + 1) * P], wo[:, h, :],
                                        start=(h == 0), stop=(h == G * H - 1))
                    ins.then_inc(attn_ready, 1)
                if kind == "x1t":
                    i = s[1]
                    pe.wait_ge(x1_ready, i + 1)
                    xc = row[:, i % 2, 0:M].rearrange("t (p c) -> t c p", c=MC)
                    for c in range(MC):
                        ins = pe.transpose(bank(s)[:, c * P:(c + 1) * P], xc[:, c, :], ident[:, :])
                    ins.then_inc(x1t_ready, 1)
                if kind == "rtr":
                    read(pe, ("x1t", s[1]))
                    pe.wait_ge(wmisc_lo_ready, 2)
                    for c in range(MC):
                        for xp, wp in PASSES:
                            ins = pe.matmul(bank(s)[:, 0:E + 2 * F], (x1t_hi, x1t_lo)[xp][:, c, :],
                                            (wr_hi, wr_lo)[wp][:, c, :],
                                            start=(c == 0 and xp == wp == 0), stop=(c == MC - 1 and xp == 1))
                    ins.then_inc(rtr_ready, 1)
                if kind == "ht":
                    read(pe, ("rtr", s[1]))
                    pe.transpose(bank(s)[0:F, 0:P], hid[:, :], ident[:, :]).then_inc(ht_ready, 1)
                if kind == "count":
                    pe.wait_ge(chose_ready, s[1] + 1)
                    pe.matmul(bank(s)[:, 0:E], before_bf[:, :], chose[:, :], start=True, stop=False)
                    pe.matmul(bank(s)[:, 0:E], ones_bf[:, :], taken[:, :], start=False, stop=True
                              ).then_inc(count_ready, 1)
                if kind == "sd":
                    read(pe, ("ht", s[1]))
                    for n, (hp, wp) in enumerate(PASSES):
                        ins = pe.matmul(bank(s)[:, 0:M], (ht_hi, ht_lo)[hp][:, :], (wsd_hi, wsd_lo)[wp][:, :],
                                        start=(n == 0), stop=(n == 2))
                    ins.then_inc(sd_ready, 1)

            pe.wait_ge(attention_left, 1)

            def slots_t(r, k):
                n, r, k = at(r, WB, k), r + k // WB, k % WB
                pe.wait_ge(srow_loaded[k], at(r, 16, 16))
                used(pe, sxt_ready, n - 1)
                xc = srow[:, k, 0:M].rearrange("t (p c) -> t c p", c=MC)
                for c in range(MC):
                    ins = pe.transpose(s_ps[:, k % 2, c * P:(c + 1) * P], xc[:, c, :], ident[:, :])
                ins.then_inc(st_ready, 1)

            def gate_up(r, k):
                n = at(r, WB, k)
                pe.wait_ge(experts_loaded[k], at(r, 48, 48))
                pe.wait_ge(sxt_ready, n + 1)
                used(pe, hid_e_ready, n - 1)
                for e in range(2):
                    half = slice(e * HALF, (e + 1) * HALF)
                    for c in range(MC):
                        ins = pe.matmul(s_ps[half, k % 2, 512:512 + 2 * F], sxt[:, k % 2, c, half],
                                        wgu[:, k, e, :, c, :], start=(c == 0), stop=(c == MC - 1))
                ins.then_inc(gu_ready, 1)

            def hidden_t(r, k):
                n, k = at(r, WB, k), k % WB
                pe.wait_ge(hid_e_ready, n + 1)
                used(pe, hid_t_ready, n)
                pe.transpose(ring[0:F, 2, 0:P], hid_e[:, k % 2, :], ident[:, :]).then_inc(htr_ready, 1)

            def down(r, k):
                n, k = at(r, WB, k), k % WB
                pe.wait_ge(hid_t_ready, n + 1)
                used(pe, erow_ready, n - 1)
                for e in range(2):
                    half = slice(e * HALF, (e + 1) * HALF)
                    ins = pe.matmul(ring[half, k % 2, 0:M], hid_t[:, k % 2, half], wdn[:, k, e, :],
                                    start=True, stop=True)
                ins.then_inc(dn_ready, 1)

            def expert_round(r, last=False):
                for k in range(WB):
                    if not (last and k == WB - 1):
                        slots_t(r, k + 1)
                    gate_up(r, k)
                    if k >= 2 or not isinstance(r, int) or r > 0:
                        down(r, k - 2)
                    if k >= 1 or not isinstance(r, int) or r > 0:
                        hidden_t(r, k - 1)

            slots_t(0, 0)
            expert_round(0)
            with pe.Fori(1, ROUNDS - 1) as r:
                expert_round(r)
            expert_round(ROUNDS - 1, last=True)
            down(ROUNDS - 1, WB - 2)
            hidden_t(ROUNDS - 1, WB - 1)
            down(ROUNDS - 1, WB - 1)

        @block.vector
        def _(dve):
            def low(lo, raw, hi):
                return dve.tensor_tensor(lo, raw, hi.bitcast(F32), ALU.subtract)

            links = [0]

            def later(ins):
                links[0] += 1
                ins.then_inc(dve_own, 1)

            def settled():
                dve.wait_ge(dve_own, links[0])

            def after(ins):
                later(ins)
                settled()

            def hold(n):
                dve.tensor_copy(held[0:1, n:n + 1], minus_half[0:1, :])

            def each(ap, n):
                return ap.rearrange("p (x a) -> p x a", a=1).to_broadcast([P, ap.shape[1], n])

            dve.wait_ge(const_ready, 2)
            for s in SEQ:
                for name in SPLIT_AT.get(s, []):
                    n = BLOCKS.index(name)
                    dve.wait_ge(whi_ready[n], 1)
                    low(w_lo_f[:, n, :], w_raw[:, n, :], w_hi_f[:, n, :]).then_inc(wlo_ready[n], 1)
                if s == ("score", 0, 0):
                    dve.wait_ge(wmisc_hi_ready, 2)
                    low(wr_lo[:, :, :], raw_r, wr_hi[:, :, :]).then_inc(wmisc_lo_ready, 1)
                    low(wsd_lo[:, :], raw_d, wsd_hi[:, :]).then_inc(wmisc_lo_ready, 1)
                    dve.wait_ge(wmisc_lo_ready, 2)
                kind = s[0]
                if kind == "xt":
                    dve.wait_ge(xt_hi_ready, s[1] + 1)
                    reader(low(xt_lo[:, :, :], bank(s)[:, 0:MC * P].rearrange("p (c t) -> p c t", c=MC),
                               xt_hi[:, :, :]), s)
                if kind == "proj" and s[2] != "V" and not by_pool(s):
                    i, n = s[1], ROPE_AT[s[1:]]
                    dve.wait_ge(proj_ready, PROJ_AT[s[1:]] + 1)
                    if n >= 1:
                        dve.wait_ge(rot_ready, n)
                    if n == 0:
                        dve.wait_ge(table_loaded, 32)
                    src = bank(s).rearrange("p (x d) -> p x d", d=D // 2)
                    dve.tensor_tensor(q_cos[:, :, :, :].rearrange("p h a d -> p (h a) d"), src,
                                      wide(cos_sb[:, i % NT, :], 2 * H), ALU.mult)
                    reader(dve.tensor_tensor(q_sin[:, :, :, :].rearrange("p h a d -> p (h a) d"), src,
                                             wide(sin_sb[:, i % NT, :], 2 * H), ALU.mult), s)
                if kind == "qkt":
                    i, name = s[1:]
                    dve.wait_ge(qk_hi_ready, QKT_AT[s[1:]] + 1)
                    if name == "K":
                        kt_cols = slice(i % NT * P, (i % NT + 1) * P)
                        reader(low(kt_lo[:, :, kt_cols], bank(s).rearrange("p (g t) -> p g t", g=G),
                                   kt_hi[:, :, kt_cols]), s)
                    else:
                        u = i * G + name
                        reader(low(qt_lo[:, u % 2, :], bank(s), qt_hi[:, u % 2, :]), s)
                if kind == "score":
                    u, h = s[1:]
                    n = u * H + h
                    dve.wait_ge(scores_ready, n + 1)
                    dve.tensor_reduce(neg_max[:, n % 8:n % 8 + 1], s_ps[:, n % 2, score_cols(n)], AX_X, ALU.max,
                                      negate=True).then_inc(max_ready, 1)
                if kind == "scale":
                    u, h = divmod(s[1], H)
                    dve.wait_ge(probs_ready, s[1] + 1)
                    if not scaled_first(u - 2):
                        dve.wait_ge(linv_ready, INV_AT[u - 2] + 1)
                    p = probs[:, u % 2, h, 0:blocks(u) * P]
                    after(dve.reciprocal(inv_sum[:, u % 2, h:h + 1], row_sum[:, u % 2, h:h + 1]))
                    dve.tensor_scalar(p, p, inv_sum[:, u % 2, h:h + 1], None, ALU.mult).then_inc(scaled_ready, 1)
                if kind == "ptrans" and s[2] == 0 and not scaled_first(s[1]):
                    u = s[1]
                    dve.wait_ge(probs_ready, H * (u + 1))
                    if u >= 2:
                        dve.wait_ge(linv_ready, INV_AT[max(v for v in INV_AT if v <= u - 2)] + 1)
                    dve.reciprocal(inv_sum[:, u % 2, :], row_sum[:, u % 2, :]).then_inc(inv_ready, 1)
                if kind == "omul":
                    u = s[1]
                    i, g = divmod(u, G)
                    if not scaled_first(u):
                        read(dve, ("linv", u))
                    dve.wait_ge(pv_done, PT_AT[(u, blocks(u) - 1)] + 1)
                    if i >= 1:
                        dve.wait_ge(attn_ready, i)
                    if scaled_first(u):
                        dve.tensor_copy(ot[:, g, :], o_ps[:, :]).then_inc(o_ready, 1)
                    else:
                        dve.tensor_tensor(ot[:, g, :], o_ps[:, :], inv_row[:, :], ALU.mult).then_inc(o_ready, 1)
                if kind == "outproj":
                    i = s[1]
                    dve.wait_ge(attn_ready, i + 1)
                    reader(dve.tensor_tensor(y_sb[:, :], bank(s)[:, 0:M], x_sb[:, i % XB, :], ALU.add), s)
                    read(dve, s)
                    after(dve.bn_stats(stats[:, :], y_sb[:, :]))
                    after(dve.bn_aggr(mean_var[:, :], stats[:, :]))
                    dve.tensor_scalar(var_eps[:, :], mean_var[:, 1:2], EPS, None, ALU.add).then_inc(var_ready, 1)
                if kind == "norm":
                    i = s[1]
                    dve.wait_ge(rstd_ready, i + 1)
                    if i >= 2:
                        dve.wait_ge(scattered[i % 2], 16 * K * (i // 2))
                    dve.tensor_scalar(row[:, i % 2, 0:M], y_sb[:, :], mean_var[:, 0:1], rstd[:, 0:1],
                                      ALU.subtract, ALU.mult).then_inc(x1_ready, 1)
                    after(dve.tensor_scalar(token[:, :], token[:, :], float(P), None, ALU.add))
                    dve.tensor_copy(row[:, i % 2, T_AT:T_AT + 1], token[:, :])
                if kind == "x1t":
                    dve.wait_ge(x1t_hi_ready, s[1] + 1)
                    reader(low(x1t_lo[:, :, :], bank(s)[:, 0:MC * P].rearrange("p (c t) -> p c t", c=MC),
                               x1t_hi[:, :, :]), s)
                if kind == "rtr":
                    dve.wait_ge(exp_ready, s[1] + 1)
                    if s[1] >= 1:
                        dve.wait_ge(ht_ready, s[1])
                    after(dve.tensor_scalar(sig[:, :], sig[:, :], 1.0, None, ALU.add))
                    after(dve.reciprocal(sig[:, :], sig[:, :]))
                    after(dve.tensor_tensor(hid[:, :], bank(s)[:, E:E + F], sig[:, E:], ALU.mult))
                    reader(dve.tensor_tensor(hid[:, :], bank(s)[:, E + F:E + 2 * F], hid[:, :], ALU.mult), s)
                if kind == "pick":
                    i, part = s[1:]
                    settled()
                if kind == "pick" and part == 0:
                    if i == 0:
                        dve.wait_ge(bias_loaded, 16)
                    after(dve.tensor_tensor(biased[:, :], sig[:, 0:E], bias_sb[:, :], ALU.add))
                    for n in range(EG - 1):
                        dve.max(top2[:, n, :], biased[:, n * 8:(n + 1) * 8])
                    later(dve.max(top2[:, EG - 1, :], biased[:, E - 8:]))
                if kind == "pick" and part == 1:
                    after(dve.tensor_tensor(group[:, :], top2[:, :, 0], top2[:, :, 1], ALU.add))
                    later(dve.max(group_top[:, :], group[:, :]))
                if kind == "pick" and part == 2:
                    after(dve.max_index(group_at[:, :], group_top[:, :], group[:, :]))
                    later(dve.tensor_copy(group_atf[:, :], group_at[:, :]))
                if kind == "pick" and part == 3:
                    after(dve.tensor_tensor(kept4[:, :, :], each(iota_e[:, 0:EG], KG),
                                            wide(group_atf[:, 0:KG], EG), ALU.is_equal))
                    later(dve.tensor_reduce(kept[:, :], kept4[:, :, :], AX_X, ALU.add))
                if kind == "pick" and part == 4:
                    dve.tensor_tensor(open_[:, :].rearrange("p (g e) -> p g e", g=EG),
                                      biased[:, :].rearrange("p (g e) -> p g e", g=EG),
                                      each(kept[:, :], E // EG), ALU.mult)
                    after(dve.tensor_scalar(barred[:, :], kept[:, :], 1.0, -NEG, ALU.subtract, ALU.mult))
                    later(dve.tensor_tensor(open_[:, :].rearrange("p (g e) -> p g e", g=EG),
                                            open_[:, :].rearrange("p (g e) -> p g e", g=EG),
                                            each(barred[:, :], E // EG), ALU.add))
                if kind == "pick" and part == 5:
                    after(dve.max(top8[:, :], open_[:, :]))
                    after(dve.max_index(top_at[:, :], top8[:, :], open_[:, :]))
                    later(dve.tensor_copy(top_atf[:, :], top_at[:, :]))
                if kind == "pick" and part == 6:
                    after(dve.tensor_tensor(onehot[:, :, :], wide(iota_e[:, :], K),
                                            each(top_atf[:, 0:K], E), ALU.is_equal))
                    if i >= 1:
                        dve.wait_ge(count_ready, i)
                    with nc.allow_low_precision("zeros and ones"):
                        dve.tensor_reduce(chose[:, :], onehot[:, :, :].rearrange("p k e -> p e k"), AX_X, ALU.add
                                          ).then_inc(chose_ready, 1)
                if kind == "pick" and part == 7:
                    after(dve.tensor_tensor(onehot_s[:, :, :], onehot[:, :, :], wide(sig[:, 0:E], K), ALU.mult))
                    dve.tensor_reduce(top_s[:, :], onehot_s[:, :, :], AX_X, ALU.add).then_inc(picked, 1)
                    dve.wait_ge(picked, i + 1)
                    after(dve.tensor_reduce(top_sum[:, :], top_s[:, :], AX_X, ALU.add))
                    after(dve.reciprocal(top_inv[:, :], top_sum[:, :]))
                    dve.tensor_scalar(row[:, i % 2, W_AT:W_AT + K], top_s[:, :], top_inv[:, 0:1], SCALE,
                                      ALU.mult, ALU.mult)
                if kind == "ht":
                    dve.wait_ge(ht_hi_ready, s[1] + 1)
                    reader(low(ht_lo[:, :], bank(s)[0:F, 0:P], ht_hi[:, :]), s)
                if kind == "count":
                    dve.wait_ge(count_ready, s[1] + 1)
                    reader(dve.tensor_tensor(onehot_s[:, :, :], onehot[:, :, :], wide(bank(s)[:, 0:E], K), ALU.mult), s)
                if kind == "sd":
                    i = s[1]
                    dve.wait_ge(sd_ready, i + 1)
                    if i >= 1:
                        dve.wait_ge(z_stored, 16 * i)
                    reader(dve.tensor_tensor(z_sb[:, :], bank(s)[:, 0:M], row[:, i % 2, 0:M], ALU.add), s)
                if kind == "place":
                    i = s[1]
                    read(dve, ("count", i))
                    after(dve.tensor_reduce(pos6[:, :], onehot_s[:, :, :], AX_X, ALU.add))
                    with nc.allow_low_precision("at most one a tile"):
                        dve.tensor_tensor(taken[:, :], taken[:, :], chose[:, :], ALU.add)
                    after(dve.tensor_scalar(over[:, :], pos6[:, :], float(CAP), FAR, ALU.is_ge, ALU.mult))
                    after(dve.tensor_tensor(pos6[:, :], pos6[:, :], over[:, :], ALU.add))
                    after(dve.scalar_tensor_tensor(row[:, i % 2, S_AT:S_AT + K], top_atf[:, 0:K], float(HALF),
                                                             pos6[:, :], ALU.mult, ALU.add))
                    dve.tensor_copy(slot_u[:, i % 2, :], row[:, i % 2, S_AT:S_AT + K]).then_inc(placed, 1)
            dve.wait_ge(placed, TILES)
            dve.tensor_copy(dve_cell[:, :], pos6[:, 0:1]).then_inc(attention_left, 1)

            dve.wait_ge(slot_now_ready, 1)
            links[0] = 0

            def after2(r, ins):
                links[0] += 1
                ins.then_inc(dve_own2, 1)
                return at(r, EXPERT_LINKS * WB, links[0])

            def need(mark):
                dve.wait_ge(dve_own2, mark)

            def expert_round(r):
                links[0] = 0
                for k in range(WB):
                    n = at(r, WB, k)
                    gate_up = s_ps[:, k % 2, 512:512 + 2 * F]
                    dve.wait_ge(srow_loaded[k], at(r, 16, 16))
                    now = after2(r, dve.tensor_scalar(slot_now[:, :], slot_now[:, :], float(P), None, ALU.add))
                    dve.wait_ge(gexp_ready, n + 1)
                    plus = after2(r, dve.tensor_scalar(gsig[:, :], gexp[:, :], 1.0, None, ALU.add))
                    need(now)
                    used(dve, erow_ready, at(r, WB, k - WB + 1))
                    dve.scalar_tensor_tensor(mine[:, :], srow[:, k, S_AT:S_AT + K], slot_now[:, 0:1],
                                             srow[:, k, W_AT:W_AT + K], ALU.is_equal, ALU.mult,
                                             accum_out=slot_w[:, k:k + 1])
                    place = after2(r, dve.scalar_tensor_tensor(mine_k[:, :], srow[:, k, S_AT:S_AT + K],
                                                               slot_now[:, 0:1], choice_far[:, :],
                                                               ALU.is_equal, ALU.mult, accum_out=which[:, :]))
                    need(plus)
                    inverse = after2(r, dve.reciprocal(gact[:, :], gsig[:, :]))
                    need(place)
                    goal_at = after2(r, dve.tensor_scalar(goal[:, :], srow[:, k, T_AT:T_AT + 1], float(K),
                                                          which[:, 0:1], ALU.mult, ALU.add))
                    need(inverse)
                    gated = after2(r, dve.tensor_tensor(gsig[:, :], gate_up[:, 0:F], gact[:, :], ALU.mult))
                    need(goal_at)
                    used(dve, erow_sent[k % EB], at(r, 16 * WB // EB, 16 * (k // EB)))
                    dve.tensor_scalar(goal_u[:, k % EB:k % EB + 1], goal[:, :], FAR, None, ALU.add
                                      ).then_inc(goal_ready, 1)
                    need(gated)
                    used(dve, htr_ready, n - 1)
                    dve.tensor_tensor(hid_e[:, k % 2, :], gate_up[:, F:], gsig[:, :], ALU.mult).then_inc(hid_e_ready, 1)
                assert links[0] == EXPERT_LINKS * WB, links[0] / WB

            expert_round(0)
            with dve.Fori(1, ROUNDS) as r:
                expert_round(r)

            def add(r, ins):
                links[0] += 1
                ins.then_inc(fin_own, 1)
                dve.wait_ge(fin_own, at(r, SUM_LINKS * FB, links[0]))

            def add_up(r, k):
                t = at(r, FB, k)
                dve.wait_ge(half_ready, t + 1)
                dve.wait_ge(zf_loaded[k], at(r, 16, 16))
                used(dve, fout_ready, t - FB + 1)
                dve.tensor_tensor(ysum[:, k, :], yk[:, k, 0, :], zf[:, k, :], ALU.add)
                add(r, dve.tensor_tensor(yk[:, k, 1, :], yk[:, k, 1, :], yk[:, k, 2, :], ALU.add))
                add(r, dve.tensor_tensor(ysum[:, k, :], ysum[:, k, :], yk[:, k, 1, :], ALU.add))
                add(r, dve.bn_stats(fstats[:, :], ysum[:, k, :]))
                hold(k)
                add(r, dve.bn_aggr(fmv[:, k, :], fstats[:, :]))
                dve.tensor_scalar(fve[:, k, :], fmv[:, k, 1:2], EPS, None, ALU.add).then_inc(fvar_ready, 1)

            def shift(r, k):
                dve.wait_ge(frs_ready, at(r, FB, k + 1))
                dve.tensor_scalar(nmr[:, k, :], fmv[:, k, 0:1], -1.0, frs[:, k, 0:1], ALU.mult, ALU.mult
                                  ).then_inc(nmr_ready, 1)

            def final_round(r):
                links[0] = 0
                for k in range(FB):
                    add_up(r, k)
                    if k:
                        shift(r, k - 1)
                shift(r, FB - 1)
                assert links[0] == SUM_LINKS * FB, links

            final_round(0)
            with dve.Fori(1, TILES // FB) as r:
                final_round(r)


_INS = ["L0_attn_x", "L0_attn_w_aq", "L0_attn_w_ak", "L0_attn_w_av", "L0_attn_w_ao", "L0_ffn_gate_w", "L0_ffn_bias",
        "L0_ffn_w_gate", "L0_ffn_w_up", "L0_ffn_w_down", "L0_ffn_ws_gate", "L0_ffn_ws_up", "L0_ffn_ws_down"]


def rope_tables():
    half = D // 2
    freqs = np.power(10000.0, -np.arange(half) / half).astype(np.float32)
    angles = (np.arange(T, dtype=np.float32)[:, None] * freqs[None, :]).astype(np.float64)
    scale = float(D) ** -0.25
    return (np.cos(angles) * scale).astype(np.float32), (np.sin(angles) * scale).astype(np.float32)


def kernel(**inputs):
    import concourse.bacc as _bacc
    from concourse import mybir as _mybir
    from concourse.bass_utils import run_bass_kernel_spmd as _run

    nc = _bacc.Bacc("TRN2", target_bir_lowering=False, num_devices=1)
    arrays, args = {}, []
    cos, sin = rope_tables()
    for name, a in [(n, np.ascontiguousarray(inputs[n])) for n in _INS] + [("rope_cos", cos), ("rope_sin", sin)]:
        arrays[f"in_{name}_dram"] = a
        args.append(nc.dram_tensor(f"in_{name}_dram", a.shape, _mybir.dt.from_np(a.dtype), kind="ExternalInput").ap())
    args.append(nc.dram_tensor("out_0_dram", (B, T, M), F32, kind="ExternalOutput").ap())
    build(nc, *args)
    r = _run(nc, [arrays], core_ids=[0])
    return r.results[0]["out_0_dram"]
```
